# Optimizing a Trainium2 kernel written in Bass

```python
import numpy as np
import jax
import jax.numpy as jnp

def _softmax(x, axis=-1):
    return jax.nn.softmax(x, axis=axis)

def _gelu(x):
    return jax.nn.gelu(x, approximate=True)

def _silu(x):
    return jax.nn.silu(x)

def _sigmoid(x):
    return jax.nn.sigmoid(x)

def _layernorm(x, axis=-1, eps=1e-05):
    m = jnp.mean(x, axis=axis, keepdims=True)
    v = jnp.var(x, axis=axis, keepdims=True)
    return (x - m) / jnp.sqrt(v + eps)

def _scatter_add(tgt, idx, src, axis=0):
    return tgt.at[idx].add(src)

def _segment_sum(src, seg, n):
    return jax.ops.segment_sum(src, seg, n)
kernel_name = 'mk_gnn_resnorm_d4_gnn_r16_82a430'

def setup_inputs(seed: int=0):
    np.random.seed(seed)
    _w = jnp.asarray

    def _rec_inputs():
        import jax
        import jax.numpy as jnp
        _gk = jax.random.key(seed)
        x = -0.0002117 + 1 * jax.random.normal(jax.random.fold_in(_gk, 1), (3125, 256), jnp.float32)
        src = jax.random.randint(jax.random.fold_in(_gk, 2), (50000,), 0, 3125, jnp.int32)
        dst = jnp.minimum((3125 * jax.random.uniform(jax.random.fold_in(_gk, 3), (50000,)) ** 2.0).astype(jnp.int32), 49999)
        _o = jnp.argsort(dst, stable=True)
        src = src[_o]
        dst = dst[_o]
        edge_attr_8 = -0.00019784 + 0.999804 * jax.random.normal(jax.random.fold_in(_gk, 12), (50000, 8), jnp.float32)
        edge_type_8 = jax.random.randint(jax.random.fold_in(_gk, 14), (50000,), 0, 8, jnp.int32)
        node_type_4 = jax.random.randint(jax.random.fold_in(_gk, 15), (3125,), 0, 4, jnp.int32)
        node_vec = jax.random.uniform(jax.random.fold_in(_gk, 16), (3125,), jnp.float32, 0.0, 0.999991)
        return (x, src, dst, edge_attr_8, edge_type_8, node_type_4, node_vec)
    x, src, dst, edge_attr_8, edge_type_8, node_type_4, node_vec = _rec_inputs()

    def _L0_gnn_setup():
        import jax, jax.numpy as jnp
        import numpy as np
        N_NODES = 6250
        N_EDGES = 100000
        DIM = 256
        N_LAYERS = 4
        LN_EPS = 1e-05

        def _layer_norm(x, gamma, beta):
            mu = jnp.mean(x, axis=-1, keepdims=True)
            var = jnp.mean(jnp.square(x - mu), axis=-1, keepdims=True)
            return (x - mu) * jax.lax.rsqrt(var + LN_EPS) * gamma + beta
        key = jax.random.key(seed)
        ks = jax.random.split(key, 10)
        h = jax.random.normal(ks[0], (N_NODES, DIM), dtype=jnp.float32)
        src = jax.random.randint(ks[1], (N_EDGES,), 0, N_NODES, dtype=jnp.int32)
        dst = jax.random.randint(ks[2], (N_EDGES,), 0, N_NODES, dtype=jnp.int32)
        s = 1.0 / np.sqrt(DIM)
        W1 = jax.random.normal(ks[3], (N_LAYERS, DIM, DIM), dtype=jnp.float32) * s
        b1 = jnp.zeros((N_LAYERS, DIM), dtype=jnp.float32)
        W2 = jax.random.normal(ks[4], (N_LAYERS, DIM, DIM), dtype=jnp.float32) * s
        b2 = jnp.zeros((N_LAYERS, DIM), dtype=jnp.float32)
        eps = jnp.zeros((N_LAYERS,), dtype=jnp.float32)
        gamma = jnp.ones((DIM,), dtype=jnp.float32)
        beta = jnp.zeros((DIM,), dtype=jnp.float32)
        return {'h': h, 'src': src, 'dst': dst, 'W1': W1, 'b1': b1, 'W2': W2, 'b2': b2, 'eps': eps, 'gamma': gamma, 'beta': beta}
    _L0_gnn_all = _L0_gnn_setup()
    _L0_gnn_in = {k: v for k, v in _L0_gnn_all.items() if k in ('W1', 'b1', 'W2', 'b2', 'eps', 'gamma', 'beta')}
    del _L0_gnn_all

    def _L1_gnn_setup():
        import jax, jax.numpy as jnp
        import numpy as np
        N = 6250
        E = 50000
        FEAT = 256
        HEADS = 8
        HEAD_DIM = FEAT // HEADS
        SCALING = HEAD_DIM ** (-0.5)
        key = jax.random.key(seed)
        ks = jax.random.split(key, 8)
        w_scale = (2.0 / (FEAT + FEAT)) ** 0.5
        return {'nfeat': jax.random.normal(ks[0], (N, FEAT), dtype=jnp.float32), 'attn_bias': jax.random.normal(ks[1], (E, HEADS), dtype=jnp.float32), 'Wq': jax.random.normal(ks[2], (FEAT, FEAT), dtype=jnp.float32) * w_scale, 'Wk': jax.random.normal(ks[3], (FEAT, FEAT), dtype=jnp.float32) * w_scale, 'Wv': jax.random.normal(ks[4], (FEAT, FEAT), dtype=jnp.float32) * w_scale, 'Wo': jax.random.normal(ks[5], (FEAT, FEAT), dtype=jnp.float32) * w_scale, 'src': jax.random.randint(ks[6], (E,), 0, N, dtype=jnp.int32), 'dst': jax.random.randint(ks[7], (E,), 0, N, dtype=jnp.int32)}
    _L1_gnn_all = _L1_gnn_setup()
    _L1_gnn_in = {k: v for k, v in _L1_gnn_all.items() if k in ('Wq', 'Wk', 'Wv', 'Wo')}
    del _L1_gnn_all

    def _L2_gnn_setup():
        import jax, jax.numpy as jnp
        import numpy as np
        N = 6250
        E = 200000
        IN_DIM = 256
        OUT_DIM = 256
        EGO_DIM = OUT_DIM // 2
        NB_DIM = OUT_DIM - EGO_DIM
        key = jax.random.key(seed)
        ks = jax.random.split(key, 10)
        x = jax.random.normal(ks[0], (N, IN_DIM), dtype=jnp.float32)
        edge_index = jax.random.randint(ks[1], (2, E), 0, N, dtype=jnp.int64)
        delta_agg = jax.random.uniform(ks[2], (N,), dtype=jnp.float32)
        s = 1.0 / np.sqrt(IN_DIM)
        W_mean = jax.random.uniform(ks[3], (IN_DIM, OUT_DIM), minval=-s, maxval=s, dtype=jnp.float32)
        b_mean = jax.random.uniform(ks[4], (OUT_DIM,), minval=-s, maxval=s, dtype=jnp.float32)
        W_ego = jax.random.uniform(ks[5], (IN_DIM, EGO_DIM), minval=-s, maxval=s, dtype=jnp.float32)
        b_ego = jax.random.uniform(ks[6], (EGO_DIM,), minval=-s, maxval=s, dtype=jnp.float32)
        W_nb = jax.random.uniform(ks[7], (IN_DIM, NB_DIM), minval=-s, maxval=s, dtype=jnp.float32)
        b_nb = jax.random.uniform(ks[8], (NB_DIM,), minval=-s, maxval=s, dtype=jnp.float32)
        gate_weight = jnp.float32(1.0)
        gate_bias = jnp.float32(0.0)
        return {'x': x, 'edge_index': edge_index, 'delta_agg': delta_agg, 'W_mean': W_mean, 'b_mean': b_mean, 'W_ego': W_ego, 'b_ego': b_ego, 'W_nb': W_nb, 'b_nb': b_nb, 'gate_weight': gate_weight, 'gate_bias': gate_bias}
    _L2_gnn_all = _L2_gnn_setup()
    _L2_gnn_in = {k: v for k, v in _L2_gnn_all.items() if k in ('W_mean', 'b_mean', 'W_ego', 'b_ego', 'W_nb', 'b_nb', 'gate_weight', 'gate_bias')}
    del _L2_gnn_all

    def _L3_gnn_setup():
        import jax, jax.numpy as jnp
        import numpy as np
        N_NODES = 1250
        N_EDGES = 20000
        IN_DIM = 256
        OUT_DIM = 256
        N_HEADS = 4
        D_K = OUT_DIM // N_HEADS
        N_NTYPES = 4
        N_RELS = 8
        SQRT_DK = float(np.sqrt(D_K))

        def _typed_matmul(x, W, node_type):
            all_t = jnp.einsum('ni,tio->tno', x, W)
            return all_t[node_type, jnp.arange(x.shape[0])]
        key = jax.random.key(seed)
        ks = jax.random.split(key, 12)
        xav = lambda k, shape, fan: jax.random.normal(k, shape, jnp.float32) * (1.0 / np.sqrt(fan))
        return {'h': jax.random.normal(ks[0], (N_NODES, IN_DIM), jnp.float32), 'k_linears': xav(ks[1], (N_NTYPES, IN_DIM, OUT_DIM), IN_DIM), 'q_linears': xav(ks[2], (N_NTYPES, IN_DIM, OUT_DIM), IN_DIM), 'v_linears': xav(ks[3], (N_NTYPES, IN_DIM, OUT_DIM), IN_DIM), 'a_linears': xav(ks[4], (N_NTYPES, OUT_DIM, OUT_DIM), OUT_DIM), 'relation_att': xav(ks[5], (N_RELS, N_HEADS, D_K, D_K), D_K), 'relation_msg': xav(ks[6], (N_RELS, N_HEADS, D_K, D_K), D_K), 'relation_pri': jnp.ones((N_RELS, N_HEADS), jnp.float32), 'skip': jnp.ones((N_NTYPES,), jnp.float32), 'node_type': jax.random.randint(ks[7], (N_NODES,), 0, N_NTYPES), 'etype': jnp.sort(jax.random.randint(ks[8], (N_EDGES,), 0, N_RELS)), 'row_idx': jax.random.randint(ks[9], (N_EDGES,), 0, N_NODES), 'col_idx': jax.random.randint(ks[10], (N_EDGES,), 0, N_NODES)}
    _L3_gnn_all = _L3_gnn_setup()
    _L3_gnn_in = {k: v for k, v in _L3_gnn_all.items() if k in ('k_linears', 'q_linears', 'v_linears', 'a_linears', 'relation_att', 'relation_msg', 'relation_pri', 'skip')}
    del _L3_gnn_all
    return {'x': x, 'src': src, 'dst': dst, 'edge_attr_8': edge_attr_8, 'edge_type_8': edge_type_8, 'node_type_4': node_type_4, 'node_vec': node_vec, 'L0_gnn_W1': _L0_gnn_in['W1'], 'L0_gnn_b1': _L0_gnn_in['b1'], 'L0_gnn_W2': _L0_gnn_in['W2'], 'L0_gnn_b2': _L0_gnn_in['b2'], 'L0_gnn_eps': _L0_gnn_in['eps'], 'L0_gnn_gamma': _L0_gnn_in['gamma'], 'L0_gnn_beta': _L0_gnn_in['beta'], 'L1_gnn_Wq': _L1_gnn_in['Wq'], 'L1_gnn_Wk': _L1_gnn_in['Wk'], 'L1_gnn_Wv': _L1_gnn_in['Wv'], 'L1_gnn_Wo': _L1_gnn_in['Wo'], 'L2_gnn_W_mean': _L2_gnn_in['W_mean'], 'L2_gnn_b_mean': _L2_gnn_in['b_mean'], 'L2_gnn_W_ego': _L2_gnn_in['W_ego'], 'L2_gnn_b_ego': _L2_gnn_in['b_ego'], 'L2_gnn_W_nb': _L2_gnn_in['W_nb'], 'L2_gnn_b_nb': _L2_gnn_in['b_nb'], 'L2_gnn_gate_weight': _L2_gnn_in['gate_weight'], 'L2_gnn_gate_bias': _L2_gnn_in['gate_bias'], 'L3_gnn_k_linears': _L3_gnn_in['k_linears'], 'L3_gnn_q_linears': _L3_gnn_in['q_linears'], 'L3_gnn_v_linears': _L3_gnn_in['v_linears'], 'L3_gnn_a_linears': _L3_gnn_in['a_linears'], 'L3_gnn_relation_att': _L3_gnn_in['relation_att'], 'L3_gnn_relation_msg': _L3_gnn_in['relation_msg'], 'L3_gnn_relation_pri': _L3_gnn_in['relation_pri'], 'L3_gnn_skip': _L3_gnn_in['skip']}

def reference(x, src, dst, edge_attr_8, edge_type_8, node_type_4, node_vec, L0_gnn_W1, L0_gnn_b1, L0_gnn_W2, L0_gnn_b2, L0_gnn_eps, L0_gnn_gamma, L0_gnn_beta, L1_gnn_Wq, L1_gnn_Wk, L1_gnn_Wv, L1_gnn_Wo, L2_gnn_W_mean, L2_gnn_b_mean, L2_gnn_W_ego, L2_gnn_b_ego, L2_gnn_W_nb, L2_gnn_b_nb, L2_gnn_gate_weight, L2_gnn_gate_bias, L3_gnn_k_linears, L3_gnn_q_linears, L3_gnn_v_linears, L3_gnn_a_linears, L3_gnn_relation_att, L3_gnn_relation_msg, L3_gnn_relation_pri, L3_gnn_skip):
    import jax
    import jax.numpy as jnp

    def _L0_gnn_ref(h, src, dst, W1, b1, W2, b2, eps, gamma, beta):
        import jax, jax.numpy as jnp
        import numpy as np
        N_NODES = 6250
        N_EDGES = 100000
        DIM = 256
        N_LAYERS = 4
        LN_EPS = 1e-05

        def _layer_norm(x, gamma, beta):
            mu = jnp.mean(x, axis=-1, keepdims=True)
            var = jnp.mean(jnp.square(x - mu), axis=-1, keepdims=True)
            return (x - mu) * jax.lax.rsqrt(var + LN_EPS) * gamma + beta
        for i in range(N_LAYERS):
            h_res = h
            agg = jnp.zeros_like(h).at[dst].add(h[src])
            x = (1.0 + eps[i]) * h + agg
            x = jax.nn.relu(x @ W1[i] + b1[i]) @ W2[i] + b2[i]
            x = _layer_norm(x, gamma, beta)
            x = jax.nn.relu(x)
            h = x + h_res
        return h

    def _L1_gnn_ref(nfeat, attn_bias, Wq, Wk, Wv, Wo, src, dst):
        import jax, jax.numpy as jnp
        import numpy as np
        N = 6250
        E = 50000
        FEAT = 256
        HEADS = 8
        HEAD_DIM = FEAT // HEADS
        SCALING = HEAD_DIM ** (-0.5)
        n = nfeat.shape[0]
        q = (nfeat @ Wq.T).reshape(n, HEADS, HEAD_DIM) / SCALING
        k = (nfeat @ Wk.T).reshape(n, HEADS, HEAD_DIM)
        v = (nfeat @ Wv.T).reshape(n, HEADS, HEAD_DIM)
        attn = jnp.einsum('ehd,ehd->eh', k[src], q[dst])
        attn = attn + attn_bias
        m = jax.ops.segment_max(attn, dst, num_segments=n)
        a = jnp.exp(attn - m[dst])
        s = jax.ops.segment_sum(a, dst, num_segments=n)
        a = a / s[dst]
        out = jax.ops.segment_sum(v[src] * a[:, :, None], dst, num_segments=n)
        return out.reshape(n, FEAT) @ Wo.T

    def _L2_gnn_ref(x, edge_index, delta_agg, W_mean, b_mean, W_ego, b_ego, W_nb, b_nb, gate_weight, gate_bias):
        import jax, jax.numpy as jnp
        import numpy as np
        N = 6250
        E = 200000
        IN_DIM = 256
        OUT_DIM = 256
        EGO_DIM = OUT_DIM // 2
        NB_DIM = OUT_DIM - EGO_DIM
        n = x.shape[0]
        row, col = (edge_index[0], edge_index[1])
        neighbor_sum = jax.ops.segment_sum(x[col], row, num_segments=n)
        deg = jax.ops.segment_sum(jnp.ones((row.shape[0],), dtype=x.dtype), row, num_segments=n)
        deg = jnp.maximum(deg, 1.0)
        mean_neighbor = neighbor_sum / deg[:, None]
        h_mean = (x + mean_neighbor) * 0.5 @ W_mean + b_mean
        h_ego = x @ W_ego + b_ego
        h_neighbor = mean_neighbor @ W_nb + b_nb
        h_concat = jnp.concatenate([h_ego, h_neighbor], axis=1)
        gate = jax.nn.sigmoid(gate_weight * delta_agg + gate_bias)[:, None]
        return (1.0 - gate) * h_mean + gate * h_concat

    def _L3_gnn_ref(h, k_linears, q_linears, v_linears, a_linears, relation_att, relation_msg, relation_pri, skip, node_type, etype, row_idx, col_idx):
        import jax, jax.numpy as jnp
        import numpy as np
        N_NODES = 1250
        N_EDGES = 20000
        IN_DIM = 256
        OUT_DIM = 256
        N_HEADS = 4
        D_K = OUT_DIM // N_HEADS
        N_NTYPES = 4
        N_RELS = 8
        SQRT_DK = float(np.sqrt(D_K))

        def _typed_matmul(x, W, node_type):
            all_t = jnp.einsum('ni,tio->tno', x, W)
            return all_t[node_type, jnp.arange(x.shape[0])]
        n = h.shape[0]
        k = _typed_matmul(h, k_linears, node_type).reshape(n, N_HEADS, D_K)
        q = _typed_matmul(h, q_linears, node_type).reshape(n, N_HEADS, D_K)
        v = _typed_matmul(h, v_linears, node_type).reshape(n, N_HEADS, D_K)
        q_att = jnp.einsum('nhd,rhde->rnhe', q, relation_att)
        v_msg = jnp.einsum('nhd,rhde->rnhe', v, relation_msg)
        aw_q_edge = q_att[etype, col_idx]
        msg_edge = v_msg[etype, row_idx]
        attn_score = jnp.sum(aw_q_edge * k[row_idx], axis=-1)
        score = attn_score * (relation_pri[etype] / SQRT_DK)
        m = jax.ops.segment_max(score, col_idx, num_segments=n)
        ex = jnp.exp(score - m[col_idx])
        denom = jax.ops.segment_sum(ex, col_idx, num_segments=n)
        alpha = ex / denom[col_idx]
        agg = jax.ops.segment_sum(alpha[..., None] * msg_edge, col_idx, num_segments=n)
        agg = agg.reshape(n, OUT_DIM)
        out = _typed_matmul(agg, a_linears, node_type)
        out = jax.nn.sigmoid(skip)[node_type][:, None] * out
        return out
    edge_index = jnp.stack([src, dst])
    x = _layernorm(x + _L0_gnn_ref(x, src, dst, L0_gnn_W1, L0_gnn_b1, L0_gnn_W2, L0_gnn_b2, L0_gnn_eps, L0_gnn_gamma, L0_gnn_beta), axis=-1)
    x = _layernorm(x + _L1_gnn_ref(x, edge_attr_8, L1_gnn_Wq, L1_gnn_Wk, L1_gnn_Wv, L1_gnn_Wo, src, dst), axis=-1)
    x = _layernorm(x + _L2_gnn_ref(x, edge_index, node_vec, L2_gnn_W_mean, L2_gnn_b_mean, L2_gnn_W_ego, L2_gnn_b_ego, L2_gnn_W_nb, L2_gnn_b_nb, L2_gnn_gate_weight, L2_gnn_gate_bias), axis=-1)
    x = _layernorm(x + _L3_gnn_ref(x, L3_gnn_k_linears, L3_gnn_q_linears, L3_gnn_v_linears, L3_gnn_a_linears, L3_gnn_relation_att, L3_gnn_relation_msg, L3_gnn_relation_pri, L3_gnn_skip, node_type_4, edge_type_8, src, dst), axis=-1)
    return x

_drawn_inputs = setup_inputs


def setup_inputs(seed=0):
    import zlib

    import numpy as np

    out = dict(_drawn_inputs(seed))
    spreads = {'L0_gnn_b1': (0.0, 0.1),
     'L0_gnn_b2': (0.0, 0.1),
     'L0_gnn_eps': (0.0, 0.1),
     'L0_gnn_gamma': (1.0, 0.2),
     'L0_gnn_beta': (0.0, 0.1),
     'L3_gnn_relation_pri': (1.0, 0.2),
     'L3_gnn_skip': (1.0, 0.6)}
    factors = {'L2_gnn_b_mean': 4.034, 'L2_gnn_b_ego': 3.428, 'L2_gnn_b_nb': 3.383}
    for name, (base, spread) in spreads.items():
        noise = np.random.default_rng([zlib.crc32(name.encode()), seed]).standard_normal(out[name].shape)
        drawn = base * np.exp(spread * noise) if base else spread * noise
        out[name] = jnp.asarray(drawn.astype(out[name].dtype))
    for name, factor in factors.items():
        out[name] = (out[name] * factor).astype(out[name].dtype)
    return out
```

```python
from contextlib import ExitStack

import concourse.bass as bass
from concourse import mybir

P = 128
N = 3125
E = 50000
D = 256
NB = -(-N // P)
NP = NB * P
TAIL = N - (NB - 1) * P
LAYERS = 4
CH = 5
CB = NB // CH
CW = CB * P
PARTS = [(0, 3), (3, 2)]
LN_EPS = 1e-5
BIG = 1.0e30
TILES = -(-(E // P + NB) // 32) * 32
GE = 512
GROUPS = -(-(E // GE + NB) // 2) * 2
EP, EF = 80, E // 80
ROW = 16
C_SRC, C_REL, C_DST, C_ATTR = 0, 1, 2, 4
KB = 16
RELS, TYPES = 8, 4

ALU = mybir.AluOpType
ACT = mybir.ActivationFunctionType
AX = mybir.AxisListType.X
F32 = mybir.dt.float32
F16 = mybir.dt.float16
BF16 = mybir.dt.bfloat16
I32 = mybir.dt.int32


class Place:

    def __init__(self, nc, base, stage):
        self.nc, self.at, self.stage = nc, base, stage

    def __call__(self, name, shape, dt):
        size = 2 if dt in (F16, BF16) else 4
        for s in shape[1:]:
            size *= s
        t = self.nc.alloc_sbuf_tensor_at(f"{self.stage}_{name}", shape, dt, offset=self.at)
        self.at += -(-size // 32) * 32
        return t


def hold(eng, sem, value, marks):
    eng.wait_ge(sem, value)
    eng.sem_inc(marks, 1)


class G:
    pass


def program(nc, a, out):
    with ExitStack() as ctx:
        g = G()
        g.nc, g.a, g.out = nc, a, out
        g.stage_sems = []

        def sem(name):
            handle = nc.alloc_semaphore(name)
            g.stage_sems.append(handle)
            return handle

        g.sem = sem
        keep = lambda name, shape, dt: ctx.enter_context(nc.sbuf_tensor(name, shape, dt))
        dram = lambda name, shape, dt: nc.dram_tensor(name, shape, dt, kind="Internal").ap()
        ctx.enter_context(nc.allow_non_contiguous_dma(reason="small vectors and broadcasts, once"))
        g.psum = ctx.enter_context(nc.psum_tensor("psum", [P, 8, 512], F32))
        g.bank = lambda b: g.psum[:, b, :]
        g.marks = {e: nc.alloc_semaphore(f"marks_{e}") for e in ("sp", "act", "pool", "pe", "dve")}

        g.ident = keep("ident", [P, P], F32)
        g.ident16 = keep("ident16", [P, P], F16)
        g.identb = keep("identb", [P, P], BF16)
        g.iota = keep("iota", [P, P], F32)
        g.tile_e0 = keep("tile_e0", [P, TILES], I32)
        g.tile_blk = keep("tile_blk", [P, TILES], I32)
        g.tile_base = keep("tile_base", [P, TILES], F32)
        g.group_e0 = keep("group_e0", [P, GROUPS], I32)
        g.group_blk = keep("group_blk", [P, GROUPS], I32)
        g.group_base = keep("group_base", [P, GROUPS], F32)
        g.gate = keep("gate", [P, NB], F32)
        g.ngate = keep("ngate", [P, NB], F32)
        g.tmask = keep("tmask", [P, NB, TYPES], F32)
        g.smask = keep("smask", [P, NB, TYPES], F32)

        base = nc.sbuf_base
        g.base = -(-base // 32) * 32
        g.x = nc.alloc_sbuf_tensor_at("x_nodes", [P, NB, D], F32, offset=g.base)
        g.after_x = g.base + NB * D * 4
        g.slot1 = g.after_x
        g.slot2 = g.slot1 + 27136
        g.rest = g.slot2 + NB * 2 * D * 2

        g.edge_rows = dram("edge_rows", [E + P, ROW], I32)
        g.src_f = dram("src_f", [E + GE], F32)
        g.dst_f = dram("dst_f", [E + GE], F32)
        g.adj_sd = [dram(f"adj_sd{p}", [CH, P, NB, PARTS[p][1] * P], BF16) for p in range(2)]
        g.adj_ds = [dram(f"adj_ds{p}", [CH, P, NB, PARTS[p][1] * P], BF16) for p in range(2)]
        g.kv1 = dram("kv1", [NP, 2 * D], F32)
        g.kv3 = dram("kv3", [RELS * NP, 2 * D], F32)

        stages = [
            lambda: prepare(g),
            lambda: build_adjacency(g),
            lambda: store_adjacency(g),
            lambda: gin_layers(g),
            lambda: qkv_pass(g),
            lambda: attention(g, 1),
            lambda: attention_out(g),
            lambda: mean_layer(g),
            lambda: typed_pass(g),
            lambda: attention(g, 3),
            lambda: typed_out(g),
        ]
        for stage in stages:
            stage()
            nc.clear_and_free_semaphores(g.stage_sems)
            nc.all_engine_barrier()
            g.stage_sems = []


def prepare(g):
    nc, a = g.nc, g.a
    t = Place(nc, g.after_x, "prep")
    srci = t("srci", [EP, EF], I32)
    dsti = t("dsti", [EP, EF], I32)
    etyi = t("etyi", [EP, EF], I32)
    attr = t("attr", [EP, EF, 8], F32)
    srcf = t("srcf", [EP, EF], F32)
    dstf = t("dstf", [EP, EF], F32)
    relf = t("relf", [EP, EF], F32)
    rows = t("rows", [EP, EF, ROW], I32)
    less = t("less", [EP, 26, EF // 5], F32)
    lessp = t("lessp", [EP, 5, 26], F32)
    lessc = t("lessc", [EP, 26], F32)
    bndi = t("bndi", [P, 26], I32)
    bnd = t("bnd", [P, 26], F32)
    ones = t("ones", [P, P], F32)
    iotai = t("iotai", [P, TILES], I32)
    iotaf = t("iotaf", [P, TILES], F32)
    start = t("start", [P, 26], F32)
    cnt = t("cnt", [P, 26], F32)
    cnti = t("cnti", [P, 26], I32)
    cnt2 = t("cnt2", [P, 26], I32)
    zero = t("zero", [P, 32], F32)
    tb = t("tb", [P, 32], F32)
    off = t("off", [P, 32], F32)
    step = t("step", [P, 32], F32)
    cmp = t("cmp", [P, TILES // 2, 25], F32)
    blkf = t("blkf", [P, TILES], F32)
    e0f = t("e0f", [P, TILES], F32)
    padrow = t("padrow", [P, ROW], I32)
    padf = t("padf", [1, GE], F32)
    nvec = t("nvec", [32, P], F32)
    ntypi = t("ntypi", [32, P], I32)
    ntyp = t("ntyp", [32, P], F32)
    nv = t("nv", [P, 32], F32)
    nt = t("nt", [P, 32], F32)
    gw = t("gw", [P, 2], F32)
    skip = t("skip", [P, TYPES], F32)

    loaded, consts, zeroed = g.sem("p_loaded"), g.sem("p_consts"), g.sem("p_zeroed")
    less_ready, starts_ready, node_rows, nodes_t = (g.sem("p_less"), g.sem("p_starts"), g.sem("p_node_rows"),
                                                    g.sem("p_nodes_t"))
    rows_ready, stored, pads, gate_in, gate_out = (g.sem("p_rows"), g.sem("p_stored"), g.sem("p_pads"),
                                                   g.sem("p_gate_in"), g.sem("p_gate_out"))

    with nc.Block() as block:
        @block.sync
        def _(sp):
            for dst, src in ((dsti, a["dst"]), (srci, a["src"]), (etyi, a["edge_type_8"])):
                sp.dma_start(dst[:, :], src.rearrange("(p e) -> p e", p=EP)).then_inc(loaded, 16)
            sp.dma_start(attr[:, :, :], a["edge_attr_8"].rearrange("(p e) h -> p e h", p=EP)).then_inc(loaded, 16)
            sp.dma_start(gw[:, 0:1], a["L2_gnn_gate_weight"].unsqueeze(0).broadcast_to([P, 1])).then_inc(loaded, 16)
            sp.dma_start(gw[:, 1:2], a["L2_gnn_gate_bias"].unsqueeze(0).broadcast_to([P, 1])).then_inc(loaded, 16)
            sp.dma_start(skip[:, :], a["L3_gnn_skip"].unsqueeze(0).broadcast_to([P, TYPES])).then_inc(loaded, 16)
            sp.wait_ge(zeroed, 2)
            for dst, src in ((nvec, a["node_vec"]), (ntypi, a["node_type_4"])):
                sp.dma_start(dst[0:NB - 1, :], src[0:(NB - 1) * P].rearrange("(b p) -> b p", p=P)).then_inc(loaded, 16)
                sp.dma_start(dst[NB - 1:NB, 0:TAIL], src[(NB - 1) * P:N].unsqueeze(0)).then_inc(loaded, 16)
            sp.wait_ge(pads, 2)
            sp.dma_start(g.edge_rows[E:E + P], padrow[:, :]).then_inc(stored, 16)
            sp.dma_start(g.src_f[E:E + GE].unsqueeze(0), padf[:, :]).then_inc(stored, 16)
            sp.dma_start(g.dst_f[E:E + GE].unsqueeze(0), padf[:, :]).then_inc(stored, 16)
            sp.wait_ge(rows_ready, 1)
            sp.dma_start(g.edge_rows[0:E].rearrange("(p e) w -> p e w", p=EP), rows[:, :, :]).then_inc(stored, 16)
            sp.dma_start(g.src_f[0:E].rearrange("(p e) -> p e", p=EP), srcf[:, :]).then_inc(stored, 16)
            sp.dma_start(g.dst_f[0:E].rearrange("(p e) -> p e", p=EP), dstf[:, :]).then_inc(stored, 16)
            sp.wait_ge(stored, 16 * 6)

        @block.gpsimd
        def _(pool):
            nc.gpsimd.memset(nvec[:, :], 0.0).then_inc(zeroed, 1)
            nc.gpsimd.memset(ntypi[:, :], 0).then_inc(zeroed, 1)
            nc.gpsimd.memset(padf[:, :], -1.0).then_inc(pads, 1)
            nc.gpsimd.memset(g.ident[:, :], 0.0)
            nc.gpsimd.iota(bndi[:, :], [[P, 26]], base=0, channel_multiplier=0).then_inc(consts, 1)
            nc.gpsimd.iota(iotai[:, :], [[1, TILES]], base=0, channel_multiplier=0).then_inc(consts, 1)
            pool.drain()
            nc.gpsimd.affine_select(out=g.ident[:, :], in_=g.ident[:, :], compare_op=ALU.not_equal, fill=1.0, base=0,
                                    pattern=[[-1, P]], channel_multiplier=1).then_inc(consts, 1)

        @block.tensor
        def _(pe):
            pe.wait_ge(less_ready, 1)
            pe.matmul(g.bank(0)[:, 0:26], ones[0:EP, :], lessc[:, :], start=True, stop=True).then_inc(starts_ready, 1)
            pe.wait_ge(node_rows, 1)
            pe.wait_ge(consts, 3)
            pe.transpose(g.bank(1)[:, 0:32], nvec[:, :], g.ident[0:32, 0:32])
            pe.transpose(g.bank(1)[:, 32:64], ntyp[:, :], g.ident[0:32, 0:32]).then_inc(nodes_t, 1)

        @block.scalar
        def _(act):
            act.wait_ge(gate_in, 1)
            act.wait_ge(loaded, 16 * 11)
            nc.scalar.activation(g.gate[:, :], nv[:, 0:NB], ACT.Sigmoid, bias=gw[:, 1:2], scale=gw[:, 0:1])
            nc.scalar.activation(skip[:, :], skip[:, :], ACT.Sigmoid).then_inc(gate_out, 1)

        @block.vector
        def _(dve):
            v = nc.vector

            def tile_list(count, size, shift, e0, blk, nbase):
                v.tensor_tensor(cnt[:, 0:25], start[:, 1:26], start[:, 0:25], ALU.subtract)
                v.memset(tb[:, 0:1], 0.0)
                dve.drain()
                v.tensor_scalar(cnt[:, 0:25], cnt[:, 0:25], float(size - 1), None, ALU.add)
                dve.drain()
                v.tensor_copy(cnti[:, 0:25], cnt[:, 0:25])
                dve.drain()
                v.tensor_scalar(cnt2[:, 0:25], cnti[:, 0:25], shift, None, ALU.arith_shift_right)
                dve.drain()
                v.tensor_copy(cnt[:, 0:25], cnt2[:, 0:25])
                dve.drain()
                v.tensor_tensor_scan(tb[:, 1:26], cnt[:, 0:25], zero[:, 0:25], 0.0, ALU.add, ALU.add)
                dve.drain()
                v.scalar_tensor_tensor(off[:, 0:26], tb[:, 0:26], -float(size), start[:, 0:26], ALU.mult, ALU.add)
                dve.drain()
                v.tensor_tensor(step[:, 0:25], off[:, 1:26], off[:, 0:25], ALU.subtract)
                dve.drain()
                for lo in range(0, count, TILES // 2):
                    w = min(TILES // 2, count - lo)
                    it = iotaf[:, lo:lo + w].unsqueeze(2).broadcast_to([P, w, 25])
                    v.tensor_tensor(cmp[:, 0:w, :], it, tb[:, 1:26].unsqueeze(1).broadcast_to([P, w, 25]), ALU.is_ge)
                    dve.drain()
                    v.tensor_reduce(blkf[:, lo:lo + w], cmp[:, 0:w, :], AX, ALU.add)
                    dve.drain()
                    v.tensor_tensor(cmp[:, 0:w, :], cmp[:, 0:w, :],
                                    step[:, 0:25].unsqueeze(1).broadcast_to([P, w, 25]), ALU.mult)
                    dve.drain()
                    v.tensor_reduce(e0f[:, lo:lo + w], cmp[:, 0:w, :], AX, ALU.add)
                    dve.drain()
                v.scalar_tensor_tensor(e0f[:, 0:count], iotaf[:, 0:count], float(size), e0f[:, 0:count],
                                       ALU.mult, ALU.add)
                v.tensor_scalar(blkf[:, 0:count], blkf[:, 0:count], float(NB - 1), None, ALU.min)
                dve.drain()
                v.tensor_scalar(e0f[:, 0:count], e0f[:, 0:count], float(E), None, ALU.min)
                v.tensor_copy(blk[:, :], blkf[:, 0:count])
                v.tensor_scalar(nbase[:, :], blkf[:, 0:count], float(P), None, ALU.mult)
                dve.drain()
                v.tensor_copy(e0[:, :], e0f[:, 0:count])
                dve.drain()

            v.memset(ones[:, :], 1.0)
            v.memset(zero[:, :], 0.0)
            v.memset(padrow[:, :], 0)
            v.memset(rows[:, :, :], 0)
            dve.drain()
            v.memset(padrow[:, C_DST:C_DST + 1].bitcast(F32), -1.0).then_inc(pads, 1)
            dve.wait_ge(consts, 3)
            v.tensor_copy(bnd[:, :], bndi[:, :])
            v.tensor_copy(iotaf[:, :], iotai[:, :])
            v.tensor_copy(g.ident16[:, :], g.ident[:, :])
            v.tensor_copy(g.identb[:, :], g.ident[:, :])
            dve.drain()
            v.tensor_copy(g.iota[:, :], iotaf[:, 0:P])
            dve.wait_ge(loaded, 16 * 11)
            v.tensor_copy(ntyp[:, :], ntypi[:, :]).then_inc(node_rows, 1)
            v.tensor_copy(dstf[:, :], dsti[:, :])
            v.tensor_copy(srcf[:, :], srci[:, :])
            v.tensor_copy(relf[:, :], etyi[:, :])
            dve.drain()
            w = EF // 5
            for q in range(5):
                v.tensor_tensor(less[:, :, :], dstf[:, q * w:(q + 1) * w].unsqueeze(1).broadcast_to([EP, 26, w]),
                                bnd[0:EP, :].unsqueeze(2).broadcast_to([EP, 26, w]), ALU.is_lt)
                dve.drain()
                v.tensor_reduce(lessp[:, q, :], less[:, :, :], AX, ALU.add)
                dve.drain()
            v.tensor_reduce(lessc[:, :], lessp[:, :, :].rearrange("p q b -> p b q"), AX, ALU.add).then_inc(less_ready, 1)
            v.scalar_tensor_tensor(relf[:, :], relf[:, :], float(NP), srcf[:, :], ALU.mult, ALU.add)
            v.tensor_copy(rows[:, :, C_SRC], srci[:, :])
            v.tensor_copy(rows[:, :, C_DST].bitcast(F32), dstf[:, :])
            v.tensor_copy(rows[:, :, C_ATTR:C_ATTR + 8].bitcast(F32), attr[:, :, :])
            dve.drain()
            v.tensor_copy(rows[:, :, C_REL], relf[:, :])
            dve.drain().then_inc(rows_ready, 1)
            dve.wait_ge(starts_ready, 1)
            v.tensor_copy(start[:, :], g.bank(0)[:, 0:26])
            dve.drain()
            tile_list(TILES, P, 7, g.tile_e0, g.tile_blk, g.tile_base)
            tile_list(GROUPS, GE, 9, g.group_e0, g.group_blk, g.group_base)
            dve.wait_ge(nodes_t, 1)
            v.tensor_copy(nv[:, :], g.bank(1)[:, 0:32]).then_inc(gate_in, 1)
            v.tensor_copy(nt[:, :], g.bank(1)[:, 32:64])
            dve.drain()
            for k in range(TYPES):
                v.tensor_scalar(g.tmask[:, :, k], nt[:, 0:NB], float(k), None, ALU.is_equal)
            dve.wait_ge(gate_out, 1)
            v.tensor_scalar(g.ngate[:, :], g.gate[:, :], -1.0, 1.0, ALU.mult, ALU.add)
            dve.drain()
            for k in range(TYPES):
                v.tensor_scalar(g.smask[:, :, k], g.tmask[:, :, k], skip[:, k:k + 1], None, ALU.mult)


def build_adjacency(g):
    nc = g.nc
    g.adj = Place(nc, (nc.sbuf_usable_end - NB * NP * 2) // 32 * 32, "adj")("rows", [P, NB, NP], BF16)
    u = Place(nc, g.base, "adj")
    oh_src = [u(f"oh_src{k}", [P, NP], BF16) for k in range(4)]
    wide = u("wide_iota", [P, NP], F16)
    oh_dst = [u(f"oh_dst{k}", [P, P], BF16) for k in range(4)]
    ends = [u(f"ends{k}", [P, 2, 4], F32) for k in range(2)]
    loc = [u(f"loc{k}", [P, 2, 4], F32) for k in range(2)]
    HALF = float(NP // 2)

    ends_ready = [g.sem(f"b_ends_ready{k}") for k in range(2)]
    ends_used, iota_ready, oh_ready, oh_used, sums_ready, sums_used = (
        g.sem("b_ends_used"), g.sem("b_iota"), g.sem("b_oh_ready"), g.sem("b_oh_used"), g.sem("b_sums_ready"),
        g.sem("b_sums_used"))
    cols = [(c, min(512, NP - c)) for c in range(0, NP, 512)]

    with nc.Block() as block:
        @block.gpsimd
        def _(pool):
            nc.gpsimd.iota(wide[:, :], [[1, NP]], base=-NP // 2, channel_multiplier=0,
                           allow_small_or_imprecise_dtypes=True).then_inc(iota_ready, 1)

        @block.sync
        def _(sp):
            def load(k, grp):
                e0 = sp.value_load(g.group_e0[0:1, bass.ds(grp, 1)], min_val=0, max_val=E)
                for n, flat in enumerate((g.src_f, g.dst_f)):
                    sp.dma_start(ends[k][:, n, :], flat[bass.ds(e0, GE)].rearrange("(p e) -> p e", p=P))\
                        .then_inc(ends_ready[k], 16)

            with sp.Fori(0, GROUPS // 2) as i:
                for k in range(2):
                    hold(sp, ends_used, i * 2 + (k + 1), g.marks["sp"])
                    load(k, i * 2 + k)

        @block.vector
        def _(dve):
            v = nc.vector
            v.memset(g.adj[:, :, :], 0.0)
            dve.sem_inc(ends_used, 2)
            dve.sem_inc(sums_used, 1)
            dve.wait_ge(iota_ready, 1)

            def one_hots(grp, it, k):
                hold(dve, ends_ready[k], it * 32 + 32, g.marks["dve"])
                v.tensor_scalar(loc[k][:, 0, :], ends[k][:, 0, :], -HALF, None, ALU.add)
                v.tensor_scalar(loc[k][:, 1, :], ends[k][:, 1, :], g.group_base[:, bass.ds(grp, 1)], None, ALU.subtract)
                dve.drain().then_inc(ends_used, 1)
                for e in range(4):
                    hold(dve, oh_used, grp * 4 + (e + 1), g.marks["dve"])
                    v.tensor_scalar(oh_dst[e][:, :], g.iota[:, :], loc[k][:, 1, e:e + 1], None, ALU.is_equal)
                    v.tensor_scalar(oh_src[e][:, :], wide[:, :], loc[k][:, 0, e:e + 1], None, ALU.is_equal)\
                        .then_inc(oh_ready, 1)

            def add_sums(grp):
                hold(dve, sums_ready, grp + 1, g.marks["dve"])
                blk = dve.value_load(g.group_blk[0:1, bass.ds(grp, 1)], min_val=0, max_val=NB - 1)
                row = g.adj[:, bass.ds(blk, 1), :].rearrange("p b n -> p (b n)")
                v.tensor_tensor(row, row, g.psum[:, 0:7, :].rearrange("p b n -> p (b n)")[:, 0:NP], ALU.add)\
                    .then_inc(sums_used, 1)

            one_hots(0, 0, 0)
            one_hots(1, 0, 1)
            add_sums(0)
            with dve.Fori(1, GROUPS // 2) as i:
                one_hots(i * 2, i, 0)
                add_sums(i * 2 - 1)
                one_hots(i * 2 + 1, i, 1)
                add_sums(i * 2)
            add_sums(GROUPS - 1)

        @block.tensor
        def _(pe):
            pe.sem_inc(oh_used, 4)
            with pe.Fori(0, GROUPS) as grp:
                for e in range(4):
                    hold(pe, oh_ready, grp * 4 + (e + 1), g.marks["pe"])
                    if e == 0:
                        hold(pe, sums_used, grp + 1, g.marks["pe"])
                    for n, (c, w) in enumerate(cols):
                        mm = pe.matmul(g.bank(n)[:, 0:w], oh_dst[e][:, :], oh_src[e][:, c:c + w],
                                       start=(e == 0), stop=(e == 3))
                    mm.then_inc(oh_used, 1)
                pe.drain().then_inc(sums_ready, 1)


def store_adjacency(g):
    nc = g.nc
    stage = Place(nc, g.base, "sto")("turned", [P, NB, CW], BF16)
    turned, taken = g.sem("s_turned"), g.sem("s_taken")
    taken_by = [g.sem("s_taken_act"), g.sem("s_taken_dve")]
    staged_out, rows_out = g.sem("s_staged_out"), g.sem("s_rows_out")

    with nc.Block() as block:
        @block.gpsimd
        def _(pool):
            for c in range(CH):
                for p, (k0, nb) in enumerate(PARTS):
                    pool.dma_start(g.adj_ds[p][c], g.adj[:, :, c * CW + k0 * P:c * CW + (k0 + nb) * P])\
                        .then_inc(rows_out, 16)
            pool.wait_ge(rows_out, 16 * 2 * CH)

        @block.tensor
        def _(pe):
            pe.sem_inc(taken_by[0], 1)
            pe.sem_inc(taken_by[1], 1)
            with pe.Fori(0, CH) as c:
                for s in range(NB):
                    q = s % 2
                    per = 13 if q == 0 else 12
                    hold(pe, taken_by[q], c * per + (s // 2 + 1), g.marks["pe"])
                    for k in range(CB):
                        o = g.psum[:, 2 * q:2 * q + 2, :].rearrange("p b n -> p (b n)")[:, k * P:(k + 1) * P]
                        lhs = g.adj[:, bass.ds(c * CB + k, 1), s * P:(s + 1) * P].rearrange("p b n -> p (b n)")
                        mm = pe.matmul(o, lhs, g.identb[:, :], start=True, stop=True)
                    mm.then_inc(turned, 1)

        def copies(eng, q, per, copy):
            with eng.Fori(0, CH) as c:
                hold(eng, staged_out, c * 32 + 1, g.marks["act" if q == 0 else "dve"])
                for s in range(q, NB, 2):
                    hold(eng, turned, c * NB + (s + 1), g.marks["act" if q == 0 else "dve"])
                    copy(stage[:, s, :], g.psum[:, 2 * q:2 * q + 2, :].rearrange("p b n -> p (b n)")[:, 0:CW])\
                        .then_inc(taken_by[q], 1)

        @block.scalar
        def _(act):
            copies(act, 0, 13, nc.scalar.copy)

        @block.vector
        def _(dve):
            dve.sem_inc(staged_out, 1)
            copies(dve, 1, 12, nc.vector.tensor_copy)

        @block.sync
        def _(sp):
            with sp.Fori(0, CH) as c:
                hold(sp, taken_by[0], c * 13 + 14, g.marks["sp"])
                hold(sp, taken_by[1], c * 12 + 13, g.marks["sp"])
                for p, (k0, nb) in enumerate(PARTS):
                    sp.dma_start(g.adj_sd[p][bass.ds(c, 1)].rearrange("c p s n -> (c p) s n"),
                                 stage[:, :, k0 * P:(k0 + nb) * P]).then_inc(staged_out, 16)
            sp.wait_ge(staged_out, 32 * CH + 1)


class Norm:

    def __init__(self, g, t, name):
        self.g = g
        self.st, self.mv = t("st", [P, CB, 6], F32), t("mv", [P, CB, 2], F32)
        self.ve, self.rstd, self.power = t("ve", [P, CB], F32), t("rstd", [P, CB], F32), t("power", [P, CB], F32)
        self.var_ready, self.rstd_ready, self.cleared = (g.sem(f"{name}_var_ready"), g.sem(f"{name}_rstd_ready"),
                                                         g.sem(f"{name}_ve_cleared"))

    def roots(self, pool, calls):
        pool.memset(self.power[:, :], -0.5)
        pool.memset(self.ve[:, :], 1.0)
        pool.drain().then_inc(self.cleared, 1)
        with pool.Fori(0, calls) as i:
            hold(pool, self.var_ready, i + 1, self.g.marks["pool"])
            pool.tensor_tensor(self.rstd[:, :], self.ve[:, :], self.power[:, :], ALU.pow).then_inc(self.rstd_ready, 1)

    def rows(self, dve, z, nb, call):
        v = self.g.nc.vector
        for k in range(nb):
            v.bn_stats(self.st[:, k, :], z[:, k, :])
        dve.drain()
        for k in range(nb):
            v.bn_aggr(self.mv[:, k, :], self.st[:, k, :])
        dve.drain()
        v.tensor_scalar(self.ve[:, 0:nb], self.mv[:, 0:nb, 1], LN_EPS, None, ALU.add).then_inc(self.var_ready, 1)
        hold(dve, self.rstd_ready, call + 1, self.g.marks["dve"])


def split16(nc, dve, hi, lo, full):
    nc.vector.tensor_copy(hi, full)
    dve.drain()
    nc.vector.tensor_tensor(lo, full, hi, ALU.subtract)


def piece_sems(g, name):
    g.a_loaded = [[g.sem(f"{name}_a_loaded{p}{j}") for j in range(CH)] for p in range(2)]
    g.a_used = [[g.sem(f"{name}_a_used{p}{j}") for j in range(CH)] for p in range(2)]


def load_pieces(g, sp, adj, abuf, c, it):
    for p in range(2):
        for j in range(CH):
            hold(sp, g.a_used[p][j], it + 1, g.marks["sp"])
            sp.dma_start(abuf[p][:, j * CB:(j + 1) * CB, :],
                         adj[p][bass.ds(c, 1), :, j * CB:(j + 1) * CB, :].rearrange("c p s n -> (c p) s n"))\
                .then_inc(g.a_loaded[p][j], 16)


def gin_layers(g):
    nc, a = g.nc, g.a
    t = Place(nc, g.after_x, "gin")
    g.h = t("h", [P, NB, D], F32)
    hs = [t(f"hs{q}", [P, NB, 2, D], F16) for q in range(2)]
    abuf = [t(f"abuf{p}", [P, NB, PARTS[p][1] * P], BF16) for p in range(2)]
    xT = [t(f"xT{p}", [P, 2, PARTS[p][1] * P], F32) for p in range(2)]
    yT = [t(f"yT{p}", [P, 2, PARTS[p][1] * P], F32) for p in range(2)]
    w1 = [t(f"w1{q}", [P, 2, D], F32) for q in range(2)]
    w2 = [t(f"w2{q}", [P, 2, D], F32) for q in range(2)]
    b1 = [t(f"b1{q}", [P, 2], F32) for q in range(2)]
    b2 = [t(f"b2{q}", [P, D], F32) for q in range(2)]
    gam = t("gam", [P, D], F32)
    bet = t("bet", [P, D], F32)
    epsr = t("epsr", [P, LAYERS], F32)
    dful = t("dful", [P, P], F32)
    diag = t("diag", [P, LAYERS, 2, P], F16)
    z = t("z", [P, 3, D], F32)
    norm = Norm(g, t, "g")
    mv, rstd = norm.mv, norm.rstd

    piece_sems(g, "g")
    x_ready, small, diag_ready, h_done = g.sem("g_x"), g.sem("g_small"), g.sem("g_diag"), g.sem("g_h_done")
    w_loaded = [g.sem(f"g_w_loaded{q}") for q in range(2)]
    w_used = [g.sem(f"g_w_used{q}") for q in range(2)]
    agg_done = [g.sem(f"g_agg{p}") for p in range(2)]
    xt_ready = [g.sem(f"g_xt{p}") for p in range(2)]
    y_done = [g.sem(f"g_y{p}") for p in range(2)]
    yt_ready = [g.sem(f"g_yt{p}") for p in range(2)]
    z_done, z_used = g.sem("g_z_done"), g.sem("g_z_used")
    ZBANK = [6, 7, 6, 7, 6]
    ZWAIT = [3, 1, 2, 2, 2]

    def turns(eng, each_layer, a_first, body):
        with eng.Fori(0, LAYERS // 2) as lp:
            for q in range(2):
                layer = lp * 2 + q
                each_layer(layer, lp, q)
                a_first(layer * CH, 0, layer, q)
                with eng.Fori(0, CH - 1) as c:
                    body(layer * CH + c, c, layer, q, False)
                body(layer * CH + (CH - 1), CH - 1, layer, q, True)

    with nc.Block() as block:
        @block.sync
        def _(sp):
            sp.dma_start(g.x[:, 0:NB - 1, :],
                         a["x"][0:(NB - 1) * P].rearrange("(b p) d -> p b d", p=P)).then_inc(x_ready, 16)
            sp.wait_ge(small, 1)
            sp.dma_start(g.x[0:TAIL, NB - 1, :], a["x"][(NB - 1) * P:N]).then_inc(x_ready, 16)
            for row, src in ((gam, a["L0_gnn_gamma"]), (bet, a["L0_gnn_beta"]), (epsr, a["L0_gnn_eps"])):
                sp.dma_start(row[:, :], src.unsqueeze(0).broadcast_to(list(row.shape))).then_inc(x_ready, 16)
            with sp.Fori(0, LAYERS // 2) as lp:
                for q in range(2):
                    layer = lp * 2 + q
                    hold(sp, w_used[q], lp * 2 + 2, g.marks["sp"])
                    for w, src in ((w1, a["L0_gnn_W1"]), (w2, a["L0_gnn_W2"])):
                        sp.dma_start(w[q][:, :, :],
                                     src[bass.ds(layer, 1)].rearrange("l (c p) n -> p (l c) n", p=P))\
                            .then_inc(w_loaded[q], 16)
                    sp.dma_start(b1[q][:, :], a["L0_gnn_b1"][bass.ds(layer, 1)].rearrange("l (c p) -> p (l c)", p=P))\
                        .then_inc(w_loaded[q], 16)
                    sp.dma_start(b2[q][:, :], a["L0_gnn_b2"][bass.ds(layer, 1)].broadcast_to([P, D]))\
                        .then_inc(w_loaded[q], 16)
                    with sp.Fori(0, CH) as c:
                        load_pieces(g, sp, g.adj_sd, abuf, c, layer * CH + c)

        @block.gpsimd
        def _(pool):
            norm.roots(pool, 2 * CH * LAYERS)

        @block.tensor
        def _(pe):
            for p in range(2):
                for j in range(CH):
                    pe.sem_inc(g.a_used[p][j], 1)
            pe.wait_ge(diag_ready, 1)

            def aggregate(it, c, layer, q, p):
                k0, nb = PARTS[p]
                w = nb * P
                hold(pe, xt_ready[p], it + 1, g.marks["pe"])
                for j in range(CH):
                    hold(pe, g.a_loaded[p][j], it * 16 + 16, g.marks["pe"])
                    for s in range(j * CB, (j + 1) * CB):
                        for f in range(2):
                            for part in range(2):
                                mm = pe.matmul(g.bank(2 * p + f)[:, 0:w], hs[q][:, s, part, f * P:(f + 1) * P],
                                               abuf[p][:, s, :], start=(s == 0 and part == 0),
                                               stop=(s == NB - 1 and part == 1))
                    mm.then_inc(g.a_used[p][j], 1)
                    if j == 0:
                        own_rows(c, layer, q, p)
                pe.drain().then_inc(agg_done[p], 1)

            def own_rows(c, layer, q, p):
                k0, nb = PARTS[p]
                for f in range(2):
                    for k in range(nb):
                        for part in range(2):
                            lhs = hs[q][:, bass.ds(c * CB + (k0 + k), 1), part, f * P:(f + 1) * P]\
                                .rearrange("p b n -> p (b n)")
                            for e in range(2):
                                pe.matmul(g.bank(2 * p + f)[:, k * P:(k + 1) * P], lhs,
                                          diag[:, bass.ds(layer, 1), e, :].rearrange("p b n -> p (b n)"),
                                          start=False, stop=False, skip_group_check=True)

            def perceptron(it, c, q, p):
                k0, nb = PARTS[p]
                hold(pe, xt_ready[p], it + 2, g.marks["pe"])
                for f in range(2):
                    for kk in range(2):
                        mm = pe.matmul(g.bank(4 + f)[:, 0:nb * P], w1[q][:, kk, f * P:(f + 1) * P], xT[p][:, kk, :],
                                       start=(kk == 0), stop=(kk == 1))
                mm.then_inc(y_done[p], 1)
                hold(pe, yt_ready[p], it * 2 + 2, g.marks["pe"])
                for k in range(k0, k0 + nb):
                    hold(pe, z_used, it * CB + (k + ZWAIT[k]), g.marks["pe"])
                    for kk in range(2):
                        mm = pe.matmul(g.bank(ZBANK[k])[:, 0:D], yT[p][:, kk, (k - k0) * P:(k - k0 + 1) * P],
                                       w2[q][:, kk, :], start=(kk == 0), stop=(kk == 1))
                    mm.then_inc(z_done, 1)

            def each_layer(layer, lp, q):
                hold(pe, h_done, layer * (2 * CH) + 1, g.marks["pe"])
                hold(pe, w_loaded[q], lp * 64 + 64, g.marks["pe"])

            def a_first(it, c, layer, q):
                aggregate(it, c, layer, q, 0)

            def body(it, c, layer, q, last):
                aggregate(it, c, layer, q, 1)
                perceptron(it, c, q, 0)
                if not last:
                    aggregate(it + 1, c + 1, layer, q, 0)
                perceptron(it, c, q, 1)
                if last:
                    pe.drain().then_inc(w_used[q], 1)

            turns(pe, each_layer, a_first, body)

        @block.scalar
        def _(act):
            for p in range(2):
                act.sem_inc(xt_ready[p], 1)

            def take(it, p):
                w = PARTS[p][1] * P
                hold(act, agg_done[p], it + 1, g.marks["act"])
                nc.scalar.copy(xT[p][:, :, :], g.psum[:, 2 * p:2 * p + 2, 0:w]).then_inc(xt_ready[p], 1)

            def relu(it, q, p):
                w = PARTS[p][1] * P
                hold(act, y_done[p], it + 1, g.marks["act"])
                for f in range(2):
                    nc.scalar.activation(yT[p][:, f, :], g.bank(4 + f)[:, 0:w], ACT.Relu, bias=b1[q][:, f:f + 1])\
                        .then_inc(yt_ready[p], 1)

            def each_layer(layer, lp, q):
                hold(act, w_loaded[q], lp * 64 + 64, g.marks["act"])

            def body(it, c, layer, q, last):
                take(it, 1)
                relu(it, q, 0)
                if not last:
                    take(it + 1, 0)
                relu(it, q, 1)

            turns(act, each_layer, lambda it, c, layer, q: take(it, 0), body)

        @block.vector
        def _(dve):
            v = nc.vector
            dve.wait_ge(norm.cleared, 1)
            v.memset(g.x[:, NB - 1, :], 0.0).then_inc(small, 1)
            dve.sem_inc(z_used, 3)
            dve.sem_inc(w_used[0], 2)
            dve.sem_inc(w_used[1], 2)
            dve.wait_ge(x_ready, 16 * 5)
            v.tensor_copy(g.h[:, :, :], g.x[:, :, :])
            split16(nc, dve, hs[0][:, :, 0, :], hs[0][:, :, 1, :], g.x[:, :, :])
            v.tensor_scalar(epsr[:, :], epsr[:, :], 1.0, None, ALU.add)
            dve.drain().then_inc(h_done, 1)
            for layer in range(LAYERS):
                v.tensor_scalar(dful[:, :], g.ident[:, :], epsr[:, layer:layer + 1], None, ALU.mult)
                dve.drain()
                split16(nc, dve, diag[:, layer, 0, :], diag[:, layer, 1, :], dful[:, :])
                dve.drain()
            dve.drain().then_inc(diag_ready, 1)

            def finish(it, c, q, p):
                k0, nb = PARTS[p]
                for k in range(k0, k0 + nb):
                    hold(dve, z_done, it * CB + (k + 1), g.marks["dve"])
                    v.tensor_tensor(z[:, k - k0, :], g.bank(ZBANK[k])[:, 0:D], b2[q][:, :], ALU.add).then_inc(z_used, 1)
                dve.drain()
                norm.rows(dve, z, nb, it * 2 + p)
                for k in range(nb):
                    v.scalar_tensor_tensor(z[:, k, :], z[:, k, :], mv[:, k, 0:1], gam[:, :], ALU.subtract, ALU.mult)
                dve.drain()
                for k in range(nb):
                    v.scalar_tensor_tensor(z[:, k, :], z[:, k, :], rstd[:, k:k + 1], bet[:, :], ALU.mult, ALU.add)
                dve.drain()
                blocks = bass.ds(c * CB + k0, nb)
                v.scalar_tensor_tensor(g.h[:, blocks, :], z[:, 0:nb, :], 0.0, g.h[:, blocks, :], ALU.max, ALU.add)
                dve.drain()
                split16(nc, dve, hs[1 - q][:, blocks, 0, :], hs[1 - q][:, blocks, 1, :], g.h[:, blocks, :])
                dve.drain().then_inc(h_done, 1)

            def each_layer(layer, lp, q):
                hold(dve, w_loaded[q], lp * 64 + 64, g.marks["dve"])

            def body(it, c, layer, q, last):
                finish(it, c, q, 0)
                finish(it, c, q, 1)
                if last:
                    dve.sem_inc(w_used[q], 1)

            turns(dve, each_layer, lambda it, c, layer, q: None, body)



ZBANK = [6, 7, 6, 7, 6]
ZWAIT = [3, 1, 2, 2, 2]


def pe_turn(g, pe, w, turned, first_bank):
    for kc in range(2):
        for oc in range(2):
            q = 2 * kc + oc
            mm = pe.transpose(g.bank(first_bank)[:, q * P:(q + 1) * P], w[:, oc, kc * P:(kc + 1) * P], g.ident[:, :])
    mm.then_inc(turned, 1)


def pe_turn_blocks(g, pe, rows, turned, c, used):
    hold(pe, used, c * CB + 1, g.marks["pe"])
    for k in range(CB):
        for f in range(2):
            mm = pe.transpose(g.bank(k // 2)[:, (k % 2) * D + f * P:(k % 2) * D + (f + 1) * P],
                              rows[:, k, f * P:(f + 1) * P], g.ident[:, :])
        mm.then_inc(turned, 1)


def act_take_blocks(g, act, dst, turned, taken, c):
    for k in range(CB):
        hold(act, turned, c * CB + min(k // 2 * 2 + 2, CB), g.marks["act"])
        g.nc.scalar.copy(dst[:, k, :], g.bank(k // 2)[:, (k % 2) * D:(k % 2 + 1) * D]).then_inc(taken, 1)


def qkv_pass(g):
    nc, a = g.nc, g.a
    H1, HD1 = 8, 32
    g.qs = Place(nc, g.slot2, "qkv1")("qs", [P, NB, 2, D], F16)
    t = Place(nc, g.rest, "qkv")
    wraw = [t(f"wraw{i}", [P, 2, D], F32) for i in range(3)]
    wkv = t("wkv", [P, 2, 2 * D], F32)
    wq = t("wq", [P, 2, D], F32)
    z = t("z", [P, CB, D], F32)
    xs = t("xs", [P, CB, D], F32)
    xsT = t("xsT", [P, CB, D], F32)
    q32 = t("q32", [P, CB, D], F32)
    kvs = t("kvs", [P, CB, 2 * D], F32)
    norm = Norm(g, t, "q")
    mv, rstd = norm.mv, norm.rstd
    w_in, w_turned, w_ready = g.sem("q_w_in"), g.sem("q_w_turned"), g.sem("q_w_ready")
    xs_ready, xs_turned, xt_ready = g.sem("q_xs_ready"), g.sem("q_xs_turned"), g.sem("q_xt_ready")
    kv_done, kv_taken, q_done, q_taken = g.sem("q_kv_done"), g.sem("q_kv_taken"), g.sem("q_q_done"), g.sem("q_q_taken")
    kv_out = [g.sem(f"q_kv_out{k}") for k in range(CB)]
    KVB, QB = [3, 4, 3, 4, 3], [5, 6, 5, 6, 5]

    with nc.Block() as block:
        @block.sync
        def _(sp):
            for i, name in enumerate(("L1_gnn_Wk", "L1_gnn_Wv", "L1_gnn_Wq")):
                sp.dma_start(wraw[i][:, :, :], a[name].rearrange("(c p) n -> p c n", p=P)).then_inc(w_in, 16)
            with sp.Fori(0, CH) as c:
                for k in range(CB):
                    hold(sp, kv_taken, c * CB + (k + 4), g.marks["sp"])
                    sp.dma_start(g.kv1[bass.ds(c * CW + k * P, P), :], kvs[:, k, :]).then_inc(kv_out[k], 16)
            for k in range(CB):
                sp.wait_ge(kv_out[k], 16 * CH + 1)

        @block.gpsimd
        def _(pool):
            norm.roots(pool, CH)

        @block.tensor
        def _(pe):
            pe.wait_ge(w_in, 48)
            for i in range(3):
                pe_turn(g, pe, wraw[i], w_turned, i)
            pe.wait_ge(w_ready, 3)
            pe.sem_inc(xt_ready, 1)
            with pe.Fori(0, CH) as c:
                hold(pe, xs_ready, c + 1, g.marks["pe"])
                pe_turn_blocks(g, pe, xs, xs_turned, c, xt_ready)
                for k in range(CB):
                    hold(pe, xt_ready, c * CB + (k + 2), g.marks["pe"])
                    hold(pe, kv_taken, c * CB + (k + ZWAIT[k]), g.marks["pe"])
                    for f in range(2):
                        mm = pe.matmul(g.bank(KVB[k]), xsT[:, k, f * P:(f + 1) * P], wkv[:, f, :],
                                       start=(f == 0), stop=(f == 1))
                    mm.then_inc(kv_done, 1)
                    hold(pe, q_taken, c * CB + (k + ZWAIT[k]), g.marks["pe"])
                    for f in range(2):
                        mm = pe.matmul(g.bank(QB[k])[:, 0:D], xsT[:, k, f * P:(f + 1) * P], wq[:, f, :],
                                       start=(f == 0), stop=(f == 1))
                    mm.then_inc(q_done, 1)

        @block.scalar
        def _(act):
            act.sem_inc(kv_taken, 3)
            for k in range(CB):
                act.sem_inc(kv_out[k], 1)
            act.wait_ge(w_turned, 3)
            for i, dst in enumerate((wkv[:, :, 0:D], wkv[:, :, D:2 * D], wq[:, :, :])):
                nc.scalar.copy(dst, g.bank(i).rearrange("p (k n) -> p k n", k=2)).then_inc(w_ready, 1)
            with act.Fori(0, CH) as c:
                act_take_blocks(g, act, xsT, xs_turned, xt_ready, c)
                for k in range(CB):
                    hold(act, kv_done, c * CB + (k + 1), g.marks["act"])
                    hold(act, kv_out[k], c * 16 + 1, g.marks["act"])
                    nc.scalar.copy(kvs[:, k, :], g.bank(KVB[k])).then_inc(kv_taken, 1)

        @block.vector
        def _(dve):
            v = nc.vector
            dve.wait_ge(norm.cleared, 1)
            dve.sem_inc(q_taken, 3)
            with dve.Fori(0, CH) as c:
                blocks = bass.ds(c * CB, CB)
                v.tensor_tensor(z[:, :, :], g.x[:, blocks, :], g.h[:, blocks, :], ALU.add)
                dve.drain()
                norm.rows(dve, z, CB, c)
                hold(dve, xt_ready, c * CB + 1, g.marks["dve"])
                for k in range(CB):
                    v.tensor_scalar(xs[:, k, :], z[:, k, :], mv[:, k, 0:1], rstd[:, k:k + 1], ALU.subtract, ALU.mult)
                dve.drain().then_inc(xs_ready, 1)
                v.tensor_copy(g.x[:, blocks, :], xs[:, :, :])
                for k in range(CB):
                    hold(dve, q_done, c * CB + (k + 1), g.marks["dve"])
                    v.tensor_scalar(q32[:, k, :], g.bank(QB[k])[:, 0:D], float(HD1) ** 0.5, None, ALU.mult)\
                        .then_inc(q_taken, 1)
                dve.drain()
                split16(nc, dve, g.qs[:, blocks, 0, :], g.qs[:, blocks, 1, :], q32[:, :, :])
                dve.drain()


def attention(g, layer):
    nc = g.nc
    H = 8 if layer == 1 else 4
    HD = D // H
    R = KB * H
    table = g.kv1 if layer == 1 else g.kv3
    col = C_SRC if layer == 1 else C_REL
    BATCHES = TILES // KB
    g.acc = Place(nc, g.slot1, f"att{layer}a")("acc", [P, NB, H, HD + 1], F32)
    t = Place(nc, g.rest, f"att{layer}")
    kv = [t(f"kv{q}", [P, KB, 2 * D], F32) for q in range(2)]
    pay = [t(f"pay{q}", [P, KB, ROW], I32) for q in range(2)]
    oh = [t(f"oh{q}", [P, KB, P], F32) for q in range(2)]
    ohT = [t(f"ohT{q}", [P, KB, P], BF16) for q in range(2)]
    av = t("av", [P, KB, H, HD + 1], F32)
    prod = t("prod", [P, 4, D], F32)
    loc = t("loc", [P, KB], F32)
    drep = t("drep", [P, KB, H], F32)
    sc = t("sc", [P, KB, H], F32)
    arg = t("arg", [P, KB, H], F32)
    dT = t("dT", [P, P], F32)
    neq = t("neq", [P, P + 1], F32)
    pen = t("pen", [P, P], F32)
    run = t("run", [P, P], F32)
    lmT = t("lmT", [P, P], F32)
    lme = t("lme", [P, KB, H + 1], F32)
    absent = t("absent", [P, KB], F32)
    mrun = t("mrun", [P, NB, H], BF16)
    mk = [t(f"mk{q}", [P, KB, H], BF16) for q in range(2)]
    dd = t("dd", [P, KB, H], F32)
    cf = t("cf", [P, KB, H], F32)

    n = f"t{layer}_"
    pay_ready = [g.sem(f"{n}pay_ready{q}") for q in range(2)]
    pay_used = [g.sem(f"{n}pay_used{q}") for q in range(2)]
    kv_used = [g.sem(f"{n}kv_used{q}") for q in range(2)]
    (oh_ready, ohT_done, ohT_ready, qe_done, qe_used, sc_ready, st_done, lm_ready, lmT_done, lme_ready, mt_done,
     mk_ready, cf_ready, me_done, arg_ready, a_ready, av_ready, po_done, po_used) = (
        g.sem(n + s) for s in ("oh_ready", "ohT_done", "ohT_ready", "qe_done", "qe_used", "sc_ready", "st_done",
                               "lm_ready", "lmT_done", "lme_ready", "mt_done", "mk_ready", "cf_ready", "me_done",
                               "arg_ready", "a_ready", "av_ready", "po_done", "po_used"))
    kv_ready = [[g.sem(f"{n}kv_ready{q}_{k}") for k in range(KB)] for q in range(2)]
    sT, dTp, lmp = g.bank(6)[0:R, 0:P], g.bank(6)[0:R, P:2 * P], g.bank(6)[:, 2 * P:2 * P + R]
    mtp = g.bank(7)[:, 0:KB * (H + 1)].rearrange("p (k h) -> p k h", k=KB)
    mep = g.bank(7)[:, 256:256 + R].rearrange("p (k h) -> p k h", k=KB)

    def batches(eng, body):
        with eng.Fori(0, BATCHES // 2) as i:
            for q in range(2):
                body(i, i * 2 + q, q)

    with nc.Block() as block:
        @block.sync
        def _(sp):
            def body(i, j, q):
                hold(sp, pay_used[q], i + 1, g.marks["sp"])
                for k in range(KB):
                    e0 = sp.value_load(g.tile_e0[0:1, bass.ds(j * KB + k, 1)], min_val=0, max_val=E)
                    sp.dma_start(pay[q][:, k, :], g.edge_rows[bass.ds(e0, P), :]).then_inc(pay_ready[q], 16)

            batches(sp, body)

        @block.gpsimd
        def _(pool):
            def body(i, j, q):
                hold(pool, pay_ready[q], i * (16 * KB) + 16 * KB, g.marks["pool"])
                hold(pool, kv_used[q], i + 1, g.marks["pool"])
                for k in range(KB):
                    pool.indirect_dma_start(kv[q][:, k, :], None, table,
                                            bass.IndirectOffsetOnAxis(ap=pay[q][:, k, col:col + 1], axis=0))\
                        .then_inc(kv_ready[q][k], 16)

            batches(pool, body)

        @block.tensor
        def _(pe):
            def turn(j, q, s):
                for k in range(4 * s, 4 * s + 4):
                    hold(pe, oh_ready, j * KB + (k + 1), g.marks["pe"])
                    mm = pe.transpose(g.bank(s % 2)[:, (k % 4) * P:(k % 4 + 1) * P], oh[q][:, k, :], g.ident[:, :])
                mm.then_inc(ohT_done, 1)

            def queries(j, q, s):
                hold(pe, ohT_ready, j * 4 + (s + 1), g.marks["pe"])
                for k in range(4 * s, 4 * s + 4):
                    blk = pe.value_load(g.tile_blk[0:1, bass.ds(j * KB + k, 1)], min_val=0, max_val=NB - 1)
                    hold(pe, qe_used, j * KB + (k + 1), g.marks["pe"])
                    for part in range(2):
                        mm = pe.matmul(g.bank(2 + k % 2)[:, 0:D], ohT[q][:, k, :],
                                       g.qs[:, bass.ds(blk, 1), part, :].rearrange("p b n -> p (b n)"),
                                       start=(part == 0), stop=(part == 1))
                    mm.then_inc(qe_done, 1)

            def body(i, j, q):
                turn(j, q, 0)
                turn(j, q, 1)
                queries(j, q, 0)
                turn(j, q, 2)
                queries(j, q, 1)
                turn(j, q, 3)
                queries(j, q, 2)
                queries(j, q, 3)
                hold(pe, sc_ready, j + 1, g.marks["pe"])
                pe.transpose(sT, sc[:, :, :].rearrange("p k h -> p (k h)"), g.ident[:, :])
                pe.transpose(dTp, drep[:, :, :].rearrange("p k h -> p (k h)"), g.ident[:, :]).then_inc(st_done, 1)
                hold(pe, lm_ready, j + 1, g.marks["pe"])
                pe.transpose(lmp, lmT[0:R, :], g.ident[0:R, 0:R]).then_inc(lmT_done, 1)
                hold(pe, lme_ready, j + 1, g.marks["pe"])
                for k in range(KB):
                    mm = pe.matmul(mtp[:, k, :], oh[q][:, k, :], lme[:, k, :], start=True, stop=True)
                mm.then_inc(mt_done, 1)
                hold(pe, mk_ready, j + 1, g.marks["pe"])
                for k in range(KB):
                    mm = pe.matmul(mep[:, k, :], ohT[q][:, k, :], mk[q][:, k, :], start=True, stop=True)
                mm.then_inc(me_done, 1)
                for k in range(KB):
                    hold(pe, av_ready, j * KB + (k + 1), g.marks["pe"])
                    hold(pe, po_used, j * KB + (k + 1), g.marks["pe"])
                    pe.matmul(g.bank(4 + k % 2)[:, 0:D + H], oh[q][:, k, :],
                              av[:, k, :, :].rearrange("p h d -> p (h d)"), start=True, stop=True).then_inc(po_done, 1)

            batches(pe, body)

        @block.scalar
        def _(act):
            def body(i, j, q):
                for s in range(4):
                    hold(act, ohT_done, j * 4 + (s + 1), g.marks["act"])
                    nc.scalar.copy(ohT[q][:, 4 * s:4 * s + 4, :].rearrange("p k n -> p (k n)"), g.bank(s % 2))\
                        .then_inc(ohT_ready, 1)
                hold(act, mk_ready, j + 1, g.marks["act"])
                nc.scalar.activation(cf[:, :, :], dd[:, :, :], ACT.Exp).then_inc(cf_ready, 1)
                hold(act, arg_ready, j + 1, g.marks["act"])
                nc.scalar.activation(av[:, :, :, HD], arg[:, :, :], ACT.Exp).then_inc(a_ready, 1)

            batches(act, body)

        @block.vector
        def _(dve):
            v = nc.vector
            v.memset(g.acc[:, :, :, :], 0.0)
            v.memset(mrun[:, :, :], -BIG)
            v.memset(neq[:, :], 1.0)
            v.memset(lme[:, :, H:H + 1], 1.0)
            for q in range(2):
                dve.sem_inc(pay_used[q], 1)
                dve.sem_inc(kv_used[q], 1)
            dve.sem_inc(qe_used, 2)
            dve.sem_inc(po_used, 2)
            dve.drain()

            def body(i, j, q):
                hold(dve, pay_ready[q], i * (16 * KB) + 16 * KB, g.marks["dve"])
                dst = pay[q][:, :, C_DST].bitcast(F32)
                v.tensor_tensor(loc[:, :], dst, g.tile_base[:, bass.ds(j * KB, KB)], ALU.subtract)
                v.tensor_copy(drep[:, :, :], dst.unsqueeze(2).broadcast_to([P, KB, H]))
                dve.drain()
                for k in range(KB):
                    v.tensor_scalar(oh[q][:, k, :], g.iota[:, :], loc[:, k:k + 1], None, ALU.is_equal)\
                        .then_inc(oh_ready, 1)
                for s in range(4):
                    for k in range(4 * s, 4 * s + 4):
                        hold(dve, kv_ready[q][k], i * 16 + 16, g.marks["dve"])
                        hold(dve, qe_done, j * KB + (k + 1), g.marks["dve"])
                        v.tensor_tensor(prod[:, k % 4, :], kv[q][:, k, 0:D], g.bank(2 + k % 2)[:, 0:D], ALU.mult)\
                            .then_inc(qe_used, 1)
                    dve.drain()
                    v.tensor_reduce(sc[:, 4 * s:4 * s + 4, :].rearrange("p k h -> p (k h)"),
                                    prod[:, :, :].rearrange("p k (h d) -> p (k h) d", h=H), AX, ALU.add)
                    dve.drain()
                if layer == 1:
                    v.tensor_tensor(sc[:, :, :], sc[:, :, :], pay[q][:, :, C_ATTR:C_ATTR + H].bitcast(F32), ALU.add)
                    dve.drain()
                dve.drain().then_inc(sc_ready, 1)
                dve.sem_inc(pay_used[q], 1)
                hold(dve, st_done, j + 1, g.marks["dve"])
                v.tensor_copy(dT[0:R, :], dTp)
                dve.drain()
                v.tensor_tensor(neq[0:R, 1:P], dT[0:R, 1:P], dT[0:R, 0:P - 1], ALU.not_equal)
                dve.drain()
                v.tensor_scalar(pen[0:R, :], neq[0:R, 0:P], -BIG, None, ALU.mult)
                dve.drain()
                v.tensor_tensor_scan(run[0:R, :], pen[0:R, :], sT, -BIG, ALU.add, ALU.max)
                dve.drain()
                v.tensor_tensor(lmT[0:R, :], run[0:R, :], neq[0:R, 1:P + 1], ALU.mult).then_inc(lm_ready, 1)
                hold(dve, lmT_done, j + 1, g.marks["dve"])
                v.tensor_copy(lme[:, :, 0:H], lmp.rearrange("p (k h) -> p k h", k=KB)).then_inc(lme_ready, 1)
                hold(dve, mt_done, j + 1, g.marks["dve"])
                v.tensor_scalar(absent[:, :], mtp[:, :, H], 0.5, -BIG, ALU.is_lt, ALU.mult)
                dve.drain()
                for k in range(KB):
                    blk = dve.value_load(g.tile_blk[0:1, bass.ds(j * KB + k, 1)], min_val=0, max_val=NB - 1)
                    now = mrun[:, bass.ds(blk, 1), :].rearrange("p b h -> p (b h)")
                    v.scalar_tensor_tensor(mk[q][:, k, :], mtp[:, k, 0:H], absent[:, k:k + 1], now, ALU.add, ALU.max)
                    dve.drain()
                    v.tensor_tensor(dd[:, k, :], now, mk[q][:, k, :], ALU.subtract)
                    dve.drain()
                    v.tensor_copy(now, mk[q][:, k, :])
                    dve.drain()
                dve.drain().then_inc(mk_ready, 1)
                hold(dve, me_done, j + 1, g.marks["dve"])
                v.tensor_tensor(arg[:, :, :], sc[:, :, :], mep, ALU.subtract)
                dve.drain()
                v.tensor_scalar(arg[:, :, :], arg[:, :, :], 10.0, None, ALU.min)
                dve.drain().then_inc(arg_ready, 1)
                hold(dve, a_ready, j + 1, g.marks["dve"])
                for k in range(KB):
                    v.tensor_tensor(av[:, k, :, 0:HD], kv[q][:, k, D:2 * D].rearrange("p (h d) -> p h d", h=H),
                                    av[:, k, :, HD:HD + 1].broadcast_to([P, H, HD]), ALU.mult).then_inc(av_ready, 1)
                dve.drain().then_inc(kv_used[q], 1)
                hold(dve, cf_ready, j + 1, g.marks["dve"])
                for k in range(KB):
                    blk = dve.value_load(g.tile_blk[0:1, bass.ds(j * KB + k, 1)], min_val=0, max_val=NB - 1)
                    rows = g.acc[:, bass.ds(blk, 1), :, :].rearrange("p b h d -> p (b h) d")
                    v.tensor_tensor(rows, rows, cf[:, k, :].unsqueeze(2).broadcast_to([P, H, HD + 1]), ALU.mult)
                    hold(dve, po_done, j * KB + (k + 1), g.marks["dve"])
                    dve.drain()
                    v.tensor_tensor(rows, rows, g.bank(4 + k % 2)[:, 0:D + H].rearrange("p (h d) -> p h d", h=H),
                                    ALU.add).then_inc(po_used, 1)
                    dve.drain()

            batches(dve, body)


def weighted_rows(g, dve, os, rec, c, H, k):
    HD = D // H
    v = g.nc.vector
    rows = g.acc[:, bass.ds(c * CB + k, 1), :, :].rearrange("p b h d -> p (b h) d")
    v.tensor_scalar(rec[:, k, 0:H], rows[:, :, HD], 1e-30, None, ALU.max)
    dve.drain()
    v.reciprocal(rec[:, k, 0:H], rec[:, k, 0:H])
    dve.drain()
    v.tensor_tensor(os[:, k, :].rearrange("p (h d) -> p h d", h=H), rows[:, :, 0:HD],
                    rec[:, k, 0:H].unsqueeze(2).broadcast_to([P, H, HD]), ALU.mult)


def attention_out(g):
    nc, a = g.nc, g.a
    g.xs16 = Place(nc, g.slot2, "out1x")("xs16", [P, NB, 2, D], F16)
    t = Place(nc, g.rest, "out1")
    wraw, wo = t("wraw", [P, 2, D], F32), t("wo", [P, 2, D], F32)
    os, osT, z = t("os", [P, CB, D], F32), t("osT", [P, CB, D], F32), t("z", [P, CB, D], F32)
    rec = t("rec", [P, CB, 8], F32)
    norm = Norm(g, t, "o")
    mv, rstd = norm.mv, norm.rstd
    w_in, w_turned, w_ready = g.sem("o_w_in"), g.sem("o_w_turned"), g.sem("o_w_ready")
    os_ready, os_turned, ost_ready = g.sem("o_os_ready"), g.sem("o_os_turned"), g.sem("o_ost_ready")
    y_done, y_taken = g.sem("o_y_done"), g.sem("o_y_taken")

    with nc.Block() as block:
        @block.sync
        def _(sp):
            sp.dma_start(wraw[:, :, :], a["L1_gnn_Wo"].rearrange("(c p) n -> p c n", p=P)).then_inc(w_in, 16)

        @block.gpsimd
        def _(pool):
            norm.roots(pool, CH)

        @block.tensor
        def _(pe):
            pe.wait_ge(w_in, 16)
            pe_turn(g, pe, wraw, w_turned, 3)
            pe.wait_ge(w_ready, 1)
            pe.sem_inc(ost_ready, 1)
            with pe.Fori(0, CH) as c:
                hold(pe, os_ready, c + 1, g.marks["pe"])
                pe_turn_blocks(g, pe, os, os_turned, c, ost_ready)
                for k in range(CB):
                    hold(pe, ost_ready, c * CB + (k + 2), g.marks["pe"])
                    hold(pe, y_taken, c * CB + (k + ZWAIT[k]), g.marks["pe"])
                    for f in range(2):
                        mm = pe.matmul(g.bank(ZBANK[k])[:, 0:D], osT[:, k, f * P:(f + 1) * P], wo[:, f, :],
                                       start=(f == 0), stop=(f == 1))
                    mm.then_inc(y_done, 1)

        @block.scalar
        def _(act):
            act.wait_ge(w_turned, 1)
            nc.scalar.copy(wo[:, :, :], g.bank(3).rearrange("p (k n) -> p k n", k=2)).then_inc(w_ready, 1)
            with act.Fori(0, CH) as c:
                act_take_blocks(g, act, osT, os_turned, ost_ready, c)

        @block.vector
        def _(dve):
            v = nc.vector
            dve.wait_ge(norm.cleared, 1)
            dve.sem_inc(y_taken, 3)
            with dve.Fori(0, CH) as c:
                hold(dve, ost_ready, c * CB + 1, g.marks["dve"])
                for k in range(CB):
                    weighted_rows(g, dve, os, rec, c, 8, k)
                dve.drain().then_inc(os_ready, 1)
                for k in range(CB):
                    hold(dve, y_done, c * CB + (k + 1), g.marks["dve"])
                    v.tensor_tensor(z[:, k, :], g.bank(ZBANK[k])[:, 0:D],
                                    g.x[:, bass.ds(c * CB + k, 1), :].rearrange("p b n -> p (b n)"), ALU.add)\
                        .then_inc(y_taken, 1)
                dve.drain()
                norm.rows(dve, z, CB, c)
                for k in range(CB):
                    v.tensor_scalar(z[:, k, :], z[:, k, :], mv[:, k, 0:1], rstd[:, k:k + 1], ALU.subtract, ALU.mult)
                dve.drain()
                blocks = bass.ds(c * CB, CB)
                v.tensor_copy(g.x[:, blocks, :], z[:, :, :])
                split16(nc, dve, g.xs16[:, blocks, 0, :], g.xs16[:, blocks, 1, :], z[:, :, :])
                dve.drain()


def mean_layer(g):
    nc, a = g.nc, g.a
    HB2 = D // 2
    W = D + HB2
    t = Place(nc, g.rest, "mean")
    abuf = [t(f"abuf{p}", [P, NB, PARTS[p][1] * P], BF16) for p in range(2)]
    nT = [t(f"nT{p}", [P, 2, PARTS[p][1] * P], F32) for p in range(2)]
    xT = [t(f"xT{p}", [P, 2, PARTS[p][1] * P], F32) for p in range(2)]
    wx, wn = t("wx", [P, 2, W], F32), t("wn", [P, 2, W], F32)
    bm, be, bn = t("bm", [P, D], F32), t("be", [P, HB2], F32), t("bn", [P, HB2], F32)
    one = t("one", [P, 1], BF16)
    rd = t("rd", [P, 4], F32)
    u = t("u", [P, 3, W], F32)
    hm, hc, z = t("hm", [P, 3, D], F32), t("hc", [P, 3, D], F32), t("z", [P, 3, D], F32)
    norm = Norm(g, t, "m")
    mv, rstd = norm.mv, norm.rstd
    w_in, one_ready, rd_ready = g.sem("m_w_in"), g.sem("m_one"), g.sem("m_rd_ready")
    agg_done = [g.sem(f"m_agg{p}") for p in range(2)]
    nt_ready = [g.sem(f"m_nt{p}") for p in range(2)]
    p_done, p_used = g.sem("m_p_done"), g.sem("m_p_used")
    piece_sems(g, "m")
    SET = [(6, 7), (4, 5), (6, 7)]

    with nc.Block() as block:
        @block.sync
        def _(sp):
            for w in (wx, wn):
                sp.dma_start(w[:, :, 0:D], a["L2_gnn_W_mean"].rearrange("(c p) n -> p c n", p=P)).then_inc(w_in, 16)
            sp.dma_start(wx[:, :, D:W], a["L2_gnn_W_ego"].rearrange("(c p) n -> p c n", p=P)).then_inc(w_in, 16)
            sp.dma_start(wn[:, :, D:W], a["L2_gnn_W_nb"].rearrange("(c p) n -> p c n", p=P)).then_inc(w_in, 16)
            for row, name in ((bm, "L2_gnn_b_mean"), (be, "L2_gnn_b_ego"), (bn, "L2_gnn_b_nb")):
                sp.dma_start(row[:, :], a[name].unsqueeze(0).broadcast_to(list(row.shape))).then_inc(w_in, 16)
            with sp.Fori(0, CH) as c:
                load_pieces(g, sp, g.adj_ds, abuf, c, c)

        @block.gpsimd
        def _(pool):
            norm.roots(pool, 2 * CH)

        @block.tensor
        def _(pe):
            for p in range(2):
                for j in range(CH):
                    pe.sem_inc(g.a_used[p][j], 1)
            pe.wait_ge(one_ready, 1)
            pe.wait_ge(w_in, 16 * 7)

            def part(c, p):
                k0, nb = PARTS[p]
                w = nb * P
                hold(pe, nt_ready[p], c + 1, g.marks["pe"])
                hold(pe, p_used, c * CB + (k0 + 1), g.marks["pe"])
                for j in range(CH):
                    hold(pe, g.a_loaded[p][j], c * 16 + 16, g.marks["pe"])
                    for s in range(j * CB, (j + 1) * CB):
                        for f in range(2):
                            for half in range(2):
                                pe.matmul(g.bank(2 * p + f)[:, 0:w], g.xs16[:, s, half, f * P:(f + 1) * P],
                                          abuf[p][:, s, :], start=(s == 0 and half == 0), stop=(s == NB - 1 and half == 1))
                for k in range(nb):
                    for s in range(NB):
                        mm = pe.matmul(g.bank(7)[:, k:k + 1], abuf[p][:, s, k * P:(k + 1) * P], one[:, :],
                                       start=(s == 0), stop=(s == NB - 1))
                for f in range(2):
                    for k in range(nb):
                        for half in range(2):
                            lhs = g.xs16[:, bass.ds(c * CB + (k0 + k), 1), half, f * P:(f + 1) * P]\
                                .rearrange("p b n -> p (b n)")
                            mm = pe.matmul(g.bank(4 + f)[:, k * P:(k + 1) * P], lhs, g.ident16[:, :],
                                           start=(half == 0), stop=(half == 1))
                mm.then_inc(agg_done[p], 1)
                hold(pe, nt_ready[p], c + 2, g.marks["pe"])
                for j in range(CH):
                    pe.sem_inc(g.a_used[p][j], 1)
                hold(pe, rd_ready, c * 2 + (p + 1), g.marks["pe"])
                for k in range(nb):
                    if k == 2:
                        hold(pe, p_used, c * CB + (k0 + 2), g.marks["pe"])
                    for bank, rows, wgt in ((SET[k][0], xT, wx), (SET[k][1], nT, wn)):
                        for f in range(2):
                            mm = pe.matmul(g.bank(bank)[:, 0:W], rows[p][:, f, k * P:(k + 1) * P], wgt[:, f, :],
                                           start=(f == 0), stop=(f == 1))
                    mm.then_inc(p_done, 1)

            with pe.Fori(0, CH) as c:
                part(c, 0)
                part(c, 1)

        @block.scalar
        def _(act):
            act.sem_inc(nt_ready[0], 1)
            act.sem_inc(nt_ready[1], 1)
            with act.Fori(0, CH) as c:
                for p in range(2):
                    w = PARTS[p][1] * P
                    hold(act, agg_done[p], c + 1, g.marks["act"])
                    nc.scalar.copy(nT[p][:, :, :], g.psum[:, 2 * p:2 * p + 2, 0:w])
                    nc.scalar.copy(xT[p][:, :, :], g.psum[:, 4:6, 0:w])
                    act.drain().then_inc(nt_ready[p], 1)

        @block.vector
        def _(dve):
            v = nc.vector
            dve.wait_ge(norm.cleared, 1)
            v.memset(one[:, :], 1.0).then_inc(one_ready, 1)
            dve.sem_inc(p_used, 1)
            dve.wait_ge(w_in, 16 * 7)
            with dve.Fori(0, CH) as c:
                for p, (k0, nb) in enumerate(PARTS):
                    hold(dve, agg_done[p], c + 1, g.marks["dve"])
                    v.tensor_scalar(rd[:, 0:nb], g.bank(7)[:, 0:nb], 1.0, None, ALU.max)
                    dve.drain()
                    v.reciprocal(rd[:, 0:nb], rd[:, 0:nb])
                    dve.drain().then_inc(rd_ready, 1)
                    for k in range(nb):
                        hold(dve, p_done, c * CB + (k0 + k + 1), g.marks["dve"])
                        px, pn = g.bank(SET[k][0]), g.bank(SET[k][1])
                        gt = g.gate[:, bass.ds(c * CB + (k0 + k), 1)]
                        ng = g.ngate[:, bass.ds(c * CB + (k0 + k), 1)]
                        v.tensor_scalar(u[:, k, :], pn[:, 0:W], rd[:, k:k + 1], None, ALU.mult)
                        v.tensor_tensor(hc[:, k, 0:HB2], px[:, D:W], be[:, :], ALU.add)
                        dve.drain()
                        v.tensor_tensor(hm[:, k, :], px[:, 0:D], u[:, k, 0:D], ALU.add)
                        dve.drain().then_inc(p_used, 1)
                        v.scalar_tensor_tensor(hm[:, k, :], hm[:, k, :], 0.5, bm[:, :], ALU.mult, ALU.add)
                        v.tensor_tensor(hc[:, k, HB2:D], u[:, k, D:W], bn[:, :], ALU.add)
                        dve.drain()
                        v.tensor_scalar(hm[:, k, :], hm[:, k, :], ng, None, ALU.mult)
                        dve.drain()
                        v.scalar_tensor_tensor(hm[:, k, :], hc[:, k, :], gt, hm[:, k, :], ALU.mult, ALU.add)
                    dve.drain()
                    v.tensor_tensor(z[:, 0:nb, :], hm[:, 0:nb, :], g.x[:, bass.ds(c * CB + k0, nb), :], ALU.add)
                    dve.drain()
                    norm.rows(dve, z, nb, c * 2 + p)
                    for k in range(nb):
                        v.tensor_scalar(z[:, k, :], z[:, k, :], mv[:, k, 0:1], rstd[:, k:k + 1], ALU.subtract, ALU.mult)
                    dve.drain()
                    v.tensor_copy(g.x[:, bass.ds(c * CB + k0, nb), :], z[:, 0:nb, :])
                    dve.drain()


def typed_pass(g):
    nc, a = g.nc, g.a
    HH, DK = 4, D // 4
    g.qs = Place(nc, g.slot2, "typed1")("qs", [P, NB, 2, D], F16)
    t = Place(nc, g.slot1, "typed")
    w = {n: t(f"w{n}", [P, TYPES, 2, D], F32) for n in "k"}
    t.at = g.rest
    w["q"] = t("wq", [P, TYPES, 2, D], F32)
    w["v"] = t("wv", [P, TYPES, 2, D], F32)
    ra, rm, raT = (t(n, [P, RELS, 2, P], F32) for n in ("ra", "rm", "raT"))
    pri = t("pri", [P, RELS, 2], F32)
    xm = [t(f"xm{q}", [P, TYPES, D], F32) for q in range(2)]
    xmT = t("xmT", [P, 2 * TYPES, 3 * P], F32)
    kvT = t("kvT", [P, 4, 3 * P], F32)
    q32 = t("q32", [P, 3, D], F32)
    tab = t("tab", [P, 2, 4, 2 * D], F32)
    w_in, pri_in, zeroed, ra_scaled, ra_turned, ra_ready = (g.sem("y_w_in"), g.sem("y_pri_in"), g.sem("y_zeroed"),
                                                           g.sem("y_ra_scaled"), g.sem("y_ra_turned"), g.sem("y_ra_ready"))
    xm_ready, xm_turned, xmt_ready = g.sem("y_xm_ready"), g.sem("y_xm_turned"), g.sem("y_xmt_ready")
    kv_done, kv_taken, q_done, q_taken = g.sem("y_kv_done"), g.sem("y_kv_taken"), g.sem("y_q_done"), g.sem("y_q_taken")
    tab_done = g.sem("y_tab_done")
    tab_taken = [g.sem(f"y_tab_taken{q}") for q in range(2)]
    tab_out = [[g.sem(f"y_tab_out{q}{r}") for r in range(4)] for q in range(2)]
    XMB = [0, 1, 0, 1, 0]

    with nc.Block() as block:
        @block.sync
        def _(sp):
            for n, name in (("k", "L3_gnn_k_linears"), ("q", "L3_gnn_q_linears"), ("v", "L3_gnn_v_linears")):
                for ty in range(TYPES):
                    sp.dma_start(w[n][:, ty, :, :], a[name][ty].rearrange("(c p) n -> p c n", p=P)).then_inc(w_in, 16)
            sp.wait_ge(zeroed, 2)
            for dst, name in ((ra, "L3_gnn_relation_att"), (rm, "L3_gnn_relation_msg")):
                for hp in range(2):
                    for h2 in range(2):
                        sp.dma_start(dst[h2 * DK:(h2 + 1) * DK, :, hp, h2 * DK:(h2 + 1) * DK],
                                     a[name][:, 2 * hp + h2].rearrange("r d e -> d r e")).then_inc(w_in, 16)
            for h2 in range(2):
                sp.dma_start(pri[h2 * DK:(h2 + 1) * DK, :, :],
                             a["L3_gnn_relation_pri"].rearrange("r (a b) -> r a b", b=2)[:, :, h2].unsqueeze(0)
                             .broadcast_to([DK, RELS, 2])).then_inc(w_in, 16)
            with sp.Fori(0, NB) as b:
                for r in range(RELS):
                    q, k = r % 2, r // 2
                    hold(sp, tab_taken[q], b * 4 + (k + 2), g.marks["sp"])
                    sp.dma_start(g.kv3[bass.ds(b * P + r * NP, P), :], tab[:, q, k, :]).then_inc(tab_out[q][k], 16)
            for q in range(2):
                for k in range(4):
                    sp.wait_ge(tab_out[q][k], 16 * NB + 1)

        @block.gpsimd
        def _(pool):
            pool.memset(ra[:, :, :, :], 0.0).then_inc(zeroed, 1)
            pool.memset(rm[:, :, :, :], 0.0).then_inc(zeroed, 1)

        @block.tensor
        def _(pe):
            pe.wait_ge(w_in, 16 * 22)
            pe.wait_ge(ra_scaled, 1)
            for r in range(RELS):
                for hp in range(2):
                    n = 2 * r + hp
                    mm = pe.transpose(g.bank(n // 4)[:, (n % 4) * P:(n % 4 + 1) * P], ra[:, r, hp, :], g.ident[:, :])
            mm.then_inc(ra_turned, 1)
            pe.wait_ge(ra_ready, 1)
            pe.sem_inc(xmt_ready, 1)

            def part(c, p):
                k0, nb = PARTS[p]
                wd = nb * P
                for k in range(nb):
                    hold(pe, xm_ready, c * CB + (k0 + k + 1), g.marks["pe"])
                    hold(pe, xmt_ready, c * CB + (k0 + k + 1), g.marks["pe"])
                    for ty in range(TYPES):
                        for f in range(2):
                            n = 2 * ty + f
                            mm = pe.transpose(g.bank(n // 4)[:, (n % 4) * P:(n % 4 + 1) * P],
                                              xm[XMB[k0 + k]][:, ty, f * P:(f + 1) * P], g.ident[:, :])
                    mm.then_inc(xm_turned, 1)
                hold(pe, xmt_ready, c * CB + (k0 + nb + 1), g.marks["pe"])
                for n in range(4):
                    wgt = w["k"] if n < 2 else w["v"]
                    oc = n % 2
                    hold(pe, kv_taken, c * 8 + (p * 4 + n + 1), g.marks["pe"])
                    for ty in range(TYPES):
                        for f in range(2):
                            mm = pe.matmul(g.bank(2 + n % 2)[:, 0:wd], wgt[:, ty, f, oc * P:(oc + 1) * P],
                                           xmT[:, 2 * ty + f, 0:wd], start=(ty == 0 and f == 0),
                                           stop=(ty == TYPES - 1 and f == 1))
                    mm.then_inc(kv_done, 1)
                for k in range(nb):
                    hold(pe, q_taken, c * CB + (k0 + k + 1), g.marks["pe"])
                    for ty in range(TYPES):
                        for f in range(2):
                            mm = pe.matmul(g.bank(4)[:, 0:D], xmT[:, 2 * ty + f, k * P:(k + 1) * P], w["q"][:, ty, f, :],
                                           start=(ty == 0 and f == 0), stop=(ty == TYPES - 1 and f == 1))
                    mm.then_inc(q_done, 1)
                hold(pe, kv_taken, c * 8 + (p * 4 + 6), g.marks["pe"])
                for k in range(nb):
                    for r in range(RELS):
                        hold(pe, tab_taken[r % 2], c * (CB * 4) + ((k0 + k) * 4 + r // 2 + 1), g.marks["pe"])
                        for n in range(4):
                            mm = pe.matmul(g.bank(5 + r % 2)[:, n * P:(n + 1) * P], kvT[:, n, k * P:(k + 1) * P],
                                           (raT if n < 2 else rm)[:, r, n % 2, :], start=True, stop=True)
                        mm.then_inc(tab_done, 1)

            with pe.Fori(0, CH) as c:
                part(c, 0)
                part(c, 1)

        def take_tables(eng, q, c, k0, nb, copy, mark):
            for k in range(nb):
                for r in range(q, RELS, 2):
                    hold(eng, tab_done, c * (CB * RELS) + ((k0 + k) * RELS + r + 1), mark)
                    hold(eng, tab_out[q][r // 2], c * (CB * 16) + ((k0 + k) * 16 + 1), mark)
                    copy(tab[:, q, r // 2, :], g.bank(5 + q)).then_inc(tab_taken[q], 1)

        @block.scalar
        def _(act):
            for q in range(2):
                act.sem_inc(tab_taken[q], 1)
                for k in range(4):
                    act.sem_inc(tab_out[q][k], 1)
            act.sem_inc(kv_taken, 2)
            act.wait_ge(ra_turned, 1)
            nc.scalar.copy(raT[:, :, :, :].rearrange("p r h n -> p (r h n)"),
                           g.psum[:, 0:4, :].rearrange("p b n -> p (b n)")).then_inc(ra_ready, 1)
            with act.Fori(0, CH) as c:
                for p, (k0, nb) in enumerate(PARTS):
                    for k in range(nb):
                        hold(act, xm_turned, c * CB + (k0 + k + 1), g.marks["act"])
                        nc.scalar.copy(xmT[:, :, k * P:(k + 1) * P],
                                       g.psum[:, 0:2, :].rearrange("p b (t n) -> p (b t) n", t=4)).then_inc(xmt_ready, 1)
                    for n in range(4):
                        hold(act, kv_done, c * 8 + (p * 4 + n + 1), g.marks["act"])
                        nc.scalar.copy(kvT[:, n, 0:nb * P], g.bank(2 + n % 2)[:, 0:nb * P]).then_inc(kv_taken, 1)
                    take_tables(act, 0, c, k0, nb, nc.scalar.copy, g.marks["act"])

        @block.vector
        def _(dve):
            v = nc.vector
            dve.sem_inc(q_taken, 1)
            dve.wait_ge(w_in, 16 * 22)
            v.tensor_scalar(pri[:, :, :], pri[:, :, :], float(DK) ** -0.5, None, ALU.mult)
            dve.drain()
            for r in range(RELS):
                for hp in range(2):
                    v.tensor_scalar(ra[:, r, hp, :], ra[:, r, hp, :], pri[:, r, hp:hp + 1], None, ALU.mult)
            dve.drain().then_inc(ra_scaled, 1)

            def mask(c, k):
                for ty in range(TYPES):
                    ins = v.tensor_scalar(xm[XMB[k]][:, ty, :],
                                          g.x[:, bass.ds(c * CB + k, 1), :].rearrange("p b n -> p (b n)"),
                                          g.tmask[:, bass.ds(c * CB + k, 1), ty], None, ALU.mult)
                dve.drain().then_inc(xm_ready, 1)

            with dve.Fori(0, CH) as c:
                for p, (k0, nb) in enumerate(PARTS):
                    for k in range(k0, k0 + nb):
                        hold(dve, xmt_ready, c * CB + (k + 1), g.marks["dve"])
                        mask(c, k)
                    for k in range(nb):
                        hold(dve, q_done, c * CB + (k0 + k + 1), g.marks["dve"])
                        v.tensor_copy(q32[:, k, :], g.bank(4)[:, 0:D]).then_inc(q_taken, 1)
                    dve.drain()
                    blocks = bass.ds(c * CB + k0, nb)
                    split16(nc, dve, g.qs[:, blocks, 0, :], g.qs[:, blocks, 1, :], q32[:, 0:nb, :])
                    take_tables(dve, 1, c, k0, nb, v.tensor_copy, g.marks["dve"])
                    dve.drain()


def typed_out(g):
    nc, a = g.nc, g.a
    t = Place(nc, g.slot2, "fin")
    wa = t("wa", [P, TYPES, 2, D], F32)
    os = t("os", [P, CB, D], F32)
    om = [t(f"om{q}", [P, TYPES, D], F32) for q in range(2)]
    omT = [t(f"omT{q}", [P, 2 * TYPES, P], F32) for q in range(2)]
    z = t("z", [P, CB, D], F32)
    res = t("res", [P, CB, D], F32)
    rec = t("rec", [P, CB, 8], F32)
    norm = Norm(g, t, "f")
    mv, rstd = norm.mv, norm.rstd
    w_in, om_ready, om_turned, omt_ready = g.sem("f_w_in"), g.sem("f_om_ready"), g.sem("f_om_turned"), g.sem("f_omt_ready")
    y_done, y_taken, res_ready, res_out = g.sem("f_y_done"), g.sem("f_y_taken"), g.sem("f_res_ready"), g.sem("f_res_out")
    OMB = [0, 1, 0, 1, 0]
    out_rows = g.out

    with nc.Block() as block:
        @block.sync
        def _(sp):
            for ty in range(TYPES):
                sp.dma_start(wa[:, ty, :, :], a["L3_gnn_a_linears"][ty].rearrange("(c p) n -> p c n", p=P)).then_inc(w_in, 16)
            with sp.Fori(0, CH - 1) as c:
                hold(sp, res_ready, c + 1, g.marks["sp"])
                sp.dma_start(out_rows[bass.ds(c * CW, CW), :].rearrange("(b p) d -> p b d", p=P), res[:, :, :])\
                    .then_inc(res_out, 16)
            sp.wait_ge(res_ready, CH)
            last = (CH - 1) * CW
            sp.dma_start(out_rows[last:last + (CB - 1) * P, :].rearrange("(b p) d -> p b d", p=P),
                         res[:, 0:CB - 1, :]).then_inc(res_out, 16)
            sp.dma_start(out_rows[last + (CB - 1) * P:N, :], res[0:TAIL, CB - 1, :]).then_inc(res_out, 16)
            sp.wait_ge(res_out, 16 * (CH + 1) + 1)

        @block.gpsimd
        def _(pool):
            norm.roots(pool, CH)

        @block.tensor
        def _(pe):
            pe.wait_ge(w_in, 16 * TYPES)
            pe.sem_inc(omt_ready, 1)
            with pe.Fori(0, CH) as c:
                for k in range(CB):
                    hold(pe, om_ready, c * CB + (k + 1), g.marks["pe"])
                    hold(pe, omt_ready, c * CB + (k + 1), g.marks["pe"])
                    for n in range(2 * TYPES):
                        mm = pe.transpose(g.bank(n // 4)[:, (n % 4) * P:(n % 4 + 1) * P],
                                          om[OMB[k]][:, n // 2, (n % 2) * P:(n % 2 + 1) * P], g.ident[:, :])
                    mm.then_inc(om_turned, 1)
                    hold(pe, omt_ready, c * CB + (k + 2), g.marks["pe"])
                    hold(pe, y_taken, c * CB + (k + ZWAIT[k]), g.marks["pe"])
                    for n in range(2 * TYPES):
                        mm = pe.matmul(g.bank(ZBANK[k])[:, 0:D], omT[OMB[k]][:, n, :], wa[:, n // 2, n % 2, :],
                                       start=(n == 0), stop=(n == 2 * TYPES - 1))
                    mm.then_inc(y_done, 1)

        @block.scalar
        def _(act):
            act.sem_inc(res_out, 1)
            with act.Fori(0, CH) as c:
                for k in range(CB):
                    hold(act, om_turned, c * CB + (k + 1), g.marks["act"])
                    nc.scalar.copy(omT[OMB[k]][:, :, :].rearrange("p t n -> p (t n)"),
                                   g.psum[:, 0:2, :].rearrange("p b n -> p (b n)")).then_inc(omt_ready, 1)

        @block.vector
        def _(dve):
            v = nc.vector
            dve.wait_ge(norm.cleared, 1)
            dve.sem_inc(y_taken, 3)
            def take(c, k):
                hold(dve, y_done, c * CB + (k + 1), g.marks["dve"])
                v.tensor_tensor(z[:, k, :], g.bank(ZBANK[k])[:, 0:D],
                                g.x[:, bass.ds(c * CB + k, 1), :].rearrange("p b n -> p (b n)"), ALU.add)\
                    .then_inc(y_taken, 1)

            with dve.Fori(0, CH) as c:
                for k in range(CB):
                    weighted_rows(g, dve, os, rec, c, 4, k)
                    hold(dve, omt_ready, c * CB + (k + 1), g.marks["dve"])
                    dve.drain()
                    for ty in range(TYPES):
                        v.tensor_scalar(om[OMB[k]][:, ty, :], os[:, k, :], g.smask[:, bass.ds(c * CB + k, 1), ty],
                                        None, ALU.mult)
                    dve.drain().then_inc(om_ready, 1)
                    if k > 0:
                        take(c, k - 1)
                take(c, CB - 1)
                dve.drain()
                norm.rows(dve, z, CB, c)
                hold(dve, res_out, c * 16 + 1, g.marks["dve"])
                for k in range(CB):
                    v.tensor_scalar(res[:, k, :], z[:, k, :], mv[:, k, 0:1], rstd[:, k:k + 1], ALU.subtract, ALU.mult)
                dve.drain().then_inc(res_ready, 1)


_INS = ["x", "src", "dst", "edge_attr_8", "edge_type_8", "node_type_4", "node_vec",
        "L0_gnn_W1", "L0_gnn_b1", "L0_gnn_W2", "L0_gnn_b2", "L0_gnn_eps", "L0_gnn_gamma", "L0_gnn_beta",
        "L1_gnn_Wq", "L1_gnn_Wk", "L1_gnn_Wv", "L1_gnn_Wo",
        "L2_gnn_W_mean", "L2_gnn_b_mean", "L2_gnn_W_ego", "L2_gnn_b_ego", "L2_gnn_W_nb", "L2_gnn_b_nb",
        "L2_gnn_gate_weight", "L2_gnn_gate_bias",
        "L3_gnn_k_linears", "L3_gnn_q_linears", "L3_gnn_v_linears", "L3_gnn_a_linears", "L3_gnn_relation_att",
        "L3_gnn_relation_msg", "L3_gnn_relation_pri", "L3_gnn_skip"]


def kernel(**inputs):
    import numpy as _np
    import concourse.bacc as _bacc
    from concourse import mybir as _mybir
    from concourse.bass_utils import run_bass_kernel_spmd as _run

    nc = _bacc.Bacc("TRN2", target_bir_lowering=False, num_devices=1)
    arrays, a = {}, {}
    for name in _INS:
        v = _np.ascontiguousarray(inputs[name])
        arrays[f"in_{name}"] = v
        a[name] = nc.dram_tensor(f"in_{name}", v.shape, _mybir.dt.from_np(v.dtype), kind="ExternalInput").ap()
    out = nc.dram_tensor("out_0", (N, D), F32, kind="ExternalOutput").ap()
    program(nc, a, out)
    r = _run(nc, [arrays], core_ids=[0])
    return r.results[0]["out_0"]
```

```python
from contextlib import ExitStack

import concourse.bass as bass
from concourse import mybir

P = 128
N = 3125
E = 50000
D = 256
NB = -(-N // P)
NP = NB * P
TAIL = N - (NB - 1) * P
LAYERS = 4
CH = 5
CB = NB // CH
CW = CB * P
PARTS = [(0, 3), (3, 2)]
LN_EPS = 1e-5
BIG = 1.0e30
GT = 4
GE = GT * P
BG = 4
BATCHES = -(-(E // GE + NB) // BG) // 2 * 2 + 1
GROUPS = BG * BATCHES
EP, EF = 80, E // 80
ROW = 16
C_SRC, C_REL, C_DST, C_ATTR = 0, 1, 2, 4
KB = BG * GT
RELS, TYPES = 8, 4

ALU = mybir.AluOpType
ACT = mybir.ActivationFunctionType
AX = mybir.AxisListType.X
F32 = mybir.dt.float32
F16 = mybir.dt.float16
BF16 = mybir.dt.bfloat16
I32 = mybir.dt.int32


class Place:

    def __init__(self, nc, base, stage):
        self.nc, self.at, self.stage = nc, base, stage

    def __call__(self, name, shape, dt):
        size = 2 if dt in (F16, BF16) else 4
        for s in shape[1:]:
            size *= s
        t = self.nc.alloc_sbuf_tensor_at(f"{self.stage}_{name}", shape, dt, offset=self.at)
        self.at += -(-size // 32) * 32
        return t


def hold(eng, sem, value, marks):
    eng.wait_ge(sem, value)
    eng.sem_inc(marks, 1)


class G:
    pass


def program(nc, a, out):
    with ExitStack() as ctx:
        g = G()
        g.nc, g.a, g.out = nc, a, out
        g.stage_sems = []

        def sem(name):
            handle = nc.alloc_semaphore(name)
            g.stage_sems.append(handle)
            return handle

        g.sem = sem
        keep = lambda name, shape, dt: ctx.enter_context(nc.sbuf_tensor(name, shape, dt))
        dram = lambda name, shape, dt: nc.dram_tensor(name, shape, dt, kind="Internal").ap()
        ctx.enter_context(nc.allow_non_contiguous_dma(reason="small vectors and broadcasts, once"))
        g.psum = ctx.enter_context(nc.psum_tensor("psum", [P, 8, 512], F32))
        g.bank = lambda b: g.psum[:, b, :]
        g.marks = {e: nc.alloc_semaphore(f"marks_{e}") for e in ("sp", "act", "pool", "pe", "dve")}

        g.ident = keep("ident", [P, P], F32)
        g.ident16 = keep("ident16", [P, P], F16)
        g.identb = keep("identb", [P, P], BF16)
        g.iota = keep("iota", [P, P], F32)
        g.group_e0 = keep("group_e0", [P, GROUPS], I32)
        g.group_blk = keep("group_blk", [P, GROUPS], I32)
        g.group_base = keep("group_base", [P, GROUPS], F32)
        g.gate = keep("gate", [P, NB], F32)
        g.ngate = keep("ngate", [P, NB], F32)
        g.tmask = keep("tmask", [P, NB, TYPES], F32)
        g.smask = keep("smask", [P, NB, TYPES], F32)

        base = nc.sbuf_base
        g.base = -(-base // 32) * 32
        g.x = nc.alloc_sbuf_tensor_at("x_nodes", [P, NB, D], F32, offset=g.base)
        g.after_x = g.base + NB * D * 4
        g.slot1 = g.after_x
        g.slot2 = g.slot1 + 27136
        g.rest = g.slot2 + NB * 2 * D * 2

        g.edge_rows = dram("edge_rows", [E + GE, ROW], I32)
        g.src_f = dram("src_f", [E + GE], F32)
        g.dst_f = dram("dst_f", [E + GE], F32)
        g.adj_sd = [dram(f"adj_sd{p}", [CH, P, NB, PARTS[p][1] * P], F16) for p in range(2)]
        g.adj_ds = [dram(f"adj_ds{p}", [CH, P, NB, PARTS[p][1] * P], F16) for p in range(2)]
        g.kv1 = dram("kv1", [NP, 2 * D], F32)
        g.kv3 = dram("kv3", [RELS * NP, 2 * D], F32)

        stages = [
            lambda: prepare(g),
            lambda: build_adjacency(g),
            lambda: store_adjacency(g),
            lambda: gin_layers(g),
            lambda: qkv_pass(g),
            lambda: attention(g, 1),
            lambda: attention_out(g),
            lambda: mean_layer(g),
            lambda: typed_pass(g),
            lambda: attention(g, 3),
            lambda: typed_out(g),
        ]
        for stage in stages:
            stage()
            nc.clear_and_free_semaphores(g.stage_sems)
            nc.all_engine_barrier()
            g.stage_sems = []


def prepare(g):
    nc, a = g.nc, g.a
    adj_at = (nc.sbuf_usable_end - NB * NP * 2) // 32 * 32
    g.adj = Place(nc, adj_at, "adj")("rows", [P, NB, NP], F16)
    t = Place(nc, g.base, "prep")
    IW = max(P, GROUPS)
    srci = t("srci", [EP, EF], I32)
    dsti = t("dsti", [EP, EF], I32)
    etyi = t("etyi", [EP, EF], I32)
    attr = t("attr", [EP, EF, 8], F32)
    srcf = t("srcf", [EP, EF], F32)
    dstf = t("dstf", [EP, EF], F32)
    relf = t("relf", [EP, EF], F32)
    rows = t("rows", [EP, EF, ROW], I32)
    less = t("less", [EP, 26, EF // 5], F32)
    lessp = t("lessp", [EP, 5, 26], F32)
    lessc = t("lessc", [EP, 26], F32)
    bndi = t("bndi", [P, 26], I32)
    bnd = t("bnd", [P, 26], F32)
    ones = t("ones", [P, P], F32)
    iotai = t("iotai", [P, IW], I32)
    iotaf = t("iotaf", [P, IW], F32)
    start = t("start", [P, 26], F32)
    cnt = t("cnt", [P, 26], F32)
    cnti = t("cnti", [P, 26], I32)
    cnt2 = t("cnt2", [P, 26], I32)
    zero = t("zero", [P, 32], F32)
    tb = t("tb", [P, 32], F32)
    off = t("off", [P, 32], F32)
    step = t("step", [P, 32], F32)
    cmp = t("cmp", [P, GROUPS, NB], F32)
    blkf = t("blkf", [P, GROUPS], F32)
    e0f = t("e0f", [P, GROUPS], F32)
    padrow = t("padrow", [P, GT, ROW], I32)
    padf = t("padf", [1, GE], F32)
    nvec = t("nvec", [32, P], F32)
    ntypi = t("ntypi", [32, P], I32)
    ntyp = t("ntyp", [32, P], F32)
    nv = t("nv", [P, 32], F32)
    nt = t("nt", [P, 32], F32)
    gw = t("gw", [P, 2], F32)
    skip = t("skip", [P, TYPES], F32)

    g.cleared_from = max(0, -(-(t.at - adj_at) // (NP * 2)))
    assert g.cleared_from < NB

    loaded, consts, zeroed = g.sem("p_loaded"), g.sem("p_consts"), g.sem("p_zeroed")
    less_ready, starts_ready, node_rows, nodes_t = (g.sem("p_less"), g.sem("p_starts"), g.sem("p_node_rows"),
                                                    g.sem("p_nodes_t"))
    rows_ready, stored, pads, gate_in, gate_out = (g.sem("p_rows"), g.sem("p_stored"), g.sem("p_pads"),
                                                   g.sem("p_gate_in"), g.sem("p_gate_out"))

    with nc.Block() as block:
        @block.sync
        def _(sp):
            for dst, src in ((dsti, a["dst"]), (srci, a["src"]), (etyi, a["edge_type_8"])):
                sp.dma_start(dst[:, :], src.rearrange("(p e) -> p e", p=EP)).then_inc(loaded, 16)
            sp.dma_start(attr[:, :, :], a["edge_attr_8"].rearrange("(p e) h -> p e h", p=EP)).then_inc(loaded, 16)
            sp.dma_start(gw[:, 0:1], a["L2_gnn_gate_weight"].unsqueeze(0).broadcast_to([P, 1])).then_inc(loaded, 16)
            sp.dma_start(gw[:, 1:2], a["L2_gnn_gate_bias"].unsqueeze(0).broadcast_to([P, 1])).then_inc(loaded, 16)
            sp.dma_start(skip[:, :], a["L3_gnn_skip"].unsqueeze(0).broadcast_to([P, TYPES])).then_inc(loaded, 16)
            sp.wait_ge(zeroed, 2)
            for dst, src in ((nvec, a["node_vec"]), (ntypi, a["node_type_4"])):
                sp.dma_start(dst[0:NB - 1, :], src[0:(NB - 1) * P].rearrange("(b p) -> b p", p=P)).then_inc(loaded, 16)
                sp.dma_start(dst[NB - 1:NB, 0:TAIL], src[(NB - 1) * P:N].unsqueeze(0)).then_inc(loaded, 16)
            sp.wait_ge(pads, 2)
            sp.dma_start(g.edge_rows[E:E + GE].rearrange("(p k) w -> p k w", k=GT), padrow[:, :, :]).then_inc(stored, 16)
            sp.dma_start(g.src_f[E:E + GE].unsqueeze(0), padf[:, :]).then_inc(stored, 16)
            sp.dma_start(g.dst_f[E:E + GE].unsqueeze(0), padf[:, :]).then_inc(stored, 16)
            sp.wait_ge(rows_ready, 1)
            sp.dma_start(g.edge_rows[0:E].rearrange("(p e) w -> p e w", p=EP), rows[:, :, :]).then_inc(stored, 16)
            sp.dma_start(g.src_f[0:E].rearrange("(p e) -> p e", p=EP), srcf[:, :]).then_inc(stored, 16)
            sp.dma_start(g.dst_f[0:E].rearrange("(p e) -> p e", p=EP), dstf[:, :]).then_inc(stored, 16)
            sp.wait_ge(stored, 16 * 6)

        @block.gpsimd
        def _(pool):
            nc.gpsimd.memset(nvec[:, :], 0.0).then_inc(zeroed, 1)
            nc.gpsimd.memset(ntypi[:, :], 0).then_inc(zeroed, 1)
            nc.gpsimd.memset(padf[:, :], -1.0).then_inc(pads, 1)
            nc.gpsimd.memset(g.ident[:, :], 0.0)
            nc.gpsimd.iota(bndi[:, :], [[P, 26]], base=0, channel_multiplier=0).then_inc(consts, 1)
            nc.gpsimd.iota(iotai[:, :], [[1, IW]], base=0, channel_multiplier=0).then_inc(consts, 1)
            pool.drain()
            nc.gpsimd.affine_select(out=g.ident[:, :], in_=g.ident[:, :], compare_op=ALU.not_equal, fill=1.0, base=0,
                                    pattern=[[-1, P]], channel_multiplier=1).then_inc(consts, 1)
            nc.gpsimd.memset(g.adj[:, g.cleared_from:NB, :].bitcast(F32), 0.0)

        @block.tensor
        def _(pe):
            pe.wait_ge(less_ready, 1)
            pe.matmul(g.bank(0)[:, 0:26], ones[0:EP, :], lessc[:, :], start=True, stop=True).then_inc(starts_ready, 1)
            pe.wait_ge(node_rows, 1)
            pe.wait_ge(consts, 3)
            pe.transpose(g.bank(1)[:, 0:32], nvec[:, :], g.ident[0:32, 0:32])
            pe.transpose(g.bank(1)[:, 32:64], ntyp[:, :], g.ident[0:32, 0:32]).then_inc(nodes_t, 1)

        @block.scalar
        def _(act):
            act.wait_ge(gate_in, 1)
            act.wait_ge(loaded, 16 * 11)
            nc.scalar.activation(g.gate[:, :], nv[:, 0:NB], ACT.Sigmoid, bias=gw[:, 1:2], scale=gw[:, 0:1])
            nc.scalar.activation(skip[:, :], skip[:, :], ACT.Sigmoid).then_inc(gate_out, 1)

        @block.vector
        def _(dve):
            v = nc.vector

            def group_list(e0, blk, nbase):
                v.tensor_tensor(cnt[:, 0:NB], start[:, 1:NB + 1], start[:, 0:NB], ALU.subtract)
                v.memset(tb[:, 0:1], 0.0)
                dve.drain()
                v.tensor_scalar(cnt[:, 0:NB], cnt[:, 0:NB], float(GE - 1), None, ALU.add)
                dve.drain()
                v.tensor_copy(cnti[:, 0:NB], cnt[:, 0:NB])
                dve.drain()
                v.tensor_scalar(cnt2[:, 0:NB], cnti[:, 0:NB], GE.bit_length() - 1, None, ALU.arith_shift_right)
                dve.drain()
                v.tensor_copy(cnt[:, 0:NB], cnt2[:, 0:NB])
                dve.drain()
                v.tensor_tensor_scan(tb[:, 1:NB + 1], cnt[:, 0:NB], zero[:, 0:NB], 0.0, ALU.add, ALU.add)
                dve.drain()
                v.scalar_tensor_tensor(off[:, 0:NB + 1], tb[:, 0:NB + 1], -float(GE), start[:, 0:NB + 1], ALU.mult, ALU.add)
                dve.drain()
                v.tensor_tensor(step[:, 0:NB], off[:, 1:NB + 1], off[:, 0:NB], ALU.subtract)
                groups = iotaf[:, 0:GROUPS]
                v.tensor_tensor(cmp[:, :, :], groups.unsqueeze(2).broadcast_to([P, GROUPS, NB]),
                                tb[:, 1:NB + 1].unsqueeze(1).broadcast_to([P, GROUPS, NB]), ALU.is_ge)
                dve.drain()
                v.tensor_reduce(blkf[:, :], cmp[:, :, :], AX, ALU.add)
                dve.drain()
                v.tensor_tensor(cmp[:, :, :], cmp[:, :, :], step[:, 0:NB].unsqueeze(1).broadcast_to([P, GROUPS, NB]),
                                ALU.mult)
                dve.drain()
                v.tensor_reduce(e0f[:, :], cmp[:, :, :], AX, ALU.add)
                v.tensor_scalar(blkf[:, :], blkf[:, :], float(NB - 1), None, ALU.min)
                dve.drain()
                v.scalar_tensor_tensor(e0f[:, :], groups, float(GE), e0f[:, :], ALU.mult, ALU.add)
                v.tensor_copy(blk[:, :], blkf[:, :])
                v.tensor_scalar(nbase[:, :], blkf[:, :], float(P), None, ALU.mult)
                dve.drain()
                v.tensor_scalar(e0f[:, :], e0f[:, :], float(E), None, ALU.min)
                dve.drain()
                v.tensor_copy(e0[:, :], e0f[:, :])
                dve.drain()

            v.memset(ones[:, :], 1.0)
            v.memset(zero[:, :], 0.0)
            v.memset(padrow[:, :, :], 0)
            v.memset(rows[:, :, :], 0)
            dve.drain()
            v.memset(padrow[:, :, C_DST:C_DST + 1].bitcast(F32), -1.0).then_inc(pads, 1)
            dve.wait_ge(consts, 3)
            v.tensor_copy(bnd[:, :], bndi[:, :])
            v.tensor_copy(iotaf[:, :], iotai[:, :])
            v.tensor_copy(g.ident16[:, :], g.ident[:, :])
            v.tensor_copy(g.identb[:, :], g.ident[:, :])
            dve.drain()
            v.tensor_copy(g.iota[:, :], iotaf[:, 0:P])
            dve.wait_ge(loaded, 16 * 11)
            v.tensor_copy(ntyp[:, :], ntypi[:, :]).then_inc(node_rows, 1)
            v.tensor_copy(dstf[:, :], dsti[:, :])
            v.tensor_copy(srcf[:, :], srci[:, :])
            v.tensor_copy(relf[:, :], etyi[:, :])
            dve.drain()
            w = EF // 5
            for q in range(5):
                v.tensor_tensor(less[:, :, :], dstf[:, q * w:(q + 1) * w].unsqueeze(1).broadcast_to([EP, 26, w]),
                                bnd[0:EP, :].unsqueeze(2).broadcast_to([EP, 26, w]), ALU.is_lt)
                dve.drain()
                v.tensor_reduce(lessp[:, q, :], less[:, :, :], AX, ALU.add)
                dve.drain()
            v.tensor_reduce(lessc[:, :], lessp[:, :, :].rearrange("p q b -> p b q"), AX, ALU.add).then_inc(less_ready, 1)
            v.scalar_tensor_tensor(relf[:, :], relf[:, :], float(NP), srcf[:, :], ALU.mult, ALU.add)
            v.tensor_copy(rows[:, :, C_SRC], srci[:, :])
            v.tensor_copy(rows[:, :, C_DST].bitcast(F32), dstf[:, :])
            v.tensor_copy(rows[:, :, C_ATTR:C_ATTR + 8].bitcast(F32), attr[:, :, :])
            dve.drain()
            v.tensor_copy(rows[:, :, C_REL], relf[:, :])
            dve.drain().then_inc(rows_ready, 1)
            dve.wait_ge(starts_ready, 1)
            v.tensor_copy(start[:, :], g.bank(0)[:, 0:26])
            dve.drain()
            group_list(g.group_e0, g.group_blk, g.group_base)
            dve.wait_ge(nodes_t, 1)
            v.tensor_copy(nv[:, :], g.bank(1)[:, 0:32]).then_inc(gate_in, 1)
            v.tensor_copy(nt[:, :], g.bank(1)[:, 32:64])
            dve.drain()
            for k in range(TYPES):
                v.tensor_scalar(g.tmask[:, :, k], nt[:, 0:NB], float(k), None, ALU.is_equal)
            dve.wait_ge(gate_out, 1)
            v.tensor_scalar(g.ngate[:, :], g.gate[:, :], -1.0, 1.0, ALU.mult, ALU.add)
            dve.drain()
            for k in range(TYPES):
                v.tensor_scalar(g.smask[:, :, k], g.tmask[:, :, k], skip[:, k:k + 1], None, ALU.mult)


def build_adjacency(g):
    nc = g.nc
    u = Place(nc, g.base, "adj")
    oh_src = [u(f"oh_src{k}", [P, NP], BF16) for k in range(GT)]
    wide = u("wide_iota", [P, NP], F16)
    oh_dst = [[u(f"oh_dst{k}{e}", [P, P], BF16) for e in range(GT)] for k in range(2)]
    ends = [u(f"ends{k}", [P, 2, GT], F32) for k in range(2)]
    loc = [u(f"loc{k}", [P, 2, GT], F32) for k in range(2)]
    stage = [u(f"stage{k}", [P, N], F16) for k in range(2)]
    HALF = float(NP // 2)
    slabs = [(c, min(512, N - c)) for c in range(0, N, 512)]
    S = len(slabs)

    ends_ready = [g.sem(f"b_ends_ready{k}") for k in range(2)]
    ends_used, iota_ready, oh_ready, slab_done, sums_used = (
        g.sem("b_ends_used"), g.sem("b_iota"), g.sem("b_oh_ready"), g.sem("b_slab_done"),
        g.sem("b_sums_used"))
    added = g.sem("b_added")

    with nc.Block() as block:
        @block.sync
        def _(sp):
            def load(k, grp):
                e0 = sp.value_load(g.group_e0[0:1, bass.ds(grp, 1)], min_val=0, max_val=E)
                for n, flat in enumerate((g.src_f, g.dst_f)):
                    sp.dma_start(ends[k][:, n, :], flat[bass.ds(e0, GE)].rearrange("(p e) -> p e", p=P))\
                        .then_inc(ends_ready[k], 16)

            with sp.Fori(0, GROUPS // 2) as i:
                for k in range(2):
                    hold(sp, ends_used, i * 2 + (k + 1), g.marks["sp"])
                    load(k, i * 2 + k)

        @block.vector
        def _(dve):
            v = nc.vector
            dve.sem_inc(ends_used, 2)
            dve.wait_ge(iota_ready, 1)

            def one_hots(grp, i, k):
                hold(dve, ends_ready[k], i * 32 + 32, g.marks["dve"])
                v.tensor_scalar(loc[k][:, 0, :], ends[k][:, 0, :], -HALF, None, ALU.add)
                v.tensor_scalar(loc[k][:, 1, :], ends[k][:, 1, :], g.group_base[:, bass.ds(grp, 1)], None, ALU.subtract)
                dve.drain().then_inc(ends_used, 1)
                for e in range(GT):
                    v.tensor_scalar(oh_dst[k][e][:, :], g.iota[:, :], loc[k][:, 1, e:e + 1], None, ALU.is_equal)
                for n, (c, w) in enumerate(slabs):
                    hold(dve, slab_done, grp * S + (n + 1), g.marks["dve"])
                    for e in range(GT):
                        ins = v.tensor_scalar(oh_src[e][:, c:c + w], wide[:, c:c + w], loc[k][:, 0, e:e + 1], None,
                                              ALU.is_equal)
                    ins.then_inc(oh_ready, 1)

            with dve.Fori(0, GROUPS // 2) as i:
                for k in range(2):
                    one_hots(i * 2 + k, i, k)

        @block.tensor
        def _(pe):
            pe.sem_inc(slab_done, S)
            pe.sem_inc(sums_used, S)
            with pe.Fori(0, GROUPS // 2) as i:
                for k in range(2):
                    grp = i * 2 + k
                    for n, (c, w) in enumerate(slabs):
                        hold(pe, oh_ready, grp * S + (n + 1), g.marks["pe"])
                        hold(pe, sums_used, grp * S + (n + 1), g.marks["pe"])
                        for e in range(GT):
                            mm = pe.matmul(g.bank(n)[:, 0:w], oh_dst[k][e][:, :], oh_src[e][:, c:c + w],
                                           start=(e == 0), stop=(e == GT - 1))
                        mm.then_inc(slab_done, 1)

        @block.gpsimd
        def _(pool):
            nc.gpsimd.iota(wide[:, :], [[1, NP]], base=-NP // 2, channel_multiplier=0,
                           allow_small_or_imprecise_dtypes=True).then_inc(iota_ready, 1)
            pool.memset(g.adj[:, 0:g.cleared_from, :].bitcast(F32), 0.0)
            pool.drain()
            with pool.Fori(0, GROUPS // 2) as i:
                for k in range(2):
                    grp = i * 2 + k
                    hold(pool, sums_used, grp * S + 2 * S, g.marks["pool"])
                    blk = pool.value_load(g.group_blk[0:1, bass.ds(grp, 1)], min_val=0, max_val=NB - 1)
                    row = g.adj[:, bass.ds(blk, 1), 0:N].rearrange("p b n -> p (b n)")
                    pool.tensor_tensor(row, row, stage[k][:, :], ALU.add)
                    pool.drain().then_inc(added, 1)

        @block.scalar
        def _(act):
            act.sem_inc(added, 2)
            with act.Fori(0, GROUPS // 2) as i:
                for k in range(2):
                    grp = i * 2 + k
                    hold(act, added, grp + 1, g.marks["act"])
                    for n, (c, w) in enumerate(slabs):
                        hold(act, slab_done, grp * S + (S + n + 1), g.marks["act"])
                        nc.scalar.copy(stage[k][:, c:c + w], g.bank(n)[:, 0:w]).then_inc(sums_used, 1)


def store_adjacency(g):
    nc = g.nc
    stage = Place(nc, g.base, "sto")("turned", [P, NB, CW], F16)
    turned, taken = g.sem("s_turned"), g.sem("s_taken")
    taken_by = [g.sem("s_taken_act"), g.sem("s_taken_dve")]
    staged_out, rows_out = g.sem("s_staged_out"), g.sem("s_rows_out")

    with nc.Block() as block:
        @block.gpsimd
        def _(pool):
            for c in range(CH):
                for p, (k0, nb) in enumerate(PARTS):
                    pool.dma_start(g.adj_ds[p][c], g.adj[:, :, c * CW + k0 * P:c * CW + (k0 + nb) * P])\
                        .then_inc(rows_out, 16)
            pool.wait_ge(rows_out, 16 * 2 * CH)

        @block.tensor
        def _(pe):
            pe.sem_inc(taken_by[0], 1)
            pe.sem_inc(taken_by[1], 1)
            with pe.Fori(0, CH) as c:
                for s in range(NB):
                    q = s % 2
                    per = 13 if q == 0 else 12
                    hold(pe, taken_by[q], c * per + (s // 2 + 1), g.marks["pe"])
                    for k in range(CB):
                        o = g.psum[:, 2 * q:2 * q + 2, :].rearrange("p b n -> p (b n)")[:, k * P:(k + 1) * P]
                        lhs = g.adj[:, bass.ds(c * CB + k, 1), s * P:(s + 1) * P].rearrange("p b n -> p (b n)")
                        mm = pe.matmul(o, lhs, g.ident16[:, :], start=True, stop=True)
                    mm.then_inc(turned, 1)

        def copies(eng, q, per, copy):
            with eng.Fori(0, CH) as c:
                hold(eng, staged_out, c * 32 + 1, g.marks["act" if q == 0 else "dve"])
                for s in range(q, NB, 2):
                    hold(eng, turned, c * NB + (s + 1), g.marks["act" if q == 0 else "dve"])
                    copy(stage[:, s, :], g.psum[:, 2 * q:2 * q + 2, :].rearrange("p b n -> p (b n)")[:, 0:CW])\
                        .then_inc(taken_by[q], 1)

        @block.scalar
        def _(act):
            copies(act, 0, 13, nc.scalar.copy)

        @block.vector
        def _(dve):
            dve.sem_inc(staged_out, 1)
            copies(dve, 1, 12, nc.vector.tensor_copy)

        @block.sync
        def _(sp):
            with sp.Fori(0, CH) as c:
                hold(sp, taken_by[0], c * 13 + 14, g.marks["sp"])
                hold(sp, taken_by[1], c * 12 + 13, g.marks["sp"])
                for p, (k0, nb) in enumerate(PARTS):
                    sp.dma_start(g.adj_sd[p][bass.ds(c, 1)].rearrange("c p s n -> (c p) s n"),
                                 stage[:, :, k0 * P:(k0 + nb) * P]).then_inc(staged_out, 16)
            sp.wait_ge(staged_out, 32 * CH + 1)


class Norm:

    def __init__(self, g, t, name):
        self.g = g
        self.st, self.mv = t("st", [P, CB, 6], F32), t("mv", [P, CB, 2], F32)
        self.ve, self.rstd, self.power = t("ve", [P, CB], F32), t("rstd", [P, CB], F32), t("power", [P, CB], F32)
        self.var_ready, self.rstd_ready, self.cleared = (g.sem(f"{name}_var_ready"), g.sem(f"{name}_rstd_ready"),
                                                         g.sem(f"{name}_ve_cleared"))

    def roots(self, pool, calls):
        pool.memset(self.power[:, :], -0.5)
        pool.memset(self.ve[:, :], 1.0)
        pool.drain().then_inc(self.cleared, 1)
        with pool.Fori(0, calls) as i:
            hold(pool, self.var_ready, i + 1, self.g.marks["pool"])
            pool.tensor_tensor(self.rstd[:, :], self.ve[:, :], self.power[:, :], ALU.pow).then_inc(self.rstd_ready, 1)

    def rows(self, dve, z, nb, call):
        v = self.g.nc.vector
        for k in range(nb):
            v.bn_stats(self.st[:, k, :], z[:, k, :])
        dve.drain()
        for k in range(nb):
            v.bn_aggr(self.mv[:, k, :], self.st[:, k, :])
        dve.drain()
        v.tensor_scalar(self.ve[:, 0:nb], self.mv[:, 0:nb, 1], LN_EPS, None, ALU.add).then_inc(self.var_ready, 1)
        hold(dve, self.rstd_ready, call + 1, self.g.marks["dve"])


def split16(nc, dve, hi, lo, full):
    nc.vector.tensor_copy(hi, full)
    dve.drain()
    nc.vector.tensor_tensor(lo, full, hi, ALU.subtract)


def piece_sems(g, name):
    g.a_loaded = [[g.sem(f"{name}_a_loaded{p}{j}") for j in range(CH)] for p in range(2)]
    g.a_used = [[g.sem(f"{name}_a_used{p}{j}") for j in range(CH)] for p in range(2)]


def load_pieces(g, sp, adj, abuf, c, it):
    for p in range(2):
        for j in range(CH):
            hold(sp, g.a_used[p][j], it + 1, g.marks["sp"])
            sp.dma_start(abuf[p][:, j * CB:(j + 1) * CB, :],
                         adj[p][bass.ds(c, 1), :, j * CB:(j + 1) * CB, :].rearrange("c p s n -> (c p) s n"))\
                .then_inc(g.a_loaded[p][j], 16)


def gin_layers(g):
    nc, a = g.nc, g.a
    t = Place(nc, g.after_x, "gin")
    g.h = t("h", [P, NB, D], F32)
    hs = [t(f"hs{q}", [P, NB, 2, D], F16) for q in range(2)]
    abuf = [t(f"abuf{p}", [P, NB, PARTS[p][1] * P], F16) for p in range(2)]
    xT = [t(f"xT{p}", [P, 2, PARTS[p][1] * P], F32) for p in range(2)]
    yT = [t(f"yT{p}", [P, 2, PARTS[p][1] * P], F32) for p in range(2)]
    w1 = [t(f"w1{q}", [P, 2, D], F32) for q in range(2)]
    w2 = [t(f"w2{q}", [P, 2, D], F32) for q in range(2)]
    b1 = [t(f"b1{q}", [P, 2], F32) for q in range(2)]
    b2 = [t(f"b2{q}", [P, D], F32) for q in range(2)]
    gam = t("gam", [P, D], F32)
    bet = t("bet", [P, D], F32)
    epsr = t("epsr", [P, LAYERS], F32)
    dful = t("dful", [P, P], F32)
    diag = t("diag", [P, LAYERS, 2, P], F16)
    z = t("z", [P, 3, D], F32)
    norm = Norm(g, t, "g")
    mv, rstd = norm.mv, norm.rstd

    piece_sems(g, "g")
    x_ready, small, diag_ready, h_done = g.sem("g_x"), g.sem("g_small"), g.sem("g_diag"), g.sem("g_h_done")
    w_loaded = [g.sem(f"g_w_loaded{q}") for q in range(2)]
    w_used = [g.sem(f"g_w_used{q}") for q in range(2)]
    agg_done = [g.sem(f"g_agg{p}") for p in range(2)]
    xt_ready = [g.sem(f"g_xt{p}") for p in range(2)]
    y_done = [g.sem(f"g_y{p}") for p in range(2)]
    yt_ready = [g.sem(f"g_yt{p}") for p in range(2)]
    z_done, z_used = g.sem("g_z_done"), g.sem("g_z_used")
    ZBANK = [6, 7, 6, 7, 6]
    ZWAIT = [3, 1, 2, 2, 2]

    def turns(eng, each_layer, a_first, body):
        with eng.Fori(0, LAYERS // 2) as lp:
            for q in range(2):
                layer = lp * 2 + q
                each_layer(layer, lp, q)
                a_first(layer * CH, 0, layer, q)
                with eng.Fori(0, CH - 1) as c:
                    body(layer * CH + c, c, layer, q, False)
                body(layer * CH + (CH - 1), CH - 1, layer, q, True)

    with nc.Block() as block:
        @block.sync
        def _(sp):
            sp.dma_start(g.x[:, 0:NB - 1, :],
                         a["x"][0:(NB - 1) * P].rearrange("(b p) d -> p b d", p=P)).then_inc(x_ready, 16)
            sp.wait_ge(small, 1)
            sp.dma_start(g.x[0:TAIL, NB - 1, :], a["x"][(NB - 1) * P:N]).then_inc(x_ready, 16)
            for row, src in ((gam, a["L0_gnn_gamma"]), (bet, a["L0_gnn_beta"]), (epsr, a["L0_gnn_eps"])):
                sp.dma_start(row[:, :], src.unsqueeze(0).broadcast_to(list(row.shape))).then_inc(x_ready, 16)
            with sp.Fori(0, LAYERS // 2) as lp:
                for q in range(2):
                    layer = lp * 2 + q
                    hold(sp, w_used[q], lp * 2 + 2, g.marks["sp"])
                    for w, src in ((w1, a["L0_gnn_W1"]), (w2, a["L0_gnn_W2"])):
                        sp.dma_start(w[q][:, :, :],
                                     src[bass.ds(layer, 1)].rearrange("l (c p) n -> p (l c) n", p=P))\
                            .then_inc(w_loaded[q], 16)
                    sp.dma_start(b1[q][:, :], a["L0_gnn_b1"][bass.ds(layer, 1)].rearrange("l (c p) -> p (l c)", p=P))\
                        .then_inc(w_loaded[q], 16)
                    sp.dma_start(b2[q][:, :], a["L0_gnn_b2"][bass.ds(layer, 1)].broadcast_to([P, D]))\
                        .then_inc(w_loaded[q], 16)
                    with sp.Fori(0, CH) as c:
                        load_pieces(g, sp, g.adj_sd, abuf, c, layer * CH + c)

        @block.gpsimd
        def _(pool):
            norm.roots(pool, 2 * CH * LAYERS)

        @block.tensor
        def _(pe):
            for p in range(2):
                for j in range(CH):
                    pe.sem_inc(g.a_used[p][j], 1)
            pe.wait_ge(diag_ready, 1)

            def aggregate(it, c, layer, q, p, first=False):
                k0, nb = PARTS[p]
                w = nb * P
                hold(pe, xt_ready[p], it + 1, g.marks["pe"])
                for j in range(CH):
                    hold(pe, g.a_loaded[p][j], it * 16 + 16, g.marks["pe"])
                    if first:
                        hold(pe, h_done, layer * (2 * CH) + 2 * (j + 1), g.marks["pe"])
                    for s in range(j * CB, (j + 1) * CB):
                        for f in range(2):
                            for part in range(2):
                                mm = pe.matmul(g.bank(2 * p + f)[:, 0:w], hs[q][:, s, part, f * P:(f + 1) * P],
                                               abuf[p][:, s, :], start=(s == 0 and part == 0),
                                               stop=(s == NB - 1 and part == 1))
                    mm.then_inc(g.a_used[p][j], 1)
                    if j == 0:
                        own_rows(c, layer, q, p)
                pe.drain().then_inc(agg_done[p], 1)

            def own_rows(c, layer, q, p):
                k0, nb = PARTS[p]
                for f in range(2):
                    for k in range(nb):
                        for part in range(2):
                            lhs = hs[q][:, bass.ds(c * CB + (k0 + k), 1), part, f * P:(f + 1) * P]\
                                .rearrange("p b n -> p (b n)")
                            for e in range(2):
                                pe.matmul(g.bank(2 * p + f)[:, k * P:(k + 1) * P], lhs,
                                          diag[:, bass.ds(layer, 1), e, :].rearrange("p b n -> p (b n)"),
                                          start=False, stop=False, skip_group_check=True)

            def perceptron(it, c, q, p):
                k0, nb = PARTS[p]
                hold(pe, xt_ready[p], it + 2, g.marks["pe"])
                for f in range(2):
                    for kk in range(2):
                        mm = pe.matmul(g.bank(4 + f)[:, 0:nb * P], w1[q][:, kk, f * P:(f + 1) * P], xT[p][:, kk, :],
                                       start=(kk == 0), stop=(kk == 1))
                mm.then_inc(y_done[p], 1)
                hold(pe, yt_ready[p], it * 2 + 2, g.marks["pe"])
                for k in range(k0, k0 + nb):
                    hold(pe, z_used, it * CB + (k + ZWAIT[k]), g.marks["pe"])
                    for kk in range(2):
                        mm = pe.matmul(g.bank(ZBANK[k])[:, 0:D], yT[p][:, kk, (k - k0) * P:(k - k0 + 1) * P],
                                       w2[q][:, kk, :], start=(kk == 0), stop=(kk == 1))
                    mm.then_inc(z_done, 1)

            def each_layer(layer, lp, q):
                hold(pe, w_loaded[q], lp * 64 + 64, g.marks["pe"])

            def a_first(it, c, layer, q):
                aggregate(it, c, layer, q, 0, first=True)

            def body(it, c, layer, q, last):
                aggregate(it, c, layer, q, 1)
                perceptron(it, c, q, 0)
                if not last:
                    aggregate(it + 1, c + 1, layer, q, 0)
                perceptron(it, c, q, 1)
                if last:
                    pe.drain().then_inc(w_used[q], 1)

            turns(pe, each_layer, a_first, body)

        @block.scalar
        def _(act):
            for p in range(2):
                act.sem_inc(xt_ready[p], 1)

            def take(it, p):
                w = PARTS[p][1] * P
                hold(act, agg_done[p], it + 1, g.marks["act"])
                nc.scalar.copy(xT[p][:, :, :], g.psum[:, 2 * p:2 * p + 2, 0:w]).then_inc(xt_ready[p], 1)

            def relu(it, q, p):
                w = PARTS[p][1] * P
                hold(act, y_done[p], it + 1, g.marks["act"])
                for f in range(2):
                    nc.scalar.activation(yT[p][:, f, :], g.bank(4 + f)[:, 0:w], ACT.Relu, bias=b1[q][:, f:f + 1])\
                        .then_inc(yt_ready[p], 1)

            def each_layer(layer, lp, q):
                hold(act, w_loaded[q], lp * 64 + 64, g.marks["act"])

            def body(it, c, layer, q, last):
                take(it, 1)
                relu(it, q, 0)
                if not last:
                    take(it + 1, 0)
                relu(it, q, 1)

            turns(act, each_layer, lambda it, c, layer, q: take(it, 0), body)

        @block.vector
        def _(dve):
            v = nc.vector
            dve.wait_ge(norm.cleared, 1)
            v.memset(g.x[:, NB - 1, :], 0.0).then_inc(small, 1)
            dve.sem_inc(z_used, 3)
            dve.sem_inc(w_used[0], 2)
            dve.sem_inc(w_used[1], 2)
            dve.wait_ge(x_ready, 16 * 5)
            v.tensor_copy(g.h[:, :, :], g.x[:, :, :])
            split16(nc, dve, hs[0][:, :, 0, :], hs[0][:, :, 1, :], g.x[:, :, :])
            v.tensor_scalar(epsr[:, :], epsr[:, :], 1.0, None, ALU.add)
            dve.drain().then_inc(h_done, 2 * CH)
            for layer in range(LAYERS):
                v.tensor_scalar(dful[:, :], g.ident[:, :], epsr[:, layer:layer + 1], None, ALU.mult)
                dve.drain()
                split16(nc, dve, diag[:, layer, 0, :], diag[:, layer, 1, :], dful[:, :])
                dve.drain()
            dve.drain().then_inc(diag_ready, 1)

            def finish(it, c, q, p):
                k0, nb = PARTS[p]
                for k in range(k0, k0 + nb):
                    hold(dve, z_done, it * CB + (k + 1), g.marks["dve"])
                    v.tensor_tensor(z[:, k - k0, :], g.bank(ZBANK[k])[:, 0:D], b2[q][:, :], ALU.add).then_inc(z_used, 1)
                dve.drain()
                norm.rows(dve, z, nb, it * 2 + p)
                for k in range(nb):
                    v.scalar_tensor_tensor(z[:, k, :], z[:, k, :], mv[:, k, 0:1], gam[:, :], ALU.subtract, ALU.mult)
                dve.drain()
                for k in range(nb):
                    v.scalar_tensor_tensor(z[:, k, :], z[:, k, :], rstd[:, k:k + 1], bet[:, :], ALU.mult, ALU.add)
                dve.drain()
                blocks = bass.ds(c * CB + k0, nb)
                v.scalar_tensor_tensor(g.h[:, blocks, :], z[:, 0:nb, :], 0.0, g.h[:, blocks, :], ALU.max, ALU.add)
                dve.drain()
                split16(nc, dve, hs[1 - q][:, blocks, 0, :], hs[1 - q][:, blocks, 1, :], g.h[:, blocks, :])
                dve.drain().then_inc(h_done, 1)

            def each_layer(layer, lp, q):
                hold(dve, w_loaded[q], lp * 64 + 64, g.marks["dve"])

            def body(it, c, layer, q, last):
                finish(it, c, q, 0)
                finish(it, c, q, 1)
                if last:
                    dve.sem_inc(w_used[q], 1)

            turns(dve, each_layer, lambda it, c, layer, q: None, body)



ZBANK = [6, 7, 6, 7, 6]
ZWAIT = [3, 1, 2, 2, 2]


def pe_turn(g, pe, w, turned, first_bank):
    for kc in range(2):
        for oc in range(2):
            q = 2 * kc + oc
            mm = pe.transpose(g.bank(first_bank)[:, q * P:(q + 1) * P], w[:, oc, kc * P:(kc + 1) * P], g.ident[:, :])
    mm.then_inc(turned, 1)


def pe_turn_blocks(g, pe, rows, turned, c, used):
    hold(pe, used, c * CB + 1, g.marks["pe"])
    for k in range(CB):
        for f in range(2):
            mm = pe.transpose(g.bank(k // 2)[:, (k % 2) * D + f * P:(k % 2) * D + (f + 1) * P],
                              rows[:, k, f * P:(f + 1) * P], g.ident[:, :])
        mm.then_inc(turned, 1)


def act_take_blocks(g, act, dst, turned, taken, c):
    for k in range(CB):
        hold(act, turned, c * CB + min(k // 2 * 2 + 2, CB), g.marks["act"])
        g.nc.scalar.copy(dst[:, k, :], g.bank(k // 2)[:, (k % 2) * D:(k % 2 + 1) * D]).then_inc(taken, 1)


def qkv_pass(g):
    nc, a = g.nc, g.a
    H1, HD1 = 8, 32
    g.qs = Place(nc, g.slot2, "qkv1")("qs", [P, NB, 2, D], F16)
    t = Place(nc, g.rest, "qkv")
    wraw = [t(f"wraw{i}", [P, 2, D], F32) for i in range(3)]
    wkv = t("wkv", [P, 2, 2 * D], F32)
    wq = t("wq", [P, 2, D], F32)
    z = t("z", [P, CB, D], F32)
    xs = t("xs", [P, CB, D], F32)
    xsT = t("xsT", [P, CB, D], F32)
    q32 = t("q32", [P, CB, D], F32)
    kvs = t("kvs", [P, CB, 2 * D], F32)
    norm = Norm(g, t, "q")
    mv, rstd = norm.mv, norm.rstd
    w_in, w_turned, w_ready = g.sem("q_w_in"), g.sem("q_w_turned"), g.sem("q_w_ready")
    xs_ready, xs_turned, xt_ready = g.sem("q_xs_ready"), g.sem("q_xs_turned"), g.sem("q_xt_ready")
    kv_done, kv_taken, q_done, q_taken = g.sem("q_kv_done"), g.sem("q_kv_taken"), g.sem("q_q_done"), g.sem("q_q_taken")
    kv_out = [g.sem(f"q_kv_out{k}") for k in range(CB)]
    KVB, QB = [3, 4, 3, 4, 3], [5, 6, 5, 6, 5]

    with nc.Block() as block:
        @block.sync
        def _(sp):
            for i, name in enumerate(("L1_gnn_Wk", "L1_gnn_Wv", "L1_gnn_Wq")):
                sp.dma_start(wraw[i][:, :, :], a[name].rearrange("(c p) n -> p c n", p=P)).then_inc(w_in, 16)
            with sp.Fori(0, CH) as c:
                for k in range(CB):
                    hold(sp, kv_taken, c * CB + (k + 4), g.marks["sp"])
                    sp.dma_start(g.kv1[bass.ds(c * CW + k * P, P), :], kvs[:, k, :]).then_inc(kv_out[k], 16)
            for k in range(CB):
                sp.wait_ge(kv_out[k], 16 * CH + 1)

        @block.gpsimd
        def _(pool):
            norm.roots(pool, CH)

        @block.tensor
        def _(pe):
            pe.wait_ge(w_in, 48)
            for i in range(3):
                pe_turn(g, pe, wraw[i], w_turned, i)
            pe.wait_ge(w_ready, 3)
            pe.sem_inc(xt_ready, 1)
            with pe.Fori(0, CH) as c:
                hold(pe, xs_ready, c + 1, g.marks["pe"])
                pe_turn_blocks(g, pe, xs, xs_turned, c, xt_ready)
                for k in range(CB):
                    hold(pe, xt_ready, c * CB + (k + 2), g.marks["pe"])
                    hold(pe, kv_taken, c * CB + (k + ZWAIT[k]), g.marks["pe"])
                    for f in range(2):
                        mm = pe.matmul(g.bank(KVB[k]), xsT[:, k, f * P:(f + 1) * P], wkv[:, f, :],
                                       start=(f == 0), stop=(f == 1))
                    mm.then_inc(kv_done, 1)
                    hold(pe, q_taken, c * CB + (k + ZWAIT[k]), g.marks["pe"])
                    for f in range(2):
                        mm = pe.matmul(g.bank(QB[k])[:, 0:D], xsT[:, k, f * P:(f + 1) * P], wq[:, f, :],
                                       start=(f == 0), stop=(f == 1))
                    mm.then_inc(q_done, 1)

        @block.scalar
        def _(act):
            act.sem_inc(kv_taken, 3)
            for k in range(CB):
                act.sem_inc(kv_out[k], 1)
            act.wait_ge(w_turned, 3)
            for i, dst in enumerate((wkv[:, :, 0:D], wkv[:, :, D:2 * D], wq[:, :, :])):
                nc.scalar.copy(dst, g.bank(i).rearrange("p (k n) -> p k n", k=2)).then_inc(w_ready, 1)
            with act.Fori(0, CH) as c:
                act_take_blocks(g, act, xsT, xs_turned, xt_ready, c)
                for k in range(CB):
                    hold(act, kv_done, c * CB + (k + 1), g.marks["act"])
                    hold(act, kv_out[k], c * 16 + 1, g.marks["act"])
                    nc.scalar.copy(kvs[:, k, :], g.bank(KVB[k])).then_inc(kv_taken, 1)

        @block.vector
        def _(dve):
            v = nc.vector
            dve.wait_ge(norm.cleared, 1)
            dve.sem_inc(q_taken, 3)
            with dve.Fori(0, CH) as c:
                blocks = bass.ds(c * CB, CB)
                v.tensor_tensor(z[:, :, :], g.x[:, blocks, :], g.h[:, blocks, :], ALU.add)
                dve.drain()
                norm.rows(dve, z, CB, c)
                hold(dve, xt_ready, c * CB + 1, g.marks["dve"])
                for k in range(CB):
                    v.tensor_scalar(xs[:, k, :], z[:, k, :], mv[:, k, 0:1], rstd[:, k:k + 1], ALU.subtract, ALU.mult)
                dve.drain().then_inc(xs_ready, 1)
                v.tensor_copy(g.x[:, blocks, :], xs[:, :, :])
                for k in range(CB):
                    hold(dve, q_done, c * CB + (k + 1), g.marks["dve"])
                    v.tensor_scalar(q32[:, k, :], g.bank(QB[k])[:, 0:D], float(HD1) ** 0.5, None, ALU.mult)\
                        .then_inc(q_taken, 1)
                dve.drain()
                split16(nc, dve, g.qs[:, blocks, 0, :], g.qs[:, blocks, 1, :], q32[:, :, :])
                dve.drain()


def attention(g, layer):
    nc = g.nc
    H = 8 if layer == 1 else 4
    HD = D // H
    R = KB * H
    table = g.kv1 if layer == 1 else g.kv3
    col = C_SRC if layer == 1 else C_REL
    g.acc = Place(nc, g.slot1, f"att{layer}a")("acc", [P, NB, H, HD + 1], F32)
    t = Place(nc, g.rest, f"att{layer}")
    kv = [t(f"kv{q}", [P, KB, 2 * D], F32) for q in range(2)]
    pay = [t(f"pay{q}", [P, KB, ROW], I32) for q in range(2)]
    oh = [t(f"oh{q}", [P, KB, P], BF16) for q in range(2)]
    oh32 = [t(f"oh32{q}", [P, KB, P], F32) for q in range(2)]
    ohT = [t(f"ohT{q}", [P, KB, P], BF16) for q in range(2)]
    av = t("av", [P, KB, H, HD + 1], F32)
    prod = [t(f"prod{q}", [P, GT, D], F32) for q in range(2)]
    loc = t("loc", [P, KB], F32)
    drep = t("drep", [P, KB, H], F32)
    sc = [t(f"sc{q}", [P, KB, H], F32) for q in range(2)]
    arg = t("arg", [P, KB, H], F32)
    dT = t("dT", [P, P], F32)
    neq = t("neq", [P, P + 1], F32)
    run = t("run", [P, P], F32)
    lme = t("lme", [P, KB, H + 1], BF16)
    absent = t("absent", [P, KB], F32)
    gmax = t("gmax", [P, BG, H], F32)
    mrun = t("mrun", [P, NB, H], BF16)
    mk = t("mk", [P, BG, H], BF16)
    dd = t("dd", [P, BG, H], F32)
    cf = t("cf", [P, BG, H], F32)

    n = f"t{layer}_"
    pay_ready = [g.sem(f"{n}pay_ready{q}") for q in range(2)]
    pay_used = [g.sem(f"{n}pay_used{q}") for q in range(2)]
    (oh_ready, oh32_ready, ohT_done, ohT_ready, qe_done, qe_used, sc_ready, st_done, lm_ready, lmT_done, lme_ready,
     mt_done, mk_ready, cf_ready, me_done, arg_ready, a_ready, av_ready, po_done, po_used) = (
        g.sem(n + s) for s in ("oh_ready", "oh32_ready", "ohT_done", "ohT_ready", "qe_done", "qe_used", "sc_ready",
                               "st_done", "lm_ready", "lmT_done", "lme_ready", "mt_done", "mk_ready", "cf_ready",
                               "me_done", "arg_ready", "a_ready", "av_ready", "po_done", "po_used"))
    kv_ready = [[g.sem(f"{n}kv_ready{q}_{s}") for s in range(BG)] for q in range(2)]
    AV0 = 2 * BG
    sT, dTp, lmp = g.bank(6)[0:R, 0:P], g.bank(6)[0:R, P:2 * P], g.bank(6)[:, 2 * P:2 * P + R]
    mtp = g.bank(7)[:, 0:KB * (H + 1)].rearrange("p (k h) -> p k h", k=KB)
    mep = g.bank(7)[:, 256:256 + R].rearrange("p (k h) -> p k h", k=KB)
    flat = lambda ap: ap.rearrange("p k h -> p (k h)")

    def all_batches(eng, body):
        with eng.Fori(0, BATCHES // 2) as i:
            for q in range(2):
                body(i, i * 2 + q, q)
        body(BATCHES // 2, BATCHES - 1, 0)

    def overlapped(eng, first, step, last):
        first()
        with eng.Fori(0, BATCHES // 2) as i:
            for q in range(2):
                step(i, i * 2 + q, q)
        last(BATCHES // 2, BATCHES - 1, 0)

    with nc.Block() as block:
        @block.sync
        def _(sp):
            def body(i, j, q):
                hold(sp, pay_used[q], i + 1, g.marks["sp"])
                for s in range(BG):
                    e0 = sp.value_load(g.group_e0[0:1, bass.ds(j * BG + s, 1)], min_val=0, max_val=E)
                    sp.dma_start(pay[q][:, s * GT:(s + 1) * GT, :],
                                 g.edge_rows[bass.ds(e0, GE), :].rearrange("(p k) w -> p k w", k=GT))\
                        .then_inc(pay_ready[q], 16)

            all_batches(sp, body)

        @block.gpsimd
        def _(pool):
            def body(i, j, q):
                hold(pool, pay_ready[q], i * (16 * BG) + 16 * BG, g.marks["pool"])
                for s in range(BG):
                    hold(pool, av_ready, j * BG + (s + 1), g.marks["pool"])
                    for k in range(GT * s, GT * s + GT):
                        pool.indirect_dma_start(kv[q][:, k, :], None, table,
                                                bass.IndirectOffsetOnAxis(ap=pay[q][:, k, col:col + 1], axis=0))\
                            .then_inc(kv_ready[q][s], 16)

            all_batches(pool, body)

        @block.tensor
        def _(pe):
            def turn(j, q, s):
                if s % 2 == 0:
                    hold(pe, oh_ready, j * 2 + (s // 2 + 1), g.marks["pe"])
                for k in range(GT * s, GT * s + GT):
                    mm = pe.matmul(g.bank(s % 2)[:, (k % GT) * P:(k % GT + 1) * P], oh[q][:, k, :], g.identb[:, :],
                                   start=True, stop=True)
                mm.then_inc(ohT_done, 1)

            def queries(j, q, s):
                hold(pe, ohT_ready, j * BG + (s + 1), g.marks["pe"])
                blk = pe.value_load(g.group_blk[0:1, bass.ds(j * BG + s, 1)], min_val=0, max_val=NB - 1)
                for k in range(GT * s, GT * s + GT):
                    pair, half = k // 2, k % 2
                    if half == 0:
                        hold(pe, qe_used, j * (KB // 2) + (pair + 1), g.marks["pe"])
                    for part in range(2):
                        mm = pe.matmul(g.bank(2 + pair % 2)[:, half * D:(half + 1) * D], ohT[q][:, k, :],
                                       g.qs[:, bass.ds(blk, 1), part, :].rearrange("p b n -> p (b n)"),
                                       start=(part == 0), stop=(part == 1))
                    if half == 1:
                        mm.then_inc(qe_done, 1)

            def turn_scores(j, q):
                hold(pe, sc_ready, j + 1, g.marks["pe"])
                pe.transpose(sT, flat(sc[q][:, :, :]), g.ident[:, :])
                pe.transpose(dTp, flat(drep[:, :, :]), g.ident[:, :]).then_inc(st_done, 1)

            def tile_maxima(j, q):
                hold(pe, lm_ready, j + 1, g.marks["pe"])
                pe.transpose(lmp, run[0:R, :], g.ident[0:R, 0:R]).then_inc(lmT_done, 1)
                hold(pe, lme_ready, j + 1, g.marks["pe"])
                for k in range(KB):
                    mm = pe.matmul(mtp[:, k, :], oh[q][:, k, :], lme[:, k, :], start=True, stop=True)
                mm.then_inc(mt_done, 1)

            def edge_maxima(j, q):
                hold(pe, mk_ready, j + 1, g.marks["pe"])
                for k in range(KB):
                    mm = pe.matmul(mep[:, k, :], ohT[q][:, k, :], mk[:, k // GT, :], start=True, stop=True)
                mm.then_inc(me_done, 1)

            def sums(j, q, s):
                if s == 0:
                    hold(pe, oh32_ready, j * 2 + 2, g.marks["pe"])
                hold(pe, av_ready, j * BG + (s + 1 + AV0), g.marks["pe"])
                hold(pe, po_used, j * BG + (s + 1), g.marks["pe"])
                for k in range(GT * s, GT * s + GT):
                    mm = pe.matmul(g.bank(4 + s % 2)[:, 0:D + H], oh32[q][:, k, :],
                                   av[:, k, :, :].rearrange("p h d -> p (h d)"),
                                   start=(k % GT == 0), stop=(k % GT == GT - 1))
                mm.then_inc(po_done, 1)

            def first():
                for s in range(BG):
                    turn(0, 0, s)
                    queries(0, 0, s)
                turn_scores(0, 0)
                tile_maxima(0, 0)

            def step(i, j, q):
                turn(j + 1, 1 - q, 0)
                turn(j + 1, 1 - q, 1)
                queries(j + 1, 1 - q, 0)
                edge_maxima(j, q)
                turn(j + 1, 1 - q, 2)
                queries(j + 1, 1 - q, 1)
                turn(j + 1, 1 - q, 3)
                queries(j + 1, 1 - q, 2)
                sums(j, q, 0)
                queries(j + 1, 1 - q, 3)
                sums(j, q, 1)
                turn_scores(j + 1, 1 - q)
                sums(j, q, 2)
                sums(j, q, 3)
                tile_maxima(j + 1, 1 - q)

            def last(i, j, q):
                edge_maxima(j, q)
                for s in range(BG):
                    sums(j, q, s)

            overlapped(pe, first, step, last)

        @block.scalar
        def _(act):
            def take_turned(j, q, s):
                hold(act, ohT_done, j * BG + (s + 1), g.marks["act"])
                nc.scalar.copy(flat(ohT[q][:, GT * s:GT * s + GT, :]), g.bank(s % 2)).then_inc(ohT_ready, 1)

            def widen(j, q, half):
                hold(act, oh_ready, j * 2 + (half + 1), g.marks["act"])
                ks = slice(half * KB // 2, (half + 1) * KB // 2)
                nc.scalar.copy(flat(oh32[q][:, ks, :]), flat(oh[q][:, ks, :])).then_inc(oh32_ready, 1)

            def factors(j):
                hold(act, mk_ready, j + 1, g.marks["act"])
                nc.scalar.activation(cf[:, :, :], dd[:, :, :], ACT.Exp).then_inc(cf_ready, 1)

            def weights(j):
                hold(act, arg_ready, j + 1, g.marks["act"])
                nc.scalar.activation(av[:, :, :, HD], arg[:, :, :], ACT.Exp).then_inc(a_ready, 1)

            def first():
                for s in range(BG):
                    take_turned(0, 0, s)
                widen(0, 0, 0)
                widen(0, 0, 1)

            def step(i, j, q):
                take_turned(j + 1, 1 - q, 0)
                take_turned(j + 1, 1 - q, 1)
                factors(j)
                take_turned(j + 1, 1 - q, 2)
                weights(j)
                take_turned(j + 1, 1 - q, 3)
                widen(j + 1, 1 - q, 0)
                widen(j + 1, 1 - q, 1)

            def last(i, j, q):
                factors(j)
                weights(j)

            overlapped(act, first, step, last)

        @block.vector
        def _(dve):
            v = nc.vector
            v.memset(g.acc[:, :, :, :], 0.0)
            v.memset(mrun[:, :, :], -BIG)
            v.memset(neq[:, :], 1.0)
            v.memset(lme[:, :, H:H + 1], 1.0)
            for q in range(2):
                dve.sem_inc(pay_used[q], 1)
            dve.sem_inc(av_ready, AV0)
            dve.sem_inc(qe_used, 2)
            dve.sem_inc(po_used, 2)
            dve.drain()

            def one_hots(i, j, q):
                hold(dve, pay_ready[q], i * (16 * BG) + 16 * BG, g.marks["dve"])
                dst = pay[q][:, :, C_DST].bitcast(F32)
                v.tensor_tensor(loc[:, :].rearrange("p (s k) -> p s k", k=GT), dst.rearrange("p (s k) -> p s k", k=GT),
                                g.group_base[:, bass.ds(j * BG, BG)].unsqueeze(2).broadcast_to([P, BG, GT]), ALU.subtract)
                v.tensor_copy(drep[:, :, :], dst.unsqueeze(2).broadcast_to([P, KB, H]))
                dve.drain()
                for half in range(2):
                    ks = slice(half * KB // 2, (half + 1) * KB // 2)
                    v.tensor_tensor(oh[q][:, ks, :], g.iota[:, :].unsqueeze(1).broadcast_to([P, KB // 2, P]),
                                    loc[:, ks].unsqueeze(2).broadcast_to([P, KB // 2, P]), ALU.is_equal)\
                        .then_inc(oh_ready, 1)

            def scores(i, j, q, s):
                hold(dve, kv_ready[q][s], i * (16 * GT) + 16 * GT, g.marks["dve"])
                hold(dve, qe_done, j * (KB // 2) + (2 * s + 2), g.marks["dve"])
                for pair in (2 * s, 2 * s + 1):
                    v.tensor_tensor(prod[s % 2][:, pair % 2 * 2:pair % 2 * 2 + 2, :], kv[q][:, 2 * pair:2 * pair + 2, 0:D],
                                    g.bank(2 + pair % 2).rearrange("p (k d) -> p k d", k=2), ALU.mult)\
                        .then_inc(qe_used, 1)
                dve.drain()
                v.tensor_reduce(flat(sc[q][:, GT * s:GT * s + GT, :]),
                                prod[s % 2][:, :, :].rearrange("p k (h d) -> p (k h) d", h=H), AX, ALU.add)
                if s == BG - 1:
                    dve.drain()
                    if layer == 1:
                        v.tensor_tensor(sc[q][:, :, :], sc[q][:, :, :], pay[q][:, :, C_ATTR:C_ATTR + H].bitcast(F32),
                                        ALU.add)
                        dve.drain()
                    dve.sem_inc(sc_ready, 1)
                    dve.sem_inc(pay_used[q], 1)

            def run_maxima(j):
                hold(dve, st_done, j + 1, g.marks["dve"])
                v.tensor_copy(dT[0:R, :], dTp)
                dve.drain()
                v.tensor_tensor(neq[0:R, 1:P], dT[0:R, 1:P], dT[0:R, 0:P - 1], ALU.not_equal)
                dve.drain()
                v.tensor_scalar(dT[0:R, :], neq[0:R, 0:P], -BIG, None, ALU.mult)
                dve.drain()
                v.tensor_tensor_scan(run[0:R, :], dT[0:R, :], sT, -BIG, ALU.add, ALU.max)
                dve.drain()
                v.tensor_tensor(run[0:R, :], run[0:R, :], neq[0:R, 1:P + 1], ALU.mult).then_inc(lm_ready, 1)

            def take_maxima(j):
                hold(dve, lmT_done, j + 1, g.marks["dve"])
                v.tensor_copy(lme[:, :, 0:H], lmp.rearrange("p (k h) -> p k h", k=KB)).then_inc(lme_ready, 1)

            def running_maxima(j):
                hold(dve, mt_done, j + 1, g.marks["dve"])
                v.tensor_scalar(absent[:, :], mtp[:, :, H], 0.5, -BIG, ALU.is_lt, ALU.mult)
                blks = [dve.value_load(g.group_blk[0:1, bass.ds(j * BG + s, 1)], min_val=0, max_val=NB - 1)
                        for s in range(BG)]
                dve.drain()
                v.tensor_tensor(arg[:, :, :], mtp[:, :, 0:H], absent[:, :].unsqueeze(2).broadcast_to([P, KB, H]), ALU.add)
                dve.drain()
                v.tensor_reduce(gmax[:, :, :], arg[:, :, :].rearrange("p (s k) h -> p s h k", k=GT), AX, ALU.max)
                dve.drain()
                for s in range(BG):
                    now = mrun[:, bass.ds(blks[s], 1), :].rearrange("p b h -> p (b h)")
                    v.tensor_tensor(mk[:, s, :], gmax[:, s, :], now, ALU.max)
                    v.tensor_copy(dd[:, s, :], now)
                    dve.drain()
                    v.tensor_copy(now, mk[:, s, :])
                    dve.drain()
                v.tensor_tensor(dd[:, :, :], dd[:, :, :], mk[:, :, :], ALU.subtract).then_inc(mk_ready, 1)
                return blks

            def exponents(j, q):
                hold(dve, me_done, j + 1, g.marks["dve"])
                v.tensor_tensor(arg[:, :, :], sc[q][:, :, :], mep, ALU.subtract)
                dve.drain()
                v.tensor_scalar(arg[:, :, :], arg[:, :, :], 10.0, None, ALU.min).then_inc(arg_ready, 1)

            def weigh(j, q, s):
                if s == 0:
                    hold(dve, a_ready, j + 1, g.marks["dve"])
                ks = slice(GT * s, GT * s + GT)
                v.tensor_tensor(av[:, ks, :, 0:HD], kv[q][:, ks, D:2 * D].rearrange("p k (h d) -> p k h d", h=H),
                                av[:, ks, :, HD:HD + 1].broadcast_to([P, GT, H, HD]), ALU.mult).then_inc(av_ready, 1)

            def add_sums(j, blks, s):
                if s == 0:
                    hold(dve, cf_ready, j + 1, g.marks["dve"])
                rows = g.acc[:, bass.ds(blks[s], 1), :, :].rearrange("p b h d -> p (b h) d")
                v.tensor_tensor(rows, rows, cf[:, s, :].unsqueeze(2).broadcast_to([P, H, HD + 1]), ALU.mult)
                hold(dve, po_done, j * BG + (s + 1), g.marks["dve"])
                dve.drain()
                v.tensor_tensor(rows, rows, g.bank(4 + s % 2)[:, 0:D + H].rearrange("p (h d) -> p h d", h=H),
                                ALU.add).then_inc(po_used, 1)
                dve.drain()

            def first():
                one_hots(0, 0, 0)
                for s in range(BG):
                    scores(0, 0, 0, s)
                run_maxima(0)
                take_maxima(0)

            def step(i, j, q):
                nxt = (i + q, j + 1, 1 - q)
                one_hots(*nxt)
                blks = running_maxima(j)
                scores(*nxt, 0)
                exponents(j, q)
                scores(*nxt, 1)
                for k in range(BG):
                    weigh(j, q, k)
                scores(*nxt, 2)
                add_sums(j, blks, 0)
                scores(*nxt, 3)
                add_sums(j, blks, 1)
                run_maxima(j + 1)
                add_sums(j, blks, 2)
                take_maxima(j + 1)
                add_sums(j, blks, 3)

            def last(i, j, q):
                blks = running_maxima(j)
                exponents(j, q)
                for s in range(BG):
                    weigh(j, q, s)
                for s in range(BG):
                    add_sums(j, blks, s)

            overlapped(dve, first, step, last)


def weighted_rows(g, dve, os, rec, c, H, k):
    HD = D // H
    v = g.nc.vector
    rows = g.acc[:, bass.ds(c * CB + k, 1), :, :].rearrange("p b h d -> p (b h) d")
    v.tensor_scalar(rec[:, k, 0:H], rows[:, :, HD], 1e-30, None, ALU.max)
    dve.drain()
    v.reciprocal(rec[:, k, 0:H], rec[:, k, 0:H])
    dve.drain()
    v.tensor_tensor(os[:, k, :].rearrange("p (h d) -> p h d", h=H), rows[:, :, 0:HD],
                    rec[:, k, 0:H].unsqueeze(2).broadcast_to([P, H, HD]), ALU.mult)


def attention_out(g):
    nc, a = g.nc, g.a
    g.xs16 = Place(nc, g.slot2, "out1x")("xs16", [P, NB, 2, D], F16)
    t = Place(nc, g.rest, "out1")
    wraw, wo = t("wraw", [P, 2, D], F32), t("wo", [P, 2, D], F32)
    os, osT, z = t("os", [P, CB, D], F32), t("osT", [P, CB, D], F32), t("z", [P, CB, D], F32)
    rec = t("rec", [P, CB, 8], F32)
    norm = Norm(g, t, "o")
    mv, rstd = norm.mv, norm.rstd
    w_in, w_turned, w_ready = g.sem("o_w_in"), g.sem("o_w_turned"), g.sem("o_w_ready")
    os_ready, os_turned, ost_ready = g.sem("o_os_ready"), g.sem("o_os_turned"), g.sem("o_ost_ready")
    y_done, y_taken = g.sem("o_y_done"), g.sem("o_y_taken")

    with nc.Block() as block:
        @block.sync
        def _(sp):
            sp.dma_start(wraw[:, :, :], a["L1_gnn_Wo"].rearrange("(c p) n -> p c n", p=P)).then_inc(w_in, 16)

        @block.gpsimd
        def _(pool):
            norm.roots(pool, CH)

        @block.tensor
        def _(pe):
            pe.wait_ge(w_in, 16)
            pe_turn(g, pe, wraw, w_turned, 3)
            pe.wait_ge(w_ready, 1)
            pe.sem_inc(ost_ready, 1)
            with pe.Fori(0, CH) as c:
                hold(pe, os_ready, c + 1, g.marks["pe"])
                pe_turn_blocks(g, pe, os, os_turned, c, ost_ready)
                for k in range(CB):
                    hold(pe, ost_ready, c * CB + (k + 2), g.marks["pe"])
                    hold(pe, y_taken, c * CB + (k + ZWAIT[k]), g.marks["pe"])
                    for f in range(2):
                        mm = pe.matmul(g.bank(ZBANK[k])[:, 0:D], osT[:, k, f * P:(f + 1) * P], wo[:, f, :],
                                       start=(f == 0), stop=(f == 1))
                    mm.then_inc(y_done, 1)

        @block.scalar
        def _(act):
            act.wait_ge(w_turned, 1)
            nc.scalar.copy(wo[:, :, :], g.bank(3).rearrange("p (k n) -> p k n", k=2)).then_inc(w_ready, 1)
            with act.Fori(0, CH) as c:
                act_take_blocks(g, act, osT, os_turned, ost_ready, c)

        @block.vector
        def _(dve):
            v = nc.vector
            dve.wait_ge(norm.cleared, 1)
            dve.sem_inc(y_taken, 3)
            with dve.Fori(0, CH) as c:
                hold(dve, ost_ready, c * CB + 1, g.marks["dve"])
                for k in range(CB):
                    weighted_rows(g, dve, os, rec, c, 8, k)
                dve.drain().then_inc(os_ready, 1)
                for k in range(CB):
                    hold(dve, y_done, c * CB + (k + 1), g.marks["dve"])
                    v.tensor_tensor(z[:, k, :], g.bank(ZBANK[k])[:, 0:D],
                                    g.x[:, bass.ds(c * CB + k, 1), :].rearrange("p b n -> p (b n)"), ALU.add)\
                        .then_inc(y_taken, 1)
                dve.drain()
                norm.rows(dve, z, CB, c)
                for k in range(CB):
                    v.tensor_scalar(z[:, k, :], z[:, k, :], mv[:, k, 0:1], rstd[:, k:k + 1], ALU.subtract, ALU.mult)
                dve.drain()
                blocks = bass.ds(c * CB, CB)
                v.tensor_copy(g.x[:, blocks, :], z[:, :, :])
                split16(nc, dve, g.xs16[:, blocks, 0, :], g.xs16[:, blocks, 1, :], z[:, :, :])
                dve.drain()


def mean_layer(g):
    nc, a = g.nc, g.a
    HB2 = D // 2
    W = D + HB2
    t = Place(nc, g.rest, "mean")
    abuf = [t(f"abuf{p}", [P, NB, PARTS[p][1] * P], F16) for p in range(2)]
    nT = [t(f"nT{p}", [P, 2, PARTS[p][1] * P], F32) for p in range(2)]
    xT = [t(f"xT{p}", [P, 2, PARTS[p][1] * P], F32) for p in range(2)]
    wx, wn = t("wx", [P, 2, W], F32), t("wn", [P, 2, W], F32)
    bm, be, bn = t("bm", [P, D], F32), t("be", [P, HB2], F32), t("bn", [P, HB2], F32)
    one = t("one", [P, 1], F16)
    rd = t("rd", [P, 4], F32)
    u = t("u", [P, 3, W], F32)
    hm, hc, z = t("hm", [P, 3, D], F32), t("hc", [P, 3, D], F32), t("z", [P, 3, D], F32)
    norm = Norm(g, t, "m")
    mv, rstd = norm.mv, norm.rstd
    w_in, one_ready, rd_ready = g.sem("m_w_in"), g.sem("m_one"), g.sem("m_rd_ready")
    agg_done = [g.sem(f"m_agg{p}") for p in range(2)]
    nt_ready = [g.sem(f"m_nt{p}") for p in range(2)]
    p_done, p_used = g.sem("m_p_done"), g.sem("m_p_used")
    piece_sems(g, "m")
    SET = [(6, 7), (4, 5), (6, 7)]

    with nc.Block() as block:
        @block.sync
        def _(sp):
            for w in (wx, wn):
                sp.dma_start(w[:, :, 0:D], a["L2_gnn_W_mean"].rearrange("(c p) n -> p c n", p=P)).then_inc(w_in, 16)
            sp.dma_start(wx[:, :, D:W], a["L2_gnn_W_ego"].rearrange("(c p) n -> p c n", p=P)).then_inc(w_in, 16)
            sp.dma_start(wn[:, :, D:W], a["L2_gnn_W_nb"].rearrange("(c p) n -> p c n", p=P)).then_inc(w_in, 16)
            for row, name in ((bm, "L2_gnn_b_mean"), (be, "L2_gnn_b_ego"), (bn, "L2_gnn_b_nb")):
                sp.dma_start(row[:, :], a[name].unsqueeze(0).broadcast_to(list(row.shape))).then_inc(w_in, 16)
            with sp.Fori(0, CH) as c:
                load_pieces(g, sp, g.adj_ds, abuf, c, c)

        @block.gpsimd
        def _(pool):
            norm.roots(pool, 2 * CH)

        @block.tensor
        def _(pe):
            for p in range(2):
                for j in range(CH):
                    pe.sem_inc(g.a_used[p][j], 1)
            pe.wait_ge(one_ready, 1)
            pe.wait_ge(w_in, 16 * 7)

            def part(c, p):
                k0, nb = PARTS[p]
                w = nb * P
                hold(pe, nt_ready[p], c + 1, g.marks["pe"])
                for j in range(CH):
                    hold(pe, g.a_loaded[p][j], c * 16 + 16, g.marks["pe"])
                    for s in range(j * CB, (j + 1) * CB):
                        for f in range(2):
                            for half in range(2):
                                pe.matmul(g.bank(2 * p + f)[:, 0:w], g.xs16[:, s, half, f * P:(f + 1) * P],
                                          abuf[p][:, s, :], start=(s == 0 and half == 0), stop=(s == NB - 1 and half == 1))
                hold(pe, p_used, c * CB + (k0 + 1), g.marks["pe"])
                for k in range(nb):
                    for s in range(NB):
                        mm = pe.matmul(g.bank(7)[:, k:k + 1], abuf[p][:, s, k * P:(k + 1) * P], one[:, :],
                                       start=(s == 0), stop=(s == NB - 1))
                for f in range(2):
                    for k in range(nb):
                        for half in range(2):
                            lhs = g.xs16[:, bass.ds(c * CB + (k0 + k), 1), half, f * P:(f + 1) * P]\
                                .rearrange("p b n -> p (b n)")
                            mm = pe.matmul(g.bank(4 + f)[:, k * P:(k + 1) * P], lhs, g.ident16[:, :],
                                           start=(half == 0), stop=(half == 1))
                mm.then_inc(agg_done[p], 1)
                hold(pe, nt_ready[p], c + 2, g.marks["pe"])
                for j in range(CH):
                    pe.sem_inc(g.a_used[p][j], 1)
                hold(pe, rd_ready, c * 2 + (p + 1), g.marks["pe"])
                for k in range(nb):
                    if k == 2:
                        hold(pe, p_used, c * CB + (k0 + 2), g.marks["pe"])
                    for bank, rows, wgt in ((SET[k][0], xT, wx), (SET[k][1], nT, wn)):
                        for f in range(2):
                            mm = pe.matmul(g.bank(bank)[:, 0:W], rows[p][:, f, k * P:(k + 1) * P], wgt[:, f, :],
                                           start=(f == 0), stop=(f == 1))
                    mm.then_inc(p_done, 1)

            with pe.Fori(0, CH) as c:
                part(c, 0)
                part(c, 1)

        @block.scalar
        def _(act):
            act.sem_inc(nt_ready[0], 1)
            act.sem_inc(nt_ready[1], 1)
            with act.Fori(0, CH) as c:
                for p in range(2):
                    w = PARTS[p][1] * P
                    hold(act, agg_done[p], c + 1, g.marks["act"])
                    nc.scalar.copy(nT[p][:, :, :], g.psum[:, 2 * p:2 * p + 2, 0:w])
                    nc.scalar.copy(xT[p][:, :, :], g.psum[:, 4:6, 0:w])
                    act.drain().then_inc(nt_ready[p], 1)

        @block.vector
        def _(dve):
            v = nc.vector
            dve.wait_ge(norm.cleared, 1)
            v.memset(one[:, :], 1.0).then_inc(one_ready, 1)
            dve.sem_inc(p_used, 1)
            dve.wait_ge(w_in, 16 * 7)
            with dve.Fori(0, CH) as c:
                for p, (k0, nb) in enumerate(PARTS):
                    hold(dve, agg_done[p], c + 1, g.marks["dve"])
                    v.tensor_scalar(rd[:, 0:nb], g.bank(7)[:, 0:nb], 1.0, None, ALU.max)
                    dve.drain()
                    v.reciprocal(rd[:, 0:nb], rd[:, 0:nb])
                    dve.drain().then_inc(rd_ready, 1)
                    for k in range(nb):
                        hold(dve, p_done, c * CB + (k0 + k + 1), g.marks["dve"])
                        px, pn = g.bank(SET[k][0]), g.bank(SET[k][1])
                        gt = g.gate[:, bass.ds(c * CB + (k0 + k), 1)]
                        ng = g.ngate[:, bass.ds(c * CB + (k0 + k), 1)]
                        v.tensor_scalar(u[:, k, :], pn[:, 0:W], rd[:, k:k + 1], None, ALU.mult)
                        v.tensor_tensor(hc[:, k, 0:HB2], px[:, D:W], be[:, :], ALU.add)
                        dve.drain()
                        v.tensor_tensor(hm[:, k, :], px[:, 0:D], u[:, k, 0:D], ALU.add)
                        dve.drain().then_inc(p_used, 1)
                        v.scalar_tensor_tensor(hm[:, k, :], hm[:, k, :], 0.5, bm[:, :], ALU.mult, ALU.add)
                        v.tensor_tensor(hc[:, k, HB2:D], u[:, k, D:W], bn[:, :], ALU.add)
                        dve.drain()
                        v.tensor_scalar(hm[:, k, :], hm[:, k, :], ng, None, ALU.mult)
                        dve.drain()
                        v.scalar_tensor_tensor(hm[:, k, :], hc[:, k, :], gt, hm[:, k, :], ALU.mult, ALU.add)
                    dve.drain()
                    v.tensor_tensor(z[:, 0:nb, :], hm[:, 0:nb, :], g.x[:, bass.ds(c * CB + k0, nb), :], ALU.add)
                    dve.drain()
                    norm.rows(dve, z, nb, c * 2 + p)
                    for k in range(nb):
                        v.tensor_scalar(z[:, k, :], z[:, k, :], mv[:, k, 0:1], rstd[:, k:k + 1], ALU.subtract, ALU.mult)
                    dve.drain()
                    v.tensor_copy(g.x[:, bass.ds(c * CB + k0, nb), :], z[:, 0:nb, :])
                    dve.drain()


def typed_pass(g):
    nc, a = g.nc, g.a
    HH, DK = 4, D // 4
    g.qs = Place(nc, g.slot2, "typed1")("qs", [P, NB, 2, D], F16)
    t = Place(nc, g.slot1, "typed")
    w = {n: t(f"w{n}", [P, TYPES, 2, D], F32) for n in "k"}
    t.at = g.rest
    w["q"] = t("wq", [P, TYPES, 2, D], F32)
    w["v"] = t("wv", [P, TYPES, 2, D], F32)
    ra, rm, raT = (t(n, [P, RELS, 2, P], F32) for n in ("ra", "rm", "raT"))
    pri = t("pri", [P, RELS, 2], F32)
    xm = [t(f"xm{q}", [P, TYPES, D], F32) for q in range(2)]
    xmT = [t(f"xmT{p}", [P, 2 * TYPES, PARTS[p][1] * P], F32) for p in range(2)]
    kvT = t("kvT", [P, 4, 3 * P], F32)
    q32 = t("q32", [P, 3, D], F32)
    tab = t("tab", [P, 2, 4, 2 * D], F32)
    w_in, pri_in, zeroed, ra_scaled, ra_turned, ra_ready = (g.sem("y_w_in"), g.sem("y_pri_in"), g.sem("y_zeroed"),
                                                           g.sem("y_ra_scaled"), g.sem("y_ra_turned"), g.sem("y_ra_ready"))
    xm_ready, xm_turned, xmt_ready = g.sem("y_xm_ready"), g.sem("y_xm_turned"), g.sem("y_xmt_ready")
    kv_done, kv_taken, q_done, q_taken = g.sem("y_kv_done"), g.sem("y_kv_taken"), g.sem("y_q_done"), g.sem("y_q_taken")
    tab_done = g.sem("y_tab_done")
    tab_taken = [g.sem(f"y_tab_taken{q}") for q in range(2)]
    tab_out = [[g.sem(f"y_tab_out{q}{r}") for r in range(4)] for q in range(2)]
    XMB = [0, 1, 0, 1, 0]

    def parts(eng, part):
        with eng.Fori(0, CH - 1) as c:
            part(c, 0, c, 1)
            part(c, 1, c + 1, 0)
        part(CH - 1, 0, CH - 1, 1)
        part(CH - 1, 1, None, None)

    with nc.Block() as block:
        @block.sync
        def _(sp):
            for n, name in (("k", "L3_gnn_k_linears"), ("q", "L3_gnn_q_linears"), ("v", "L3_gnn_v_linears")):
                for ty in range(TYPES):
                    sp.dma_start(w[n][:, ty, :, :], a[name][ty].rearrange("(c p) n -> p c n", p=P)).then_inc(w_in, 16)
            sp.wait_ge(zeroed, 2)
            for dst, name in ((ra, "L3_gnn_relation_att"), (rm, "L3_gnn_relation_msg")):
                for hp in range(2):
                    for h2 in range(2):
                        sp.dma_start(dst[h2 * DK:(h2 + 1) * DK, :, hp, h2 * DK:(h2 + 1) * DK],
                                     a[name][:, 2 * hp + h2].rearrange("r d e -> d r e")).then_inc(w_in, 16)
            for h2 in range(2):
                sp.dma_start(pri[h2 * DK:(h2 + 1) * DK, :, :],
                             a["L3_gnn_relation_pri"].rearrange("r (a b) -> r a b", b=2)[:, :, h2].unsqueeze(0)
                             .broadcast_to([DK, RELS, 2])).then_inc(w_in, 16)
            with sp.Fori(0, NB) as b:
                for r in range(RELS):
                    q, k = r % 2, r // 2
                    hold(sp, tab_taken[q], b * 4 + (k + 2), g.marks["sp"])
                    sp.dma_start(g.kv3[bass.ds(b * P + r * NP, P), :], tab[:, q, k, :]).then_inc(tab_out[q][k], 16)
            for q in range(2):
                for k in range(4):
                    sp.wait_ge(tab_out[q][k], 16 * NB + 1)

        @block.gpsimd
        def _(pool):
            pool.memset(ra[:, :, :, :], 0.0).then_inc(zeroed, 1)
            pool.memset(rm[:, :, :, :], 0.0).then_inc(zeroed, 1)

        @block.tensor
        def _(pe):
            pe.wait_ge(w_in, 16 * 22)
            pe.wait_ge(ra_scaled, 1)
            for r in range(RELS):
                for hp in range(2):
                    n = 2 * r + hp
                    mm = pe.transpose(g.bank(n // 4)[:, (n % 4) * P:(n % 4 + 1) * P], ra[:, r, hp, :], g.ident[:, :])
            mm.then_inc(ra_turned, 1)
            pe.wait_ge(ra_ready, 1)
            pe.sem_inc(xmt_ready, 1)

            def turn(c, p, k):
                kb = PARTS[p][0] + k
                hold(pe, xm_ready, c * CB + (kb + 1), g.marks["pe"])
                hold(pe, xmt_ready, c * CB + (kb + 1), g.marks["pe"])
                for ty in range(TYPES):
                    for f in range(2):
                        n = 2 * ty + f
                        mm = pe.transpose(g.bank(n // 4)[:, (n % 4) * P:(n % 4 + 1) * P],
                                          xm[XMB[kb]][:, ty, f * P:(f + 1) * P], g.ident[:, :])
                mm.then_inc(xm_turned, 1)

            def keys_values(c, p):
                k0, nb = PARTS[p]
                wd = nb * P
                hold(pe, xmt_ready, c * CB + (k0 + nb + 1), g.marks["pe"])
                for n in range(4):
                    wgt = w["k"] if n < 2 else w["v"]
                    oc = n % 2
                    hold(pe, kv_taken, c * 8 + (p * 4 + n + 1), g.marks["pe"])
                    for ty in range(TYPES):
                        for f in range(2):
                            mm = pe.matmul(g.bank(2 + n % 2)[:, 0:wd], wgt[:, ty, f, oc * P:(oc + 1) * P],
                                           xmT[p][:, 2 * ty + f, :], start=(ty == 0 and f == 0),
                                           stop=(ty == TYPES - 1 and f == 1))
                    mm.then_inc(kv_done, 1)

            def queries(c, p):
                k0, nb = PARTS[p]
                for k in range(nb):
                    hold(pe, q_taken, c * CB + (k0 + k + (2 if k == 0 else 1)), g.marks["pe"])
                    for ty in range(TYPES):
                        for f in range(2):
                            mm = pe.matmul(g.bank(4 + k % 2 * 3)[:, 0:D], xmT[p][:, 2 * ty + f, k * P:(k + 1) * P],
                                           w["q"][:, ty, f, :], start=(ty == 0 and f == 0),
                                           stop=(ty == TYPES - 1 and f == 1))
                    mm.then_inc(q_done, 1)

            def tables(c, p, k):
                k0, nb = PARTS[p]
                if k == 0:
                    hold(pe, kv_taken, c * 8 + (p * 4 + 6), g.marks["pe"])
                for r in range(RELS):
                    hold(pe, tab_taken[r % 2], c * (CB * 4) + ((k0 + k) * 4 + r // 2 + 1), g.marks["pe"])
                    for n in range(4):
                        mm = pe.matmul(g.bank(5 + r % 2)[:, n * P:(n + 1) * P], kvT[:, n, k * P:(k + 1) * P],
                                       (raT if n < 2 else rm)[:, r, n % 2, :], start=True, stop=True)
                    mm.then_inc(tab_done, 1)

            def part(c, p, nc_, np_):
                nxt = PARTS[np_][1] if np_ is not None else 0
                keys_values(c, p)
                if nxt:
                    turn(nc_, np_, 0)
                queries(c, p)
                if nxt:
                    turn(nc_, np_, 1)
                for k in range(PARTS[p][1]):
                    tables(c, p, k)
                    if k == 0 and nxt > 2:
                        turn(nc_, np_, 2)

            for k in range(PARTS[0][1]):
                turn(0, 0, k)
            parts(pe, part)

        def take_tables(eng, q, c, kb, copy, mark):
            for r in range(q, RELS, 2):
                hold(eng, tab_done, c * (CB * RELS) + (kb * RELS + r + 1), mark)
                hold(eng, tab_out[q][r // 2], c * (CB * 16) + (kb * 16 + 1), mark)
                copy(tab[:, q, r // 2, :], g.bank(5 + q)).then_inc(tab_taken[q], 1)

        @block.scalar
        def _(act):
            for q in range(2):
                act.sem_inc(tab_taken[q], 1)
                for k in range(4):
                    act.sem_inc(tab_out[q][k], 1)
            act.sem_inc(kv_taken, 2)
            act.wait_ge(ra_turned, 1)
            nc.scalar.copy(raT[:, :, :, :].rearrange("p r h n -> p (r h n)"),
                           g.psum[:, 0:4, :].rearrange("p b n -> p (b n)")).then_inc(ra_ready, 1)

            def take_turned(c, p, k):
                hold(act, xm_turned, c * CB + (PARTS[p][0] + k + 2), g.marks["act"])
                nc.scalar.copy(xmT[p][:, :, k * P:(k + 1) * P],
                               g.psum[:, 0:2, :].rearrange("p b (t n) -> p (b t) n", t=4)).then_inc(xmt_ready, 1)

            def part(c, p, nc_, np_):
                k0, nb = PARTS[p]
                nxt = PARTS[np_][1] if np_ is not None else 0
                for n in range(4):
                    hold(act, kv_done, c * 8 + (p * 4 + n + 1), g.marks["act"])
                    nc.scalar.copy(kvT[:, n, 0:nb * P], g.bank(2 + n % 2)[:, 0:nb * P]).then_inc(kv_taken, 1)
                for k in range(min(nxt, 2)):
                    take_turned(nc_, np_, k)
                for k in range(nb):
                    take_tables(act, 0, c, k0 + k, nc.scalar.copy, g.marks["act"])
                    if k == 0 and nxt > 2:
                        take_turned(nc_, np_, 2)

            for k in range(PARTS[0][1]):
                take_turned(0, 0, k)
            parts(act, part)

        @block.vector
        def _(dve):
            v = nc.vector
            dve.sem_inc(q_taken, 2)
            dve.wait_ge(w_in, 16 * 22)
            v.tensor_scalar(pri[:, :, :], pri[:, :, :], float(DK) ** -0.5, None, ALU.mult)
            dve.drain()
            for r in range(RELS):
                for hp in range(2):
                    v.tensor_scalar(ra[:, r, hp, :], ra[:, r, hp, :], pri[:, r, hp:hp + 1], None, ALU.mult)
            dve.drain().then_inc(ra_scaled, 1)

            def mask(c, p, k):
                kb = PARTS[p][0] + k
                hold(dve, xm_turned, c * CB + (kb if kb > 0 else 1), g.marks["dve"])
                for ty in range(TYPES):
                    v.tensor_scalar(xm[XMB[kb]][:, ty, :],
                                    g.x[:, bass.ds(c * CB + kb, 1), :].rearrange("p b n -> p (b n)"),
                                    g.tmask[:, bass.ds(c * CB + kb, 1), ty], None, ALU.mult)
                dve.drain().then_inc(xm_ready, 1)

            def part(c, p, nc_, np_):
                k0, nb = PARTS[p]
                nxt = PARTS[np_][1] if np_ is not None else 0
                for k in range(min(nxt, 2)):
                    mask(nc_, np_, k)
                for k in range(nb):
                    hold(dve, q_done, c * CB + (k0 + k + 1), g.marks["dve"])
                    v.tensor_copy(q32[:, k, :], g.bank(4 + k % 2 * 3)[:, 0:D]).then_inc(q_taken, 1)
                dve.drain()
                blocks = bass.ds(c * CB + k0, nb)
                split16(nc, dve, g.qs[:, blocks, 0, :], g.qs[:, blocks, 1, :], q32[:, 0:nb, :])
                if nxt > 2:
                    mask(nc_, np_, 2)
                for k in range(nb):
                    take_tables(dve, 1, c, k0 + k, v.tensor_copy, g.marks["dve"])
                dve.drain()

            dve.sem_inc(xm_turned, 1)
            for k in range(PARTS[0][1]):
                mask(0, 0, k)
            parts(dve, part)


def typed_out(g):
    nc, a = g.nc, g.a
    t = Place(nc, g.slot2, "fin")
    wa = t("wa", [P, TYPES, 2, D], F32)
    os = t("os", [P, CB, D], F32)
    om = [t(f"om{q}", [P, TYPES, D], F32) for q in range(2)]
    omT = [t(f"omT{q}", [P, 2 * TYPES, P], F32) for q in range(2)]
    z = t("z", [P, CB, D], F32)
    res = t("res", [P, CB, D], F32)
    rec = t("rec", [P, CB, 8], F32)
    norm = Norm(g, t, "f")
    mv, rstd = norm.mv, norm.rstd
    w_in, om_ready, om_turned, omt_ready = g.sem("f_w_in"), g.sem("f_om_ready"), g.sem("f_om_turned"), g.sem("f_omt_ready")
    y_done, y_taken, res_ready, res_out = g.sem("f_y_done"), g.sem("f_y_taken"), g.sem("f_res_ready"), g.sem("f_res_out")
    OMB = [0, 1, 0, 1, 0]
    out_rows = g.out

    with nc.Block() as block:
        @block.sync
        def _(sp):
            for ty in range(TYPES):
                sp.dma_start(wa[:, ty, :, :], a["L3_gnn_a_linears"][ty].rearrange("(c p) n -> p c n", p=P)).then_inc(w_in, 16)
            with sp.Fori(0, CH - 1) as c:
                hold(sp, res_ready, c + 1, g.marks["sp"])
                sp.dma_start(out_rows[bass.ds(c * CW, CW), :].rearrange("(b p) d -> p b d", p=P), res[:, :, :])\
                    .then_inc(res_out, 16)
            sp.wait_ge(res_ready, CH)
            last = (CH - 1) * CW
            sp.dma_start(out_rows[last:last + (CB - 1) * P, :].rearrange("(b p) d -> p b d", p=P),
                         res[:, 0:CB - 1, :]).then_inc(res_out, 16)
            sp.dma_start(out_rows[last + (CB - 1) * P:N, :], res[0:TAIL, CB - 1, :]).then_inc(res_out, 16)
            sp.wait_ge(res_out, 16 * (CH + 1) + 1)

        @block.gpsimd
        def _(pool):
            norm.roots(pool, CH)

        @block.tensor
        def _(pe):
            pe.wait_ge(w_in, 16 * TYPES)
            pe.sem_inc(omt_ready, 1)
            with pe.Fori(0, CH) as c:
                for k in range(CB):
                    hold(pe, om_ready, c * CB + (k + 1), g.marks["pe"])
                    hold(pe, omt_ready, c * CB + (k + 1), g.marks["pe"])
                    for n in range(2 * TYPES):
                        mm = pe.transpose(g.bank(n // 4)[:, (n % 4) * P:(n % 4 + 1) * P],
                                          om[OMB[k]][:, n // 2, (n % 2) * P:(n % 2 + 1) * P], g.ident[:, :])
                    mm.then_inc(om_turned, 1)
                    hold(pe, omt_ready, c * CB + (k + 2), g.marks["pe"])
                    hold(pe, y_taken, c * CB + (k + ZWAIT[k]), g.marks["pe"])
                    for n in range(2 * TYPES):
                        mm = pe.matmul(g.bank(ZBANK[k])[:, 0:D], omT[OMB[k]][:, n, :], wa[:, n // 2, n % 2, :],
                                       start=(n == 0), stop=(n == 2 * TYPES - 1))
                    mm.then_inc(y_done, 1)

        @block.scalar
        def _(act):
            act.sem_inc(res_out, 1)
            with act.Fori(0, CH) as c:
                for k in range(CB):
                    hold(act, om_turned, c * CB + (k + 1), g.marks["act"])
                    nc.scalar.copy(omT[OMB[k]][:, :, :].rearrange("p t n -> p (t n)"),
                                   g.psum[:, 0:2, :].rearrange("p b n -> p (b n)")).then_inc(omt_ready, 1)

        @block.vector
        def _(dve):
            v = nc.vector
            dve.wait_ge(norm.cleared, 1)
            dve.sem_inc(y_taken, 3)
            def take(c, k):
                hold(dve, y_done, c * CB + (k + 1), g.marks["dve"])
                v.tensor_tensor(z[:, k, :], g.bank(ZBANK[k])[:, 0:D],
                                g.x[:, bass.ds(c * CB + k, 1), :].rearrange("p b n -> p (b n)"), ALU.add)\
                    .then_inc(y_taken, 1)

            with dve.Fori(0, CH) as c:
                for k in range(CB):
                    weighted_rows(g, dve, os, rec, c, 4, k)
                    hold(dve, omt_ready, c * CB + (k + 1), g.marks["dve"])
                    dve.drain()
                    for ty in range(TYPES):
                        v.tensor_scalar(om[OMB[k]][:, ty, :], os[:, k, :], g.smask[:, bass.ds(c * CB + k, 1), ty],
                                        None, ALU.mult)
                    dve.drain().then_inc(om_ready, 1)
                    if k > 0:
                        take(c, k - 1)
                take(c, CB - 1)
                dve.drain()
                norm.rows(dve, z, CB, c)
                hold(dve, res_out, c * 16 + 1, g.marks["dve"])
                for k in range(CB):
                    v.tensor_scalar(res[:, k, :], z[:, k, :], mv[:, k, 0:1], rstd[:, k:k + 1], ALU.subtract, ALU.mult)
                dve.drain().then_inc(res_ready, 1)


_INS = ["x", "src", "dst", "edge_attr_8", "edge_type_8", "node_type_4", "node_vec",
        "L0_gnn_W1", "L0_gnn_b1", "L0_gnn_W2", "L0_gnn_b2", "L0_gnn_eps", "L0_gnn_gamma", "L0_gnn_beta",
        "L1_gnn_Wq", "L1_gnn_Wk", "L1_gnn_Wv", "L1_gnn_Wo",
        "L2_gnn_W_mean", "L2_gnn_b_mean", "L2_gnn_W_ego", "L2_gnn_b_ego", "L2_gnn_W_nb", "L2_gnn_b_nb",
        "L2_gnn_gate_weight", "L2_gnn_gate_bias",
        "L3_gnn_k_linears", "L3_gnn_q_linears", "L3_gnn_v_linears", "L3_gnn_a_linears", "L3_gnn_relation_att",
        "L3_gnn_relation_msg", "L3_gnn_relation_pri", "L3_gnn_skip"]


def kernel(**inputs):
    import numpy as _np
    import concourse.bacc as _bacc
    from concourse import mybir as _mybir
    from concourse.bass_utils import run_bass_kernel_spmd as _run

    nc = _bacc.Bacc("TRN2", target_bir_lowering=False, num_devices=1)
    arrays, a = {}, {}
    for name in _INS:
        v = _np.ascontiguousarray(inputs[name])
        arrays[f"in_{name}"] = v
        a[name] = nc.dram_tensor(f"in_{name}", v.shape, _mybir.dt.from_np(v.dtype), kind="ExternalInput").ap()
    out = nc.dram_tensor("out_0", (N, D), F32, kind="ExternalOutput").ap()
    program(nc, a, out)
    r = _run(nc, [arrays], core_ids=[0])
    return r.results[0]["out_0"]
```
